# Optimizing a Trainium2 kernel written in Bass

```python
import numpy as np
import jax
import jax.numpy as jnp

def _softmax(x, axis=-1):
    return jax.nn.softmax(x, axis=axis)

def _gelu(x):
    return jax.nn.gelu(x, approximate=True)

def _silu(x):
    return jax.nn.silu(x)

def _sigmoid(x):
    return jax.nn.sigmoid(x)

def _layernorm(x, axis=-1, eps=1e-05):
    m = jnp.mean(x, axis=axis, keepdims=True)
    v = jnp.var(x, axis=axis, keepdims=True)
    return (x - m) / jnp.sqrt(v + eps)

def _scatter_add(tgt, idx, src, axis=0):
    return tgt.at[idx].add(src)

def _segment_sum(src, seg, n):
    return jax.ops.segment_sum(src, seg, n)
kernel_name = 'mk_lm_tower_d1_tok_ids1024_r4_9bcc62'

def setup_inputs(seed: int=0):
    np.random.seed(seed)
    _w = jnp.asarray

    def _rec_inputs():
        import jax
        import jax.numpy as jnp
        _rk = jax.random.key(seed)
        x = jax.random.randint(jax.random.fold_in(_rk, 1), (8, 1024), 0, 12564, jnp.int32)
        return x
    x = _rec_inputs()

    def _L0_tok_setup():
        import jax, jax.numpy as jnp
        import numpy as np
        VOCAB = 50257
        D = 256
        EDGES = [0, 5000, 10000, VOCAB]
        HSZ = [256, 64, 64]
        key = jax.random.key(seed)
        ks = jax.random.split(key, 8)
        emb_input = jax.random.randint(ks[0], (8, 512), 0, VOCAB, dtype=jnp.int64)
        inp = {'emb_input': emb_input}
        for i in range(3):
            vsz = EDGES[i + 1] - EDGES[i]
            h = HSZ[i]
            inp[f'emb{i}'] = jax.random.normal(ks[1 + 2 * i], (vsz, h), dtype=jnp.float32) * 0.02
            inp[f'w{i}'] = jax.random.normal(ks[2 + 2 * i], (D, h), dtype=jnp.float32) * 0.02
        return inp
    _L0_tok_all = _L0_tok_setup()
    _L0_tok_in = {k: v for k, v in _L0_tok_all.items() if k in ('emb0', 'w0', 'emb1', 'w1', 'emb2', 'w2')}
    del _L0_tok_all

    def _L0_attn_setup():
        import jax, jax.numpy as jnp
        import numpy as np
        H, DK, DV, CHUNK = (4, 64, 64, 32)

        def _silu(x):
            return x * jax.nn.sigmoid(x)

        def _l2norm(x, eps=1e-06):
            return x * jax.lax.rsqrt(jnp.sum(x * x, -1, keepdims=True) + eps)

        def _rmsnorm(x, w, eps=1e-05):
            return x * jax.lax.rsqrt(jnp.mean(x * x, -1, keepdims=True) + eps) * w

        def _causal_dwconv(x, w):
            C = x.shape[-1]
            K = w.shape[-1]
            xp = jnp.pad(x, ((0, 0), (K - 1, 0), (0, 0))).transpose(0, 2, 1)
            y = jax.lax.conv_general_dilated(xp, w[:, None, :], (1,), 'VALID', feature_group_count=C, dimension_numbers=('NCH', 'OIH', 'NCH'))
            return y.transpose(0, 2, 1)

        def _fir(x, filt):
            B, L, h, d = x.shape
            y = _causal_dwconv(x.reshape(B, L, h * d), filt.reshape(h * d, -1))
            return y.reshape(B, L, h, d)

        def _delta_rule_chunkwise(q, k, v, beta):
            b, h, L, dk = q.shape
            dv = v.shape[-1]
            n = L // CHUNK
            q = _l2norm(q)
            k = _l2norm(k)
            v = v * beta[..., None]
            k_beta = k * beta[..., None]
            rs = lambda t: t.reshape(b, h, n, CHUNK, -1)
            q, k, v, k_beta = (rs(q), rs(k), rs(v), rs(k_beta))
            eye = jnp.eye(CHUNK, dtype=q.dtype)
            strict_lower = jnp.tril(jnp.ones((CHUNK, CHUNK), bool), -1)
            A = jnp.where(strict_lower, jnp.einsum('bhncd,bhnsd->bhncs', k_beta, k), 0.0)
            attn_inv = jax.scipy.linalg.solve_triangular(eye + A, jnp.broadcast_to(eye, A.shape), lower=True)
            u = attn_inv @ v
            w = attn_inv @ k_beta
            incl_lower = jnp.tril(jnp.ones((CHUNK, CHUNK), bool))

            def step(S, inp):
                q_i, k_i, u_i, w_i = inp
                attn_local = jnp.where(incl_lower, q_i @ jnp.swapaxes(k_i, -1, -2), 0.0)
                u_t = u_i - w_i @ S
                o_i = q_i @ S + attn_local @ u_t
                return (S + jnp.swapaxes(k_i, -1, -2) @ u_t, o_i)
            S0 = jnp.zeros((b, h, dk, dv), q.dtype)
            xs = tuple((jnp.moveaxis(t, 2, 0) for t in (q, k, u, w)))
            S, out = jax.lax.scan(step, S0, xs)
            return (jnp.moveaxis(out, 0, 2).reshape(b, h, L, dv), S)

        def _stats(x):
            return jnp.stack([x.mean(-1), x.var(-1), jnp.abs(x).mean(-1), jnp.sqrt(jnp.sum(x * x, -1))], -1)

        def _forward(x, Wq, Wk, Wv, Wb, conv_q, conv_k, conv_v, fir_long, fir_short, W1, b1, W2, b2, log_temp, base_bias, conv_residual_logit, rms_w, Wo):
            B, L, D = x.shape
            q = _silu(_causal_dwconv(x @ Wq, conv_q)).reshape(B, L, H, DK)
            k = _silu(_causal_dwconv(x @ Wk, conv_k)).reshape(B, L, H, DK)
            v = _silu(_causal_dwconv(x @ Wv, conv_v)).reshape(B, L, H, DV)
            beta = jax.nn.sigmoid(x @ Wb)
            delta, _S = _delta_rule_chunkwise(q.transpose(0, 2, 1, 3), k.transpose(0, 2, 1, 3), v.transpose(0, 2, 1, 3), beta.transpose(0, 2, 1))
            delta = delta.transpose(0, 2, 1, 3)
            f_short = _fir(v, fir_short)
            f_long = _fir(v, fir_long)
            stats = jnp.concatenate([_stats(f_short), _stats(f_long), _stats(delta), _stats(v)], -1)
            hidden_exp = jnp.broadcast_to(x[:, :, None, :], (B, L, H, D))
            gate_in = jnp.concatenate([hidden_exp, stats], -1)
            h1 = jax.nn.gelu(gate_in @ W1 + b1, approximate=False)
            logits = h1 @ W2 + b2 + base_bias
            temp = jax.nn.softplus(log_temp) + 0.0001
            p = jax.nn.softmax(logits / temp[:, None], -1)
            eps = 0.05
            p = jnp.maximum(p, jnp.array([eps, eps, 0.0, 0.0], p.dtype))
            p = p / jnp.sum(p, -1, keepdims=True)
            o = p[..., 0:1] * f_short + p[..., 1:2] * f_long + p[..., 2:3] * delta + p[..., 3:4] * v
            o = o + 0.5 * jax.nn.sigmoid(conv_residual_logit)[None, None, :, None] * f_short
            o = _rmsnorm(o, rms_w)
            return o.reshape(B, L, H * DV) @ Wo
        key = jax.random.key(seed)
        ks = jax.random.split(key, 13)
        B, L, D = (2, 512, 256)
        f = jnp.float32
        n = lambda k, shape, s=0.02: jax.random.normal(k, shape, f) * s
        return {'x': jax.random.normal(ks[0], (B, L, D), f), 'Wq': n(ks[1], (D, D)), 'Wk': n(ks[2], (D, D)), 'Wv': n(ks[3], (D, D)), 'Wb': n(ks[4], (D, H)), 'conv_q': n(ks[5], (D, 4), 0.1), 'conv_k': n(ks[6], (D, 4), 0.1), 'conv_v': n(ks[7], (D, 4), 0.1), 'fir_long': n(ks[8], (H, DV, 64)), 'fir_short': n(ks[9], (H, DV, 5)), 'W1': n(ks[10], (D + 16, D)), 'b1': jnp.zeros((D,), f), 'W2': n(ks[11], (D, 4)), 'b2': jnp.zeros((4,), f), 'log_temp': jnp.full((H,), float(np.log(np.expm1(0.7))), f), 'base_bias': jnp.tile(jnp.array([-0.5, -0.5, 1.0, 3.0], f), (H, 1)), 'conv_residual_logit': jnp.full((H,), -2.0, f), 'rms_w': jnp.ones((DV,), f), 'Wo': n(ks[12], (D, D))}
    _L0_attn_all = _L0_attn_setup()
    _L0_attn_in = {k: v for k, v in _L0_attn_all.items() if k in ('Wq', 'Wk', 'Wv', 'Wb', 'conv_q', 'conv_k', 'conv_v', 'fir_long', 'fir_short', 'W1', 'b1', 'W2', 'b2', 'log_temp', 'base_bias', 'conv_residual_logit', 'rms_w', 'Wo')}
    del _L0_attn_all

    def _L0_ffn_setup():
        import jax, jax.numpy as jnp
        import numpy as np
        B, L, D = (4, 512, 256)
        H = 16
        E = 16
        NS = 16
        S = NS // E
        F = 1024
        EPS = 1e-05

        def _layernorm(x, g, b):
            mu = jnp.mean(x, axis=-1, keepdims=True)
            var = jnp.mean(jnp.square(x - mu), axis=-1, keepdims=True)
            return (x - mu) * jax.lax.rsqrt(var + EPS) * g + b

        def _mha(q, k, v, Wq, bq, Wk, bk, Wv, bv, Wo, bo):
            Bq, Lq, Dm = q.shape
            dh = Dm // H
            qh = (q @ Wq + bq).reshape(Bq, Lq, H, dh)
            kh = (k @ Wk + bk).reshape(Bq, -1, H, dh)
            vh = (v @ Wv + bv).reshape(Bq, -1, H, dh)
            scores = jnp.einsum('bqhd,bkhd->bhqk', qh, kh) / jnp.asarray(np.sqrt(dh), q.dtype)
            attn = jax.nn.softmax(scores, axis=-1)
            out = jnp.einsum('bhqk,bkhd->bqhd', attn, vh).reshape(Bq, Lq, Dm)
            return out @ Wo + bo
        key = jax.random.key(seed)
        ks = jax.random.split(key, 32)
        s = 0.02
        d = {}
        d['x'] = jax.random.normal(ks[0], (B, L, D), jnp.float32)
        d['slot_query'] = jax.random.normal(ks[1], (1, NS, D), jnp.float32) * 0.01
        for i, nm in enumerate(['d_Wq', 'd_Wk', 'd_Wv', 'd_Wo']):
            d[nm] = jax.random.normal(ks[2 + i], (D, D), jnp.float32) * s
        for nm in ['d_bq', 'd_bk', 'd_bv', 'd_bo']:
            d[nm] = jnp.zeros((D,), jnp.float32)
        for i, nm in enumerate(['c_Wq', 'c_Wk', 'c_Wv', 'c_Wo']):
            d[nm] = jax.random.normal(ks[6 + i], (D, D), jnp.float32) * s
        for nm in ['c_bq', 'c_bk', 'c_bv', 'c_bo']:
            d[nm] = jnp.zeros((D,), jnp.float32)
        d['e_ln_g'] = jnp.ones((E, D), jnp.float32)
        d['e_ln_b'] = jnp.zeros((E, D), jnp.float32)
        d['e_W1'] = jax.random.normal(ks[10], (E, D, F), jnp.float32) * s
        d['e_b1'] = jnp.zeros((E, F), jnp.float32)
        d['e_Wg'] = jax.random.normal(ks[11], (E, D, F), jnp.float32) * s
        d['e_bg'] = jnp.zeros((E, F), jnp.float32)
        d['e_W2'] = jax.random.normal(ks[12], (E, F, D), jnp.float32) * s
        d['e_b2'] = jnp.zeros((E, D), jnp.float32)
        return d
    _L0_ffn_all = _L0_ffn_setup()
    _L0_ffn_in = {k: v for k, v in _L0_ffn_all.items() if k in ('slot_query', 'd_Wq', 'd_Wk', 'd_Wv', 'd_Wo', 'd_bq', 'd_bk', 'd_bv', 'd_bo', 'c_Wq', 'c_Wk', 'c_Wv', 'c_Wo', 'c_bq', 'c_bk', 'c_bv', 'c_bo', 'e_ln_g', 'e_ln_b', 'e_W1', 'e_b1', 'e_Wg', 'e_bg', 'e_W2', 'e_b2')}
    del _L0_ffn_all
    return {'x': x, 'L0_tok_emb0': _L0_tok_in['emb0'], 'L0_tok_w0': _L0_tok_in['w0'], 'L0_tok_emb1': _L0_tok_in['emb1'], 'L0_tok_w1': _L0_tok_in['w1'], 'L0_tok_emb2': _L0_tok_in['emb2'], 'L0_tok_w2': _L0_tok_in['w2'], 'L0_attn_Wq': _L0_attn_in['Wq'], 'L0_attn_Wk': _L0_attn_in['Wk'], 'L0_attn_Wv': _L0_attn_in['Wv'], 'L0_attn_Wb': _L0_attn_in['Wb'], 'L0_attn_conv_q': _L0_attn_in['conv_q'], 'L0_attn_conv_k': _L0_attn_in['conv_k'], 'L0_attn_conv_v': _L0_attn_in['conv_v'], 'L0_attn_fir_long': _L0_attn_in['fir_long'], 'L0_attn_fir_short': _L0_attn_in['fir_short'], 'L0_attn_W1': _L0_attn_in['W1'], 'L0_attn_b1': _L0_attn_in['b1'], 'L0_attn_W2': _L0_attn_in['W2'], 'L0_attn_b2': _L0_attn_in['b2'], 'L0_attn_log_temp': _L0_attn_in['log_temp'], 'L0_attn_base_bias': _L0_attn_in['base_bias'], 'L0_attn_conv_residual_logit': _L0_attn_in['conv_residual_logit'], 'L0_attn_rms_w': _L0_attn_in['rms_w'], 'L0_attn_Wo': _L0_attn_in['Wo'], 'L0_ffn_slot_query': _L0_ffn_in['slot_query'], 'L0_ffn_d_Wq': _L0_ffn_in['d_Wq'], 'L0_ffn_d_Wk': _L0_ffn_in['d_Wk'], 'L0_ffn_d_Wv': _L0_ffn_in['d_Wv'], 'L0_ffn_d_Wo': _L0_ffn_in['d_Wo'], 'L0_ffn_d_bq': _L0_ffn_in['d_bq'], 'L0_ffn_d_bk': _L0_ffn_in['d_bk'], 'L0_ffn_d_bv': _L0_ffn_in['d_bv'], 'L0_ffn_d_bo': _L0_ffn_in['d_bo'], 'L0_ffn_c_Wq': _L0_ffn_in['c_Wq'], 'L0_ffn_c_Wk': _L0_ffn_in['c_Wk'], 'L0_ffn_c_Wv': _L0_ffn_in['c_Wv'], 'L0_ffn_c_Wo': _L0_ffn_in['c_Wo'], 'L0_ffn_c_bq': _L0_ffn_in['c_bq'], 'L0_ffn_c_bk': _L0_ffn_in['c_bk'], 'L0_ffn_c_bv': _L0_ffn_in['c_bv'], 'L0_ffn_c_bo': _L0_ffn_in['c_bo'], 'L0_ffn_e_ln_g': _L0_ffn_in['e_ln_g'], 'L0_ffn_e_ln_b': _L0_ffn_in['e_ln_b'], 'L0_ffn_e_W1': _L0_ffn_in['e_W1'], 'L0_ffn_e_b1': _L0_ffn_in['e_b1'], 'L0_ffn_e_Wg': _L0_ffn_in['e_Wg'], 'L0_ffn_e_bg': _L0_ffn_in['e_bg'], 'L0_ffn_e_W2': _L0_ffn_in['e_W2'], 'L0_ffn_e_b2': _L0_ffn_in['e_b2']}

def reference(x, L0_tok_emb0, L0_tok_w0, L0_tok_emb1, L0_tok_w1, L0_tok_emb2, L0_tok_w2, L0_attn_Wq, L0_attn_Wk, L0_attn_Wv, L0_attn_Wb, L0_attn_conv_q, L0_attn_conv_k, L0_attn_conv_v, L0_attn_fir_long, L0_attn_fir_short, L0_attn_W1, L0_attn_b1, L0_attn_W2, L0_attn_b2, L0_attn_log_temp, L0_attn_base_bias, L0_attn_conv_residual_logit, L0_attn_rms_w, L0_attn_Wo, L0_ffn_slot_query, L0_ffn_d_Wq, L0_ffn_d_Wk, L0_ffn_d_Wv, L0_ffn_d_Wo, L0_ffn_d_bq, L0_ffn_d_bk, L0_ffn_d_bv, L0_ffn_d_bo, L0_ffn_c_Wq, L0_ffn_c_Wk, L0_ffn_c_Wv, L0_ffn_c_Wo, L0_ffn_c_bq, L0_ffn_c_bk, L0_ffn_c_bv, L0_ffn_c_bo, L0_ffn_e_ln_g, L0_ffn_e_ln_b, L0_ffn_e_W1, L0_ffn_e_b1, L0_ffn_e_Wg, L0_ffn_e_bg, L0_ffn_e_W2, L0_ffn_e_b2):
    import jax
    import jax.numpy as jnp

    def _L0_tok_ref(emb_input, emb0, w0, emb1, w1, emb2, w2):
        import jax, jax.numpy as jnp
        import numpy as np
        VOCAB = 50257
        D = 256
        EDGES = [0, 5000, 10000, VOCAB]
        HSZ = [256, 64, 64]
        B, S = emb_input.shape
        idx = emb_input.reshape(-1)
        clusters = [(emb0, w0), (emb1, w1), (emb2, w2)]
        out = jnp.zeros((idx.shape[0], D), dtype=jnp.float32)
        for i, (emb, w) in enumerate(clusters):
            lo, hi = (EDGES[i], EDGES[i + 1])
            mask = (idx >= lo) & (idx < hi)
            local = jnp.clip(idx - lo, 0, emb.shape[0] - 1)
            h = emb[local]
            proj = jnp.einsum('nh,dh->nd', h, w)
            out = out + jnp.where(mask[:, None], proj, 0.0)
        return out.reshape(B, S, D)

    def _L0_attn_ref(x, Wq, Wk, Wv, Wb, conv_q, conv_k, conv_v, fir_long, fir_short, W1, b1, W2, b2, log_temp, base_bias, conv_residual_logit, rms_w, Wo):
        import jax, jax.numpy as jnp
        import numpy as np
        H, DK, DV, CHUNK = (4, 64, 64, 32)

        def _silu(x):
            return x * jax.nn.sigmoid(x)

        def _l2norm(x, eps=1e-06):
            return x * jax.lax.rsqrt(jnp.sum(x * x, -1, keepdims=True) + eps)

        def _rmsnorm(x, w, eps=1e-05):
            return x * jax.lax.rsqrt(jnp.mean(x * x, -1, keepdims=True) + eps) * w

        def _causal_dwconv(x, w):
            C = x.shape[-1]
            K = w.shape[-1]
            xp = jnp.pad(x, ((0, 0), (K - 1, 0), (0, 0))).transpose(0, 2, 1)
            y = jax.lax.conv_general_dilated(xp, w[:, None, :], (1,), 'VALID', feature_group_count=C, dimension_numbers=('NCH', 'OIH', 'NCH'))
            return y.transpose(0, 2, 1)

        def _fir(x, filt):
            B, L, h, d = x.shape
            y = _causal_dwconv(x.reshape(B, L, h * d), filt.reshape(h * d, -1))
            return y.reshape(B, L, h, d)

        def _delta_rule_chunkwise(q, k, v, beta):
            b, h, L, dk = q.shape
            dv = v.shape[-1]
            n = L // CHUNK
            q = _l2norm(q)
            k = _l2norm(k)
            v = v * beta[..., None]
            k_beta = k * beta[..., None]
            rs = lambda t: t.reshape(b, h, n, CHUNK, -1)
            q, k, v, k_beta = (rs(q), rs(k), rs(v), rs(k_beta))
            eye = jnp.eye(CHUNK, dtype=q.dtype)
            strict_lower = jnp.tril(jnp.ones((CHUNK, CHUNK), bool), -1)
            A = jnp.where(strict_lower, jnp.einsum('bhncd,bhnsd->bhncs', k_beta, k), 0.0)
            attn_inv = jax.scipy.linalg.solve_triangular(eye + A, jnp.broadcast_to(eye, A.shape), lower=True)
            u = attn_inv @ v
            w = attn_inv @ k_beta
            incl_lower = jnp.tril(jnp.ones((CHUNK, CHUNK), bool))

            def step(S, inp):
                q_i, k_i, u_i, w_i = inp
                attn_local = jnp.where(incl_lower, q_i @ jnp.swapaxes(k_i, -1, -2), 0.0)
                u_t = u_i - w_i @ S
                o_i = q_i @ S + attn_local @ u_t
                return (S + jnp.swapaxes(k_i, -1, -2) @ u_t, o_i)
            S0 = jnp.zeros((b, h, dk, dv), q.dtype)
            xs = tuple((jnp.moveaxis(t, 2, 0) for t in (q, k, u, w)))
            S, out = jax.lax.scan(step, S0, xs)
            return (jnp.moveaxis(out, 0, 2).reshape(b, h, L, dv), S)

        def _stats(x):
            return jnp.stack([x.mean(-1), x.var(-1), jnp.abs(x).mean(-1), jnp.sqrt(jnp.sum(x * x, -1))], -1)

        def _forward(x, Wq, Wk, Wv, Wb, conv_q, conv_k, conv_v, fir_long, fir_short, W1, b1, W2, b2, log_temp, base_bias, conv_residual_logit, rms_w, Wo):
            B, L, D = x.shape
            q = _silu(_causal_dwconv(x @ Wq, conv_q)).reshape(B, L, H, DK)
            k = _silu(_causal_dwconv(x @ Wk, conv_k)).reshape(B, L, H, DK)
            v = _silu(_causal_dwconv(x @ Wv, conv_v)).reshape(B, L, H, DV)
            beta = jax.nn.sigmoid(x @ Wb)
            delta, _S = _delta_rule_chunkwise(q.transpose(0, 2, 1, 3), k.transpose(0, 2, 1, 3), v.transpose(0, 2, 1, 3), beta.transpose(0, 2, 1))
            delta = delta.transpose(0, 2, 1, 3)
            f_short = _fir(v, fir_short)
            f_long = _fir(v, fir_long)
            stats = jnp.concatenate([_stats(f_short), _stats(f_long), _stats(delta), _stats(v)], -1)
            hidden_exp = jnp.broadcast_to(x[:, :, None, :], (B, L, H, D))
            gate_in = jnp.concatenate([hidden_exp, stats], -1)
            h1 = jax.nn.gelu(gate_in @ W1 + b1, approximate=False)
            logits = h1 @ W2 + b2 + base_bias
            temp = jax.nn.softplus(log_temp) + 0.0001
            p = jax.nn.softmax(logits / temp[:, None], -1)
            eps = 0.05
            p = jnp.maximum(p, jnp.array([eps, eps, 0.0, 0.0], p.dtype))
            p = p / jnp.sum(p, -1, keepdims=True)
            o = p[..., 0:1] * f_short + p[..., 1:2] * f_long + p[..., 2:3] * delta + p[..., 3:4] * v
            o = o + 0.5 * jax.nn.sigmoid(conv_residual_logit)[None, None, :, None] * f_short
            o = _rmsnorm(o, rms_w)
            return o.reshape(B, L, H * DV) @ Wo
        return _forward(x, Wq, Wk, Wv, Wb, conv_q, conv_k, conv_v, fir_long, fir_short, W1, b1, W2, b2, log_temp, base_bias, conv_residual_logit, rms_w, Wo)

    def _L0_ffn_ref(x, slot_query, d_Wq, d_Wk, d_Wv, d_Wo, d_bq, d_bk, d_bv, d_bo, c_Wq, c_Wk, c_Wv, c_Wo, c_bq, c_bk, c_bv, c_bo, e_ln_g, e_ln_b, e_W1, e_b1, e_Wg, e_bg, e_W2, e_b2):
        import jax, jax.numpy as jnp
        import numpy as np
        B, L, D = (4, 512, 256)
        H = 16
        E = 16
        NS = 16
        S = NS // E
        F = 1024
        EPS = 1e-05

        def _layernorm(x, g, b):
            mu = jnp.mean(x, axis=-1, keepdims=True)
            var = jnp.mean(jnp.square(x - mu), axis=-1, keepdims=True)
            return (x - mu) * jax.lax.rsqrt(var + EPS) * g + b

        def _mha(q, k, v, Wq, bq, Wk, bk, Wv, bv, Wo, bo):
            Bq, Lq, Dm = q.shape
            dh = Dm // H
            qh = (q @ Wq + bq).reshape(Bq, Lq, H, dh)
            kh = (k @ Wk + bk).reshape(Bq, -1, H, dh)
            vh = (v @ Wv + bv).reshape(Bq, -1, H, dh)
            scores = jnp.einsum('bqhd,bkhd->bhqk', qh, kh) / jnp.asarray(np.sqrt(dh), q.dtype)
            attn = jax.nn.softmax(scores, axis=-1)
            out = jnp.einsum('bhqk,bkhd->bqhd', attn, vh).reshape(Bq, Lq, Dm)
            return out @ Wo + bo
        Bx = x.shape[0]
        q = jnp.broadcast_to(slot_query, (Bx, NS, D))
        o = q + _mha(q, x, x, d_Wq, d_bq, d_Wk, d_bk, d_Wv, d_bv, d_Wo, d_bo)
        os = o.reshape(Bx, E, S, D)
        h = _layernorm(os, e_ln_g[None, :, None, :], e_ln_b[None, :, None, :])
        u = jax.nn.silu(jnp.einsum('besd,edf->besf', h, e_W1) + e_b1[None, :, None, :])
        g = jax.nn.silu(jnp.einsum('besd,edf->besf', h, e_Wg) + e_bg[None, :, None, :])
        y = jnp.einsum('besf,efd->besd', u * g, e_W2) + e_b2[None, :, None, :]
        o = o + y.reshape(Bx, NS, D)
        out = _mha(x, o, o, c_Wq, c_bq, c_Wk, c_bk, c_Wv, c_bv, c_Wo, c_bo)
        return out
    h = _L0_tok_ref(x, L0_tok_emb0, L0_tok_w0, L0_tok_emb1, L0_tok_w1, L0_tok_emb2, L0_tok_w2)
    h = h + _L0_attn_ref(_layernorm(h, axis=-1), L0_attn_Wq, L0_attn_Wk, L0_attn_Wv, L0_attn_Wb, L0_attn_conv_q, L0_attn_conv_k, L0_attn_conv_v, L0_attn_fir_long, L0_attn_fir_short, L0_attn_W1, L0_attn_b1, L0_attn_W2, L0_attn_b2, L0_attn_log_temp, L0_attn_base_bias, L0_attn_conv_residual_logit, L0_attn_rms_w, L0_attn_Wo)
    h = h + _L0_ffn_ref(_layernorm(h, axis=-1), L0_ffn_slot_query, L0_ffn_d_Wq, L0_ffn_d_Wk, L0_ffn_d_Wv, L0_ffn_d_Wo, L0_ffn_d_bq, L0_ffn_d_bk, L0_ffn_d_bv, L0_ffn_d_bo, L0_ffn_c_Wq, L0_ffn_c_Wk, L0_ffn_c_Wv, L0_ffn_c_Wo, L0_ffn_c_bq, L0_ffn_c_bk, L0_ffn_c_bv, L0_ffn_c_bo, L0_ffn_e_ln_g, L0_ffn_e_ln_b, L0_ffn_e_W1, L0_ffn_e_b1, L0_ffn_e_Wg, L0_ffn_e_bg, L0_ffn_e_W2, L0_ffn_e_b2)
    return h

_drawn_inputs = setup_inputs


def setup_inputs(seed=0):
    import zlib

    import numpy as np

    out = dict(_drawn_inputs(seed))
    spreads = {'L0_attn_b1': (0.0, 0.8),
     'L0_attn_b2': (0.0, 0.8),
     'L0_attn_log_temp': (0.013658997602760792, 0.6),
     'L0_attn_conv_residual_logit': (-2.0, 0.6),
     'L0_attn_rms_w': (1.0, 0.2),
     'L0_ffn_d_bq': (0.0, 0.8),
     'L0_ffn_d_bk': (0.0, 2.0),
     'L0_ffn_d_bv': (0.0, 0.76),
     'L0_ffn_d_bo': (0.0, 0.283),
     'L0_ffn_c_bq': (0.0, 0.8),
     'L0_ffn_c_bk': (0.0, 2.0),
     'L0_ffn_c_bv': (0.0, 0.8),
     'L0_ffn_c_bo': (0.0, 0.384),
     'L0_ffn_e_ln_g': (1.0, 0.6),
     'L0_ffn_e_ln_b': (0.0, 0.8),
     'L0_ffn_e_b1': (0.0, 0.8),
     'L0_ffn_e_bg': (0.0, 0.8),
     'L0_ffn_e_b2': (0.0, 0.8)}
    factors = {'L0_attn_Wb': 8.0,
     'L0_attn_fir_long': 6.999,
     'L0_attn_fir_short': 8.0,
     'L0_attn_W1': 8.0,
     'L0_attn_W2': 8.0,
     'L0_ffn_slot_query': 8.0,
     'L0_ffn_d_Wq': 8.0,
     'L0_ffn_d_Wk': 8.0,
     'L0_ffn_d_Wv': 8.0,
     'L0_ffn_d_Wo': 6.088,
     'L0_ffn_c_Wq': 8.0,
     'L0_ffn_c_Wk': 8.0,
     'L0_ffn_e_W1': 8.0,
     'L0_ffn_e_Wg': 8.0,
     'L0_ffn_e_W2': 8.0}
    for name, (base, spread) in spreads.items():
        noise = np.random.default_rng([zlib.crc32(name.encode()), seed]).standard_normal(out[name].shape)
        drawn = base * np.exp(spread * noise) if base else spread * noise
        out[name] = jnp.asarray(drawn.astype(out[name].dtype))
    for name, factor in factors.items():
        out[name] = (out[name] * factor).astype(out[name].dtype)
    return out
```

```python
from contextlib import ExitStack
from math import sqrt

import concourse.bass as bass
from concourse import mybir

F32 = mybir.dt.float32
I32 = mybir.dt.int32
U32 = mybir.dt.uint32
ALU = mybir.AluOpType
ACT = mybir.ActivationFunctionType
AX = mybir.AxisListType

P = 128
D = 256
KD = D // P
T = 1024
NT = T // P
EDGES = (0, 5000, 10000, 50257)
EMB_W = (256, 64, 64)
KE = sum(EMB_W) // P
H, DH = 4, 64
TAPS = 4
FIR = (5, 64)
FPAD = 320
FW = (132, 192)
LEVELS = 6
AH, AD = 16, 16
NS = 16
FF = 1024


def rows_of(h):
    r = 64 * (h % 2)
    return slice(r, r + 64), h // 2


def setup(nc, ctx, A, K, dram, ps):
    sem = lambda n: ctx.enter_context(nc.semaphore(n))
    wl, cl, fl = sem("weights_loaded"), sem("consts_loaded"), sem("filters_loaded")
    pool_c, vst, pe_c, pad_st = sem("pool_consts"), sem("setup_vector_step"), sem("setup_pe_group"), sem("padded_stored")
    act_c = sem("setup_scalar_step")
    NB = A["x"].shape[0]
    NTT = NB * NT
    with ExitStack() as tmp, nc.Block() as block:
        sb = lambda n, shape, dt=F32: tmp.enter_context(nc.sbuf_tensor(n, shape, dt))
        wcat = sb("wcat", [P, KD, KE * P])
        ids_row = sb("ids_row", [NTT, P], I32)
        ids_rf = sb("ids_rf", [NTT, P])
        idf = sb("idf", [P, NTT])
        t1 = sb("t1", [P, NTT])
        t2 = sb("t2", [P, NTT])
        firw = [sb(f"firw{f}", [P, KD, FIR[f]]) for f in range(2)]
        padded = [sb(f"padded{f}", [P, KD, FPAD]) for f in range(2)]
        lt = sb("lt", [P, 8, 4])

        @block.sync
        def _(sp):
            col = 0
            for i, w in enumerate(EMB_W):
                sp.dma_start(wcat[:, :, col:col + w], A[f"L0_tok_w{i}"].rearrange("(k p) n -> p k n", p=P)).then_inc(wl, 16)
                col += w
            sp.dma_start(ids_row[:], A["x"].rearrange("b (t p) -> (b t) p", p=P)).then_inc(wl, 16)
            for f, n in enumerate(("L0_attn_fir_short", "L0_attn_fir_long")):
                sp.dma_start(firw[f][:], A[n].rearrange("h d t -> (h d) t").rearrange("(k p) t -> p k t", p=P)).then_inc(fl, 16)
            for n in ("Wq", "Wk", "Wv", "Wo"):
                sp.dma_start(K[n][:], A["L0_attn_" + n].rearrange("(k p) n -> p k n", p=P)).then_inc(cl, 16)
            sp.dma_start(K["W1x"][:], A["L0_attn_W1"][0:D, :].rearrange("(k p) n -> p k n", p=P)).then_inc(cl, 16)
            for h in range(H):
                sp.dma_start(K["W1s"][32 * h:32 * h + 16, :], A["L0_attn_W1"][D:D + 16, :]).then_inc(cl, 16)
            sp.dma_start(K["W2"][:], A["L0_attn_W2"].rearrange("(k p) n -> p k n", p=P)).then_inc(cl, 16)
            sp.dma_start(K["Wb"][:], A["L0_attn_Wb"].rearrange("(k p) n -> p k n", p=P)).then_inc(cl, 16)
            sp.wait_ge(vst, 20)
            for f in range(2):
                sp.dma_start(dram["fpad"][f].rearrange("(k p) t -> p k t", p=P), padded[f][:]).then_inc(pad_st, 16)
            sp.wait_ge(pad_st, 32)
            sp.wait_ge(cl, 16 * 17)

        @block.scalar
        def _(act):
            for j, n in enumerate(("conv_v", "conv_k", "conv_q")):
                act.dma_start(K["convw"][:, 2 * j:2 * j + 2, :], A["L0_attn_" + n].rearrange("(k p) t -> p k t", p=P)).then_inc(cl, 16)
            act.dma_start(K["b1"][:], A["L0_attn_b1"].rearrange("(k p o) -> p k o", p=P, o=1), allow_slow_non_contiguous=True).then_inc(cl, 16)
            for r in range(2):
                act.dma_start(K["rmsw"][64 * r:64 * r + 64, :], A["L0_attn_rms_w"].rearrange("(p o) -> p o", o=1)).then_inc(cl, 16)
            rowb = lambda ap, n: bass.AP(ap.tensor, 0, [[0, P], [1, n]])
            act.dma_start(K["lbias"][:], rowb(A["L0_attn_base_bias"], 16)).then_inc(fl, 16)
            act.dma_start(lt[:, 0, :], rowb(A["L0_attn_b2"], 4)).then_inc(fl, 16)
            act.dma_start(lt[:, 1, :], rowb(A["L0_attn_log_temp"], 4)).then_inc(fl, 16)
            act.dma_start(lt[:, 2, :], rowb(A["L0_attn_conv_residual_logit"], 4)).then_inc(fl, 16)
            act.wait_ge(fl, 16 * 6)
            nc.scalar.activation(lt[:, 3, :], lt[:, 1, :], ACT.Abs).then_inc(act_c, 1)
            act.wait_ge(act_c, 1)
            nc.scalar.activation(lt[:, 4, :], lt[:, 3, :], ACT.Exp, scale=-1.0).then_inc(act_c, 1)
            nc.scalar.activation(lt[:, 5, :], lt[:, 2, :], ACT.Exp, scale=-1.0).then_inc(act_c, 1)
            act.wait_ge(vst, 22)
            nc.scalar.activation(lt[:, 4, :], lt[:, 4, :], ACT.Ln).then_inc(act_c, 1)

        @block.gpsimd
        def _(pool):
            n = [0]

            def keep(where, cmp, fill, base, pattern, mult, before=None):
                pool.wait_ge(pool_c, n[0])
                nc.gpsimd.affine_select(out=where, in_=where, compare_op=cmp, fill=fill, base=base,
                                        pattern=pattern, channel_multiplier=mult).then_inc(pool_c, 1)
                n[0] += 1
                return n[0]

            def fill(where, value):
                if n[0]:
                    pool.wait_ge(pool_c, n[0])
                nc.gpsimd.memset(where, value).then_inc(pool_c, 1)
                n[0] += 1
                return n[0]

            keep(K["ident"][:], ALU.not_equal, 1.0, 0, [[-1, P]], 1, fill(K["ident"][:], 0.0))
            keep(K["up_strict"][:], ALU.is_gt, 0.0, 0, [[1, P]], -1, fill(K["up_strict"][:], 1.0))
            keep(K["up_incl"][:], ALU.is_ge, 0.0, 0, [[1, P]], -1, fill(K["up_incl"][:], 1.0))
            keep(K["anti"][:], ALU.not_equal, 1.0, 1 - P, [[1, P]], 1, fill(K["anti"][:], 0.0))
            at = fill(K["sel2"][:], 0.0)
            pool.wait_ge(pool_c, at)
            fill(K["sel2"][0:64, 0:1], 1.0)
            fill(K["sel2"][64:128, 1:2], 1.0)
            for l in range(LEVELS):
                m = 2 << l
                w = K["wmask"][:, l, :]
                v = w.rearrange("i (g two m) -> i g two m", two=2, m=m)
                at = fill(w, 0.0)
                pool.wait_ge(pool_c, at)
                at = fill(v[:, :, 0, :], -1.0)
                at = keep(v[:, :, 0, :], ALU.is_ge, 0.0, -m, [[-2 * m, P // (2 * m)], [0, m]], 1, at)
                at = keep(v[:, :, 0, :], ALU.is_ge, 0.0, 2 * m - 1, [[2 * m, P // (2 * m)], [0, m]], -1, at)
                keep(w, ALU.not_equal, 1.0, 0, [[-1, P]], 1, at)
            w = K["w1t"]
            v = w[:].rearrange("p (g two) -> p g two", two=2)
            at = fill(w[:], 0.0)
            at = keep(v[:, :, 1], ALU.not_equal, -1.0, 0, [[-2, P // 2]], 1, at)
            keep(w[:], ALU.not_equal, 1.0, 0, [[-1, P]], 1, at)
            hm = K["hmask"]
            at = fill(hm[:], 1.0)
            for k in range(KD):
                at = keep(hm[:, k, :], ALU.is_ge, 0.0, k * P, [[-AD, AH]], 1, at)
                at = keep(hm[:, k, :], ALU.is_ge, 0.0, AD - 1 - k * P, [[AD, AH]], -1, at)
            fill(K["qsel"][:], 0.0)
            for g in range(P // NS):
                keep(K["qsel"][:], ALU.not_equal, 1.0, -NS * g, [[-1, NS]], 1)
            fill(K["ones"][:], 1.0)
            pool.wait_ge(pool_c, n[0])

        @block.tensor
        def _(pe):
            pe.wait_ge(pool_c, 2)
            pe.wait_ge(wl, 64)
            for k in range(KE):
                for dh in range(KD):
                    n = k * KD + dh
                    last = nc.tensor.transpose(ps[n // 4][:, (n % 4) * P:(n % 4 + 1) * P], wcat[:, dh, k * P:(k + 1) * P], K["ident"][:])
            last.then_inc(pe_c, 1)
            pe.wait_ge(vst, 1)
            nc.tensor.transpose(ps[2][:, 0:NTT], ids_rf[:], K["ident"][0:NTT, 0:NTT]).then_inc(pe_c, 1)

        @block.vector
        def _(v):
            n = [0]

            def step(ins, fence=True):
                ins.then_inc(vst, 1)
                n[0] += 1
                if fence:
                    v.wait_ge(vst, n[0])

            v.wait_ge(wl, 64)
            step(nc.vector.tensor_copy(ids_rf[:], ids_row[:]))
            v.wait_ge(pe_c, 1)
            step(nc.vector.tensor_copy(K["WcT"][:, 0:2, :], ps[0][:].rearrange("p (k n) -> p k n", k=2)), False)
            step(nc.vector.tensor_copy(K["WcT"][:, 2, :], ps[1][:, 0:D]), False)
            v.wait_ge(pe_c, 2)
            step(nc.vector.tensor_copy(idf[:], ps[2][:, 0:NTT]))
            for i in range(3):
                lo, hi = EDGES[i], EDGES[i + 1]
                step(nc.vector.tensor_scalar(t1[:], idf[:], float(-lo), 0.0, ALU.add, ALU.max), False)
                step(nc.vector.tensor_scalar(t2[:], idf[:], float(lo), None, ALU.is_ge))
                step(nc.vector.tensor_scalar(K["rows"][:, i, :], t1[:], float(hi - lo - 1), None, ALU.min), False)
                step(nc.vector.scalar_tensor_tensor(K["mask"][:, i, :], idf[:], float(hi), t2[:], ALU.is_lt, ALU.mult))
            assert n[0] == 16
            v.wait_ge(fl, 16 * 6)
            for f in range(2):
                step(nc.vector.memset(padded[f][:], 0.0))
                a = firw[f][:]
                back = bass.AP(a.tensor, a.offset + FIR[f] - 1, [a.ap[0], [FIR[f], KD], [-1, FIR[f]]])
                step(nc.vector.tensor_copy(padded[f][:, :, P - 1:P - 1 + FIR[f]], back))
            assert n[0] == 20
            v.wait_ge(act_c, 3)
            step(nc.vector.tensor_scalar(lt[:, 5, :], lt[:, 5, :], 1.0, None, ALU.add))
            step(nc.vector.tensor_scalar(lt[:, 4, :], lt[:, 4, :], 1.0, None, ALU.add))
            v.wait_ge(act_c, 4)
            step(nc.vector.tensor_scalar(lt[:, 6, :], lt[:, 1, :], 0.0, 1e-4, ALU.max, ALU.add))
            step(nc.vector.tensor_tensor(lt[:, 6, :], lt[:, 6, :], lt[:, 4, :], ALU.add))
            step(nc.vector.reciprocal(K["itemp"][:], lt[:, 6, :]))
            step(nc.vector.tensor_copy(K["itemp16"][:].rearrange("p (h j) -> p h j", h=H), K["itemp"][:].unsqueeze(2).to_broadcast([P, H, 4])))
            step(nc.vector.reciprocal(lt[:, 7, :], lt[:, 5, :]))
            step(nc.vector.tensor_scalar(K["halfsig"][:], lt[:, 7, :], 0.5, None, ALU.mult))
            step(nc.vector.tensor_tensor(K["lbias"][:].rearrange("p (h j) -> p h j", h=H), K["lbias"][:].rearrange("p (h j) -> p h j", h=H),
                                         lt[:, 0, :].unsqueeze(1).to_broadcast([P, H, 4]), ALU.add))
            v.wait_ge(cl, 16 * 17)
            for k in range(KD):
                step(nc.vector.tensor_scalar(K["Wo"][:, k, :], K["Wo"][:, k, :], K["rmsw"][:, 0:1], None, ALU.mult), False)
            v.wait_ge(vst, n[0])


def delta_phase(nc, ctx, A, K, dram, ps):
    NB = A["x"].shape[0]
    names = ["gathered", "rows_copied", "rows_masked", "gt_ps", "gt_sb", "h_ps", "h_sb", "h_stored", "ln_stats", "ln_aggr", "ln_eps",
             "ln_std", "ln_rstd", "xn_done", "xt_ps", "xt_sb", "pj_ps", "pj_sb", "conv_step", "silu_done", "sq_done", "ss_ps",
             "norm_eps", "norm_root", "norm_inv", "gamma_sq", "gamma_done", "tm_ps", "tm_sb", "vk_done", "v_stored", "xw1_stored",
             "gk_ps", "qk_ps", "at_sb", "qkt_sb", "a1_sb", "x1t_sb", "x1_ps", "p_ps", "q_sb", "x_ps", "x_sb", "xt2_ps", "xt2_sb",
             "ks_ps", "r_sb", "y_ps", "z_sb", "ds_ps", "s_sb", "o_ps", "o_sb", "delta_stored", "pads", "gather_go", "ln_go"]
    S = {n: nc.alloc_semaphore(name=n) for n in names}

    with ExitStack() as tmp, nc.Block() as block:
        sb = lambda n, shape, dt=F32: tmp.enter_context(nc.sbuf_tensor(n, shape, dt))
        rowsb = sb("rowsb", [P, 3, NT], U32)
        G = sb("G", [P, NT, KE * P])
        GT = sb("GT", [P, KE, T])
        h_tm = sb("h_tm", [P, NT, D])
        stats = sb("stats", [P, NT, 6])
        mv = sb("mv", [P, NT, 2])
        rstd = sb("rstd", [P, 3, NT])
        xn = sb("xn", [P, NT, D])
        xnT = sb("xnT", [P, KD, T])
        raw = sb("raw", [P, 6, TAPS - 1 + T])
        cm = sb("cm", [P, 6, T])
        beta = sb("beta", [P, NT * H])
        nrm = sb("nrm", [P, 2, NT * H])
        inv = sb("inv", [P, 2, NT * H])
        gam = sb("gam", [P, 2, NT * H])
        xw1 = sb("xw1", [P, KD, T])
        v_tm = sb("v_tm", [P, NT, D])
        k_tm = sb("k_tm", [P, NT, D])
        vk = sb("vk", [P, NT, D])
        dl = sb("dl", [P, NT, D])
        AT = [sb(f"AT{j}", [P, H, P]) for j in range(2)]
        A1T = [sb(f"A1T{j}", [P, H, P]) for j in range(2)]
        X = [sb(f"X{j}", [P, H, P]) for j in range(2)]
        Q = [sb(f"Q{j}", [P, H, P]) for j in range(2)]
        XT = [sb(f"XT{j}", [P, H, P]) for j in range(4)]
        QKT = sb("QKT", [P, 4, H, P])
        St = sb("St", [P, 2, 2, DH])
        R = sb("R", [P, D])
        z = sb("z", [P, D])

        sq = raw[:, 2:6, TAPS - 1:]
        g4 = lambda bank: ps[bank][:].rearrange("p (h n) -> p h n", h=H)
        h4 = lambda bank: ps[bank][:, 0:D].rearrange("p (h n) -> p h n", h=H)
        per_head = lambda a, t, n: a[:, t * H:(t + 1) * H].unsqueeze(2).to_broadcast([P, H, n])
        by_head = lambda a: a.rearrange("p (h n) -> p h n", h=H)
        over_heads = lambda m: m.unsqueeze(1).to_broadcast([P, H, P])
        conv_order = [(p, j, i) for p in range(3) for j in range(TAPS) for i in range(2)]

        @block.gpsimd
        def _(pool):
            def gather(b):
                pool.wait_ge(S["gathered"], b * (3 * NT * 16))
                pool.wait_ge(S["gt_ps"], b * 6)
                nc.gpsimd.tensor_copy(rowsb[:], K["rows"][:, :, bass.ds(b * NT, NT)]).then_inc(S["rows_copied"], 1)
                pool.wait_ge(S["rows_copied"], b + 1).then_inc(S["gather_go"], 1)
                for t in range(NT):
                    col = 0
                    for i in range(3):
                        nc.gpsimd.indirect_dma_start(G[:, t, col:col + EMB_W[i]], None, A[f"L0_tok_emb{i}"],
                                                     bass.IndirectOffsetOnAxis(ap=rowsb[:, i, t:t + 1], axis=0)).then_inc(S["gathered"], 16)
                        col += EMB_W[i]

            def sequence(b, more):
                if more:
                    gather(b + 1)
                pool.wait_ge(S["norm_root"], b + 1)
                pool.wait_ge(S["tm_sb"], b * 8 + 4)
                nc.gpsimd.tensor_tensor(vk[:].rearrange("p t (h n) -> p (t h) n", h=H), v_tm[:].rearrange("p t (h n) -> p (t h) n", h=H),
                                        nrm[:, 0, :].unsqueeze(2).to_broadcast([P, NT * H, DH]), ALU.mult).then_inc(S["vk_done"], 1)
                for t in range(NT):
                    pool.wait_ge(S["at_sb"], b * 32 + 4 * t + 4)
                    nc.gpsimd.tensor_tensor(A1T[t % 2][:], AT[t % 2][:], over_heads(K["ident"][:]), ALU.add).then_inc(S["a1_sb"], 1)
                    pool.wait_ge(S["a1_sb"], b * NT + t + 1)
                    nc.gpsimd.tensor_tensor(XT[t % 4][:], A1T[t % 2][:], over_heads(K["w1t"][:]), ALU.mult).then_inc(S["x1t_sb"], 1)

            gather(0)
            with pool.Fori(0, NB - 1) as b:
                sequence(b, True)
            sequence(NB - 1, False)

        @block.sync
        def _(sp):
            with sp.Fori(0, NB) as b:
                sp.wait_ge(S["h_sb"], b * 4 + 4)
                sp.dma_start(dram["h"][:, bass.ds(b * NT, NT), :], h_tm[:]).then_inc(S["h_stored"], 16)
                sp.wait_ge(S["pj_sb"], b * 17 + 17)
                sp.dma_start(dram["xw1"][:, bass.ds(b * KD, KD), :], xw1[:]).then_inc(S["xw1_stored"], 16)
                sp.wait_ge(S["tm_sb"], b * 8 + 4)
                sp.dma_start(dram["v"][:, bass.ds(b * NT, NT), :], v_tm[:]).then_inc(S["v_stored"], 16)
                sp.wait_ge(S["o_sb"], b * 2 * NT + 2 * NT)
                sp.dma_start(dram["delta"][:, bass.ds(b * NT, NT), :], dl[:]).then_inc(S["delta_stored"], 16)
            for n in ("h_stored", "xw1_stored", "v_stored", "delta_stored"):
                sp.wait_ge(S[n], 16 * NB)

        @block.tensor
        def _(pe):
            ident = K["ident"][:]

            def inverse(b, p, s):
                tiles = (2 * p, 2 * p + 1)
                if s == 0:
                    if p:
                        pe.wait_ge(S["xt2_sb"], b * 48 + p * 12)
                    for w, done in ((2, "gk_ps"), (4, "qk_ps")):
                        for t in tiles:
                            tk = slice(t * P, (t + 1) * P)
                            for h in range(H):
                                rows, i = rows_of(h)
                                last = nc.tensor.matmul(g4(w - 2 + h % 2)[:, 2 * (t % 2) + i, :], cm[rows, 2 + i, tk], cm[rows, w + i, tk],
                                                        start=True, stop=True)
                        last.then_inc(S[done], 1)
                    for t in tiles:
                        j = t % 2
                        pe.wait_ge(S["x1t_sb"], b * NT + t + 1)
                        for h in range(H):
                            last = nc.tensor.transpose(g4(4 + j)[:, h, :], XT[t % 4][:, h, :], ident)
                        last.then_inc(S["x1_ps"], 1)
                    return
                l = s - 1
                for t in tiles:
                    j = t % 2
                    pe.wait_ge(S["x_sb"], b * 48 + p * 12 + 2 * l + j + 1)
                    if l:
                        pe.wait_ge(S["xt2_sb"], b * 48 + p * 12 + 2 * l + j - 1)
                    for h in range(H):
                        last = nc.tensor.matmul(g4(j)[:, h, :], A1T[j][:, h, :], X[j][:, h, :], start=True, stop=True)
                    last.then_inc(S["p_ps"], 1)

            def inverse_rest(b, p, s):
                l = s - 1
                for t in (2 * p, 2 * p + 1):
                    j = t % 2
                    pe.wait_ge(S["q_sb"], b * 48 + p * 12 + 2 * l + j + 1)
                    if l == 0:
                        pe.wait_ge(S["qkt_sb"], b * NT + 2 * p + 2)
                    if l < LEVELS - 1:
                        for h in range(H):
                            last = nc.tensor.matmul(g4(2 + j)[:, h, :], XT[t % 4][:, h, :], Q[j][:, h, :], start=True, stop=True)
                        last.then_inc(S["x_ps"], 1)
                    for h in range(H):
                        last = nc.tensor.matmul(g4(4 + j)[:, h, :], Q[j][:, h, :], XT[t % 4][:, h, :], start=True, stop=True)
                    last.then_inc(S["xt2_ps"], 1)

            def scan(b, p, s):
                t = 2 * p + s // 3
                tk = slice(t * P, (t + 1) * P)
                if s % 3 == 0:
                    pe.wait_ge(S["s_sb"], b * (NT + 1) + t + 1)
                    pe.wait_ge(S["o_sb"], b * 2 * NT + 2 * t)
                    for h in range(H):
                        rows, i = rows_of(h)
                        last = nc.tensor.matmul(h4(6 + h % 2)[:, i, :], cm[rows, 2 + i, tk], St[rows, t % 2, i, :], start=True, stop=True)
                    last.then_inc(S["ks_ps"], 1)
                elif s % 3 == 1:
                    pe.wait_ge(S["r_sb"], b * 2 * NT + 2 * t + 2)
                    pe.wait_ge(S["xt2_sb"], b * 48 + 12 * p + 12)
                    for h in range(H):
                        last = nc.tensor.matmul(h4(6)[:, h, :], XT[t % 4][:, h, :], R[:, h * DH:(h + 1) * DH], start=True, stop=True)
                    last.then_inc(S["y_ps"], 1)
                else:
                    pe.wait_ge(S["z_sb"], b * NT + t + 1)
                    for h in range(H):
                        rows, i = rows_of(h)
                        last = nc.tensor.matmul(ps[7][rows, i * DH:(i + 1) * DH], k_tm[:, t, h * DH:(h + 1) * DH], z[:, h * DH:(h + 1) * DH],
                                                start=True, stop=True)
                    last.then_inc(S["ds_ps"], 1)
                    for h in (0, 2, 1, 3):
                        rows, i = rows_of(h)
                        if h == 1:
                            pe.wait_ge(S["s_sb"], b * (NT + 1) + t + 2)
                        nc.tensor.matmul(h4(6 + h % 2)[:, i, :], cm[rows, 4 + i, tk], St[rows, t % 2, i, :], start=True, stop=False)
                        last = nc.tensor.matmul(h4(6 + h % 2)[:, i, :], QKT[:, t % 4, h, :], z[:, h * DH:(h + 1) * DH], start=False, stop=True)
                    last.then_inc(S["o_ps"], 1)

            with pe.Fori(0, NB) as b:
                pe.wait_ge(S["rows_masked"], b * 3 + 3)
                pe.wait_ge(S["xt2_sb"], b * 48)
                for n in range(6):
                    if n >= 4:
                        pe.wait_ge(S["gt_sb"], b * 6 + n - 3)
                    half, k = n // 3, n % 3
                    for q in range(4):
                        last = nc.tensor.transpose(ps[n % 4][:, q * P:(q + 1) * P], G[:, 4 * half + q, k * P:(k + 1) * P], ident)
                    last.then_inc(S["gt_ps"], 1)
                pe.wait_ge(S["o_sb"], b * 2 * NT)
                for n in range(4):
                    pe.wait_ge(S["gt_sb"], b * 6 + (3 if n < 2 else 6))
                    for q in range(2):
                        t = 2 * n + q
                        for k in range(KE):
                            last = nc.tensor.matmul(ps[4 + n][:, q * D:(q + 1) * D], GT[:, k, t * P:(t + 1) * P], K["WcT"][:, k, :],
                                                    start=(k == 0), stop=(k == KE - 1))
                    last.then_inc(S["h_ps"], 1)
                for n in range(4):
                    half, k = n // 2, n % 2
                    pe.wait_ge(S["xn_done"], b * NT + 4 * half + 4)
                    for q in range(4):
                        last = nc.tensor.transpose(ps[n][:, q * P:(q + 1) * P], xn[:, 4 * half + q, k * P:(k + 1) * P], ident)
                    last.then_inc(S["xt_ps"], 1)
                pe.wait_ge(S["h_sb"], b * 4 + 4)
                pe.wait_ge(S["xt_sb"], b * 4 + 4)
                for t in range(NT):
                    for k in range(KD):
                        last = nc.tensor.matmul(ps[4][:, t * H:(t + 1) * H], xnT[:, k, t * P:(t + 1) * P], K["Wb"][:, k, :],
                                                start=(k == 0), stop=(k == KD - 1))
                last.then_inc(S["pj_ps"], 1)
                for n in range(1, 17):
                    if n >= 4:
                        pe.wait_ge(S["pj_sb"], b * 17 + n - 3)
                    w, m, c = (n - 1) // 4, (n - 1) // 2 % 2, (n - 1) % 2
                    for k in range(KD):
                        last = nc.tensor.matmul(ps[4 + n % 4][:], K[("Wv", "Wk", "Wq", "W1x")[w]][:, k, m * P:(m + 1) * P],
                                                xnT[:, k, c * 512:(c + 1) * 512], start=(k == 0), stop=(k == KD - 1))
                    last.then_inc(S["pj_ps"], 1)
                for n in range(8):
                    i, half = n // 2, n % 2
                    pe.wait_ge(S["silu_done"], b * 6 + i + 1)
                    if n < 4:
                        pe.wait_ge(S["pj_sb"], b * 17 + 14 + n)
                    else:
                        pe.wait_ge(S["tm_sb"], b * 8 + n - 3)
                    bank = (5, 6, 7, 4)[n % 4]
                    for q in range(4):
                        t = 4 * half + q
                        last = nc.tensor.transpose(ps[bank][:, q * P:(q + 1) * P], cm[:, i, t * P:(t + 1) * P], ident)
                    last.then_inc(S["tm_ps"], 1)
                pe.wait_ge(S["sq_done"], b * 4 + 4)
                for i in range(4):
                    for t in range(NT):
                        at = (i // 2) * NT * H + t * H + (i % 2) * 2
                        last = nc.tensor.matmul(ps[0][:, at:at + 2], sq[:, i, t * P:(t + 1) * P], K["sel2"][:], start=True, stop=True)
                last.then_inc(S["ss_ps"], 1)
                pe.wait_ge(S["norm_eps"], b + 1)
                pe.wait_ge(S["tm_sb"], b * 8 + 8)
                for p in range(NT // 2 + 1):
                    for s in range(LEVELS + 1):
                        if p < NT // 2:
                            inverse(b, p, s)
                        if p and s < 6:
                            scan(b, p - 1, s)
                        if p < NT // 2 and s:
                            inverse_rest(b, p, s)

        @block.scalar
        def _(act):
            ident_copy = lambda o, i: nc.scalar.activation(o, i, ACT.Copy)
            with act.Fori(0, NB) as b:
                for n in range(6):
                    act.wait_ge(S["gt_ps"], b * 6 + n + 1)
                    ident_copy(GT[:, n % 3, n // 3 * 512:(n // 3 + 1) * 512], ps[n % 4][:]).then_inc(S["gt_sb"], 1)
                act.wait_ge(S["h_stored"], b * 16)
                for n in range(4):
                    act.wait_ge(S["h_ps"], b * 4 + n + 1)
                    ident_copy(h_tm[:, 2 * n:2 * n + 2, :], ps[4 + n][:].rearrange("p (t n) -> p t n", t=2)).then_inc(S["h_sb"], 1)
                act.wait_ge(S["ln_eps"], b + 1)
                nc.scalar.activation(rstd[:, 1, :], rstd[:, 0, :], ACT.Sqrt).then_inc(S["ln_std"], 1)
                for n in range(4):
                    act.wait_ge(S["xt_ps"], b * 4 + n + 1)
                    ident_copy(xnT[:, n % 2, n // 2 * 512:(n // 2 + 1) * 512], ps[n][:]).then_inc(S["xt_sb"], 1)
                act.wait_ge(S["pj_ps"], b * 17 + 1)
                nc.scalar.activation(beta[:], ps[4][:, 0:NT * H], ACT.Sigmoid).then_inc(S["pj_sb"], 1)
                act.wait_ge(S["pads"], 1)
                for n in range(1, 17):
                    act.wait_ge(S["pj_ps"], b * 17 + n + 1)
                    i, c = (n - 1) // 2, (n - 1) % 2
                    if i < 6:
                        ident_copy(raw[:, i, TAPS - 1 + c * 512:TAPS - 1 + (c + 1) * 512], ps[4 + n % 4][:]).then_inc(S["pj_sb"], 1)
                    else:
                        if n == 13:
                            act.wait_ge(S["xw1_stored"], b * 16)
                        ident_copy(xw1[:, i - 6, c * 512:(c + 1) * 512], ps[4 + n % 4][:]).then_inc(S["pj_sb"], 1)
                for i in range(6):
                    act.wait_ge(S["conv_step"], b * 24 + 8 * (i // 2) + 7 + i % 2)
                    nc.scalar.activation(cm[:, i, :], cm[:, i, :], ACT.Silu).then_inc(S["silu_done"], 1)
                act.wait_ge(S["v_stored"], b * 16)
                act.wait_ge(S["vk_done"], b)
                for n in range(8):
                    i, half = n // 2, n % 2
                    act.wait_ge(S["tm_ps"], b * 8 + n + 1)
                    dst = (v_tm, k_tm)[i // 2][:, 4 * half:4 * half + 4, (i % 2) * P:(i % 2 + 1) * P]
                    ident_copy(dst, ps[(5, 6, 7, 4)[n % 4]][:].rearrange("p (t n) -> p t n", t=4)).then_inc(S["tm_sb"], 1)
                act.wait_ge(S["silu_done"], b * 6 + 6)
                for i in range(4):
                    nc.scalar.activation(sq[:, i, :], cm[:, 2 + i, :], ACT.Square).then_inc(S["sq_done"], 1)
                act.wait_ge(S["norm_eps"], b + 1)
                nc.scalar.activation(nrm[:], nrm[:], ACT.Sqrt).then_inc(S["norm_root"], 1)
                for p in range(NT // 2):
                    for t in (2 * p, 2 * p + 1):
                        act.wait_ge(S["x1_ps"], b * NT + t + 1)
                        ident_copy(X[t % 2][:], g4(4 + t % 2)).then_inc(S["x_sb"], 1)
                    for l in range(LEVELS):
                        for t in (2 * p, 2 * p + 1):
                            if l < LEVELS - 1:
                                act.wait_ge(S["x_ps"], b * 40 + p * 10 + 2 * l + t % 2 + 1)
                                ident_copy(X[t % 2][:], g4(2 + t % 2)).then_inc(S["x_sb"], 1)
                            act.wait_ge(S["xt2_ps"], b * 48 + p * 12 + 2 * l + t % 2 + 1)
                            ident_copy(XT[t % 4][:], g4(4 + t % 2)).then_inc(S["xt2_sb"], 1)

        @block.vector
        def _(v):
            nc.vector.memset(raw[:, :, 0:TAPS - 1], 0.0).then_inc(S["pads"], 1)
            with v.Fori(0, NB) as b:
                v.wait_ge(S["gathered"], b * (3 * NT * 16) + 3 * NT * 16)
                col = 0
                for i in range(3):
                    g = G[:, :, col:col + EMB_W[i]]
                    nc.vector.tensor_tensor(g, g, K["mask"][:, i, bass.ds(b * NT, NT)].unsqueeze(2).to_broadcast([P, NT, EMB_W[i]]),
                                            ALU.mult).then_inc(S["rows_masked"], 1)
                    col += EMB_W[i]
                for t in range(NT):
                    v.wait_ge(S["h_sb"], b * 4 + t // 2 + 1)
                    nc.vector.bn_stats(stats[:, t, :], h_tm[:, t, :]).then_inc(S["ln_stats"], 1)
                v.wait_ge(S["ln_stats"], b * NT + NT).then_inc(S["ln_go"], 1)
                for t in range(NT):
                    nc.vector.bn_aggr(mv[:, t, :], stats[:, t, :]).then_inc(S["ln_aggr"], 1)
                v.wait_ge(S["ln_aggr"], b * NT + NT)
                nc.vector.tensor_scalar(rstd[:, 0, :], mv[:, :, 1], 1e-5, None, ALU.add).then_inc(S["ln_eps"], 1)
                v.wait_ge(S["ln_std"], b + 1)
                nc.vector.reciprocal(rstd[:, 2, :], rstd[:, 1, :]).then_inc(S["ln_rstd"], 1)
                v.wait_ge(S["ln_rstd"], b + 1)
                for t in range(NT):
                    nc.vector.tensor_scalar(xn[:, t, :], h_tm[:, t, :], mv[:, t, 0:1], rstd[:, 2, t:t + 1], ALU.subtract, ALU.mult)\
                        .then_inc(S["xn_done"], 1)
                for n, (p, j, i) in enumerate(conv_order):
                    i += 2 * p
                    if j == 0:
                        v.wait_ge(S["pj_sb"], b * 17 + 3 + 2 * i)
                        nc.vector.tensor_scalar(cm[:, i, :], raw[:, i, 0:T], K["convw"][:, i, 0:1], None, ALU.mult).then_inc(S["conv_step"], 1)
                    else:
                        v.wait_ge(S["conv_step"], b * 24 + n - 1)
                        nc.vector.scalar_tensor_tensor(cm[:, i, :], raw[:, i, j:j + T], K["convw"][:, i, j:j + 1], cm[:, i, :],
                                                       ALU.mult, ALU.add).then_inc(S["conv_step"], 1)
                v.wait_ge(S["ss_ps"], b + 1)
                nc.vector.tensor_scalar(nrm[:].rearrange("p a n -> p (a n)"), ps[0][:, 0:2 * NT * H], 1e-6, None, ALU.add).then_inc(S["norm_eps"], 1)
                v.wait_ge(S["norm_root"], b + 1)
                nc.vector.reciprocal(inv[:], nrm[:]).then_inc(S["norm_inv"], 1)
                v.wait_ge(S["norm_inv"], b + 1)
                nc.vector.tensor_tensor(gam[:, 1, :], inv[:, 0, :], inv[:, 0, :], ALU.mult).then_inc(S["gamma_sq"], 1)
                v.wait_ge(S["gamma_sq"], b + 1)
                nc.vector.tensor_tensor(gam[:, 0, :], gam[:, 1, :], beta[:], ALU.mult).then_inc(S["gamma_done"], 1)
                v.wait_ge(S["gamma_done"], b + 1)
                nc.vector.memset(St[:, 0, :, :], 0.0).then_inc(S["s_sb"], 1)

                def inverse(p, s):
                    if s == 0:
                        v.wait_ge(S["gk_ps"], b * (NT // 2) + p + 1)
                        for t in (2 * p, 2 * p + 1):
                            if t >= 2:
                                v.wait_ge(S["a1_sb"], b * NT + t - 1)
                            for h in range(H):
                                nc.vector.scalar_tensor_tensor(AT[t % 2][:, h, :], g4(h % 2)[:, 2 * (t % 2) + h // 2, :],
                                                               gam[:, 0, t * H + h:t * H + h + 1], K["up_strict"][:], ALU.mult, ALU.mult)\
                                    .then_inc(S["at_sb"], 1)
                        v.wait_ge(S["qk_ps"], b * (NT // 2) + p + 1)
                        for r in range(2):
                            q = 2 * p % 4
                            nc.vector.tensor_tensor(QKT[:, q:q + 2, r::2, :].rearrange("p t i n -> p (t i) n"), g4(2 + r),
                                                    over_heads(K["up_incl"][:]), ALU.mult).then_inc(S["qkt_sb"], 1)
                        return
                    for j in range(2):
                        v.wait_ge(S["p_ps"], b * 48 + p * 12 + 2 * (s - 1) + j + 1)
                        nc.vector.tensor_tensor(Q[j][:], g4(j), over_heads(K["wmask"][:, s - 1, :]), ALU.mult).then_inc(S["q_sb"], 1)

                def scan(p, s):
                    t = 2 * p + s // 3
                    if s % 3 == 0:
                        v.wait_ge(S["ks_ps"], b * NT + t + 1)
                        v.wait_ge(S["vk_done"], b + 1)
                        for r in range(2):
                            nc.vector.tensor_tensor(by_head(R[:])[:, r::2, :], by_head(vk[:, t, :])[:, r::2, :], h4(6 + r)[:, 0:2, :],
                                                    ALU.subtract).then_inc(S["r_sb"], 1)
                    elif s % 3 == 1:
                        v.wait_ge(S["y_ps"], b * NT + t + 1)
                        nc.vector.tensor_tensor(z[:].rearrange("p (h n) -> p h n", h=H), h4(6), per_head(gam[:, 0, :], t, DH), ALU.mult)\
                            .then_inc(S["z_sb"], 1)
                    else:
                        v.wait_ge(S["ds_ps"], b * NT + t + 1)
                        nc.vector.tensor_tensor(St[:, (t + 1) % 2, :, :], St[:, t % 2, :, :], ps[7][:, 0:P].rearrange("p (i n) -> p i n", i=2),
                                                ALU.add).then_inc(S["s_sb"], 1)
                        v.wait_ge(S["o_ps"], b * NT + t + 1)
                        if t == 0:
                            v.wait_ge(S["delta_stored"], b * 16)
                        for r in range(2):
                            nc.vector.tensor_tensor(by_head(dl[:, t, :])[:, r::2, :], h4(6 + r)[:, 0:2, :],
                                                    per_head(inv[:, 1, :], t, DH)[:, r::2, :], ALU.mult).then_inc(S["o_sb"], 1)

                for p in range(NT // 2 + 1):
                    for s in range(LEVELS + 1):
                        if p < NT // 2:
                            inverse(p, s)
                        if p and s < 6:
                            scan(p - 1, s)


def constants(nc, ctx, NB):
    shapes = {"ident": [P, P], "up_strict": [P, P], "up_incl": [P, P], "anti": [P, P], "w1t": [P, P], "wmask": [P, LEVELS, P], "sel2": [P, 2],
              "hmask": [P, KD, AH], "vecs": [P, 12], "cbo": [P, D], "dWv": [P, KD, D], "cWqT": [P, KD, D], "Md": [P, KD, D],
              "drow": [P, KD], "OT": [P, KD, NB * NS], "kT": [P, KD, NB * NS], "vT": [P, KD, NB * NS], "ones": [P, P], "WcT": [P, KE, D], "Wq": [P, KD, D], "Wk": [P, KD, D], "Wv": [P, KD, D],
              "Wo": [P, KD, D], "W1x": [P, KD, D], "W1s": [P, D], "W2": [P, KD, 4], "Wb": [P, KD, H], "convw": [P, 6, TAPS],
              "b1": [P, KD, 1], "rmsw": [P, 1], "lbias": [P, 4 * H], "itemp": [P, H], "itemp16": [P, 4 * H], "qsel": [P, NS], "halfsig": [P, H], "mask": [P, 3, NB * NT]}
    K = {n: ctx.enter_context(nc.sbuf_tensor("k_" + n, s, F32)) for n, s in shapes.items()}
    K["rows"] = ctx.enter_context(nc.sbuf_tensor("k_rows", [P, 3, NB * NT], U32))
    return K


def scratch(nc, NB, kind="Internal"):
    t = lambda n, shape: nc.dram_tensor("scr_" + n, shape, F32, kind=kind).ap()
    return {"fpad": [t(f"fpad{f}", (D, FPAD)) for f in range(2)],
            "h": t("h", (P, NB * NT, D)), "v": t("v", (P, NB * NT, D)), "delta": t("delta", (P, NB * NT, D)),
            "xw1": t("xw1", (P, NB * KD, T)), "fir": [t(f"fir{f}", (P, NB * NT, D)) for f in range(2)],
            "h2": t("h2", (P, NB * NT, D)), "xn2T": t("xn2T", (P, NB * KD, T))}

    nc.clear_and_free_semaphores(list(S.values()))
    nc.all_engine_barrier()


def filter_phase(nc, ctx, A, K, dram, ps):
    NB = A["x"].shape[0]
    CG = 8
    NG = DH // CG
    NL = 4
    NTT = NB * NT
    VT = NTT * DH // 512
    sem = lambda n: ctx.enter_context(nc.semaphore(n))
    v_loaded, zeroed, vr_ps, vr_sb = sem("vh_loaded"), sem("vh_zeroed"), sem("vrev_ps"), sem("vrev_sb")
    t_loaded = [[sem(f"toeplitz{f}{q}_loaded") for q in range(NL)] for f in range(2)]
    f_ps = [sem(f"fir{f}_ps") for f in range(2)]
    f_sb = [sem(f"fir{f}_sb") for f in range(2)]
    f_stored = [sem(f"fir{f}_stored") for f in range(2)]
    with ExitStack() as tmp, nc.Block() as block:
        sb = lambda n, shape, dt=F32: tmp.enter_context(nc.sbuf_tensor(n, shape, dt))
        V = sb("Vh", [P, NTT, DH])
        VR = [sb(f"Vrev{q}", [P, DH, NB, 1 + NT]) for q in range(2)]
        TB = [sb(f"TB{f}", [P, NL, CG, FW[f]]) for f in range(2)]
        F = [sb(f"F{f}", [P, NTT, DH]) for f in range(2)]

        @block.sync
        def _(sp):
            for hd in range(H):
                for g in range(NG):
                    n = hd * NG + g
                    for f in range(2):
                        if n >= NL:
                            sp.wait_ge(f_ps[f], n - NL + 1)
                        src = bass.AP(dram["fpad"][f].tensor, (hd * DH + g * CG) * FPAD, [[1, P], [FPAD, CG], [1, FW[f]]])
                        sp.dma_start(TB[f][:, n % NL, :, :], src).then_inc(t_loaded[f][n % NL], 16)

        @block.gpsimd
        def _(pool):
            def load_v(hd):
                if hd:
                    pool.wait_ge(vr_ps, hd * VT)
                pool.dma_start(V[:], dram["v"][:, :, hd * DH:(hd + 1) * DH]).then_inc(v_loaded, 16)

            load_v(0)
            for q in range(2):
                nc.gpsimd.memset(VR[q][:, :, :, 0], 0.0).then_inc(zeroed, 1)
            load_v(1)
            for hd in range(H):
                for f in range(2):
                    pool.wait_ge(f_sb[f], (hd + 1) * NG)
                    pool.dma_start(dram["fir"][f][:, :, hd * DH:(hd + 1) * DH], F[f][:]).then_inc(f_stored[f], 16)
                if hd + 2 < H:
                    load_v(hd + 2)
            for f in range(2):
                pool.wait_ge(f_stored[f], 16 * H)

        @block.tensor
        def _(pe):
            def turn(hd):
                pe.wait_ge(v_loaded, 16 * (hd + 1))
                v2 = V[:].rearrange("p n c -> p (n c)")
                for i in range(VT):
                    n = hd * VT + i
                    if n >= 2:
                        pe.wait_ge(vr_sb, n - 1)
                    nc.tensor.matmul(ps[6 + n % 2][:], K["anti"][:], v2[:, i * 512:(i + 1) * 512], start=True, stop=True).then_inc(vr_ps, 1)

            pe.wait_ge(zeroed, 2)
            turn(0)
            for hd in range(H):
                pe.wait_ge(vr_sb, (hd + 1) * VT)
                for g in range(NG):
                    n = hd * NG + g
                    for f in range(2):
                        bank = 3 * f + n % 3
                        pe.wait_ge(t_loaded[f][n % NL], 16 * (n // NL + 1))
                        if n >= 3:
                            pe.wait_ge(f_sb[f], n - 2)
                        for c in range(CG):
                            cols = slice(c * NTT, (c + 1) * NTT)
                            v3 = VR[hd % 2][:, g * CG + c, :, :]
                            nc.tensor.matmul(ps[bank][:, cols], TB[f][:, n % NL, c, 0:P], v3[:, :, 1:], start=True, stop=False,
                                             skip_group_check=True)
                            last = nc.tensor.matmul(ps[bank][0:FW[f] - P, cols], TB[f][:, n % NL, c, P:FW[f]], v3[:, :, 0:NT],
                                                    start=False, stop=True, skip_group_check=True)
                        last.then_inc(f_ps[f], 1)
                    if g == NG // 2 and hd + 1 < H:
                        turn(hd + 1)

        def turned(hd, i):
            n = hd * VT + i
            return VR[hd % 2][:, :, i, 1:], ps[6 + n % 2][:].rearrange("p (t c) -> p c t", c=DH)

        def evacuate(eng, f, copy):
            def turns(hd):
                for i in range(VT):
                    if i % 2 == f:
                        eng.wait_ge(vr_ps, hd * VT + i + 1)
                        o, s = turned(hd, i)
                        if hd * VT + i:
                            eng.wait_ge(vr_sb, hd * VT + i)
                        copy(o, s).then_inc(vr_sb, 1)

            turns(0)
            for hd in range(H):
                if hd:
                    eng.wait_ge(f_stored[f], 16 * hd)
                for g in range(NG):
                    n = hd * NG + g
                    eng.wait_ge(f_ps[f], n + 1)
                    copy(F[f][:, :, g * CG:(g + 1) * CG].rearrange("p n c -> p c n"),
                         ps[3 * f + n % 3][:, 0:CG * NTT].rearrange("p (c n) -> p c n", c=CG)).then_inc(f_sb[f], 1)
                    if g == NG // 2 and hd + 1 < H:
                        turns(hd + 1)

        @block.scalar
        def _(act):
            evacuate(act, 0, lambda o, i: nc.scalar.activation(o, i, ACT.Copy))

        @block.vector
        def _(v):
            evacuate(v, 1, lambda o, i: nc.vector.tensor_copy(o, i))


def slot_setup(nc, ctx, A, K, dram, ps):
    sem = lambda n: ctx.enter_context(nc.semaphore(n))
    ld, pe_c, vst, act_c = sem("slot_loaded"), sem("slot_pe_group"), sem("slot_vector_step"), sem("slot_scalar_step")
    VECS = ("d_bq", "d_bk", "d_bv", "c_bq", "c_bk", "c_bv")
    with ExitStack() as tmp, nc.Block() as block:
        sb = lambda n, shape, dt=F32: tmp.enter_context(nc.sbuf_tensor(n, shape, dt))
        vrow = sb("vrow", [2 * len(VECS), P])
        slot = sb("slot", [NS, D])
        slotT = sb("slotT", [P, KD, NS])
        wqs = sb("wqs", [P, KD, D])
        wks = sb("wks", [P, KD, D])
        wkT = sb("wkT", [P, KD, D])
        qT = sb("qT", [P, KD, NS])
        qblk = sb("qblk", [P, KD, AH, NS])
        cwq = sb("cwq", [P, KD, D])

        @block.sync
        def _(sp):
            for i, n in enumerate(VECS):
                sp.dma_start(vrow[2 * i:2 * i + 2, :], A["L0_ffn_" + n].rearrange("(k p) -> k p", p=P)).then_inc(ld, 16)
            sp.dma_start(slot[:], A["L0_ffn_slot_query"][0]).then_inc(ld, 16)
            for t, n in ((wqs, "d_Wq"), (wks, "d_Wk"), (cwq, "c_Wq"), (K["dWv"], "d_Wv")):
                sp.dma_start(t[:], A["L0_ffn_" + n].rearrange("(k p) n -> p k n", p=P)).then_inc(ld, 16)
            sp.dma_start(K["cbo"][:], bass.AP(A["L0_ffn_c_bo"].tensor, 0, [[0, P], [1, D]])).then_inc(ld, 16)
            sp.wait_ge(ld, 16 * (len(VECS) + 6))

        @block.tensor
        def _(pe):
            ident = K["ident"]
            pe.wait_ge(ld, 16 * (len(VECS) + 6))
            nc.tensor.transpose(ps[0][:, 0:12], vrow[:], ident[0:12, 0:12]).then_inc(pe_c, 1)
            for k in range(KD):
                last = nc.tensor.transpose(ps[1][:, k * NS:(k + 1) * NS], slot[:, k * P:(k + 1) * P], ident[0:NS, 0:NS])
            last.then_inc(pe_c, 1)
            for w, src in ((2, wks), (3, cwq)):
                for c in range(KD):
                    for k in range(KD):
                        last = nc.tensor.transpose(ps[w][:, c * D + k * P:c * D + (k + 1) * P], src[:, k, c * P:(c + 1) * P], ident[:])
            last.then_inc(pe_c, 1)
            pe.wait_ge(vst, 4)
            for c in range(KD):
                for k in range(KD):
                    last = nc.tensor.matmul(ps[4][:, c * NS:(c + 1) * NS], wqs[:, k, c * P:(c + 1) * P], slotT[:, k, :], start=(k == 0), stop=(k == KD - 1))
            last.then_inc(pe_c, 1)
            pe.wait_ge(vst, 8)
            for c in range(KD):
                for k in range(KD):
                    last = nc.tensor.matmul(ps[5][:, c * D:(c + 1) * D], wkT[:, k, c * P:(c + 1) * P], qblk[:, k, :, :].rearrange("p h q -> p (h q)"),
                                            start=(k == 0), stop=(k == KD - 1))
            for m in range(KD):
                for k in range(KD):
                    last = nc.tensor.matmul(ps[6][:, m:m + 1], qblk[:, k, :, :].rearrange("p h q -> p (h q)")[:, m * P:(m + 1) * P],
                                            K["vecs"][:, 2 + k:3 + k], start=(k == 0), stop=(k == KD - 1))
            last.then_inc(pe_c, 1)

        @block.vector
        def _(v):
            n = [0]

            def step(ins, fence=True):
                ins.then_inc(vst, 1)
                n[0] += 1
                if fence:
                    v.wait_ge(vst, n[0])

            v.wait_ge(pe_c, 3)
            step(nc.vector.tensor_copy(K["vecs"][:], ps[0][:, 0:12]))
            step(nc.vector.tensor_copy(slotT[:], ps[1][:, 0:KD * NS].rearrange("p (k n) -> p k n", k=KD)))
            step(nc.vector.tensor_copy(wkT[:], ps[2][:].rearrange("p (k n) -> p k n", k=KD)))
            step(nc.vector.tensor_copy(K["cWqT"][:], ps[3][:].rearrange("p (k n) -> p k n", k=KD)))
            v.wait_ge(pe_c, 4)
            for c in range(KD):
                step(nc.vector.tensor_scalar(qT[:, c, :], ps[4][:, c * NS:(c + 1) * NS], K["vecs"][:, c:c + 1], None, ALU.add))
            for c in range(KD):
                step(nc.vector.tensor_tensor(qblk[:, c, :, :], qT[:, c, :].unsqueeze(1).to_broadcast([P, AH, NS]),
                                             K["hmask"][:, c, :].unsqueeze(2).to_broadcast([P, AH, NS]), ALU.mult))
            v.wait_ge(pe_c, 5)
            step(nc.vector.tensor_copy(K["Md"][:], ps[5][:].rearrange("p (k n) -> p k n", k=KD)))
            step(nc.vector.tensor_scalar(K["drow"][:], ps[6][:, 0:KD], 0.25, None, ALU.mult))


def gate_phase(nc, ctx, A, K, dram, ps):
    NB = A["x"].shape[0]
    names = ["ln_go", "src_loaded", "xw1_loaded", "h_loaded", "square", "red", "st_step", "st_root", "pad", "st_ps", "st_sb", "pre_ps", "pre_sb",
             "gelu", "lg_ps", "sm", "sm_exp", "pool_mix", "mix", "osq", "rms", "rms_root", "on", "ot_ps", "ot_sb", "h2_ps", "h2_sb",
             "ln_stats", "ln_aggr", "ln_eps", "ln_std", "ln_rstd", "xn_done", "h2b", "h2_stored", "xt_ps", "xt_sb", "xt_stored",
             "sc_ps", "sc_max", "sc_exp", "sum_inv", "sq_sum", "floor", "et_ps", "et_sb", "ctx_ps", "ctx_sb", "ctxT_ps", "ctxT_sb", "z_ps", "z_sb", "o_ps", "o_sb"]
    S = {n: nc.alloc_semaphore(name="g_" + n) for n in names}
    N2 = NT * H
    with ExitStack() as tmp, nc.Block() as block:
        sb = lambda n, shape, dt=F32: tmp.enter_context(nc.sbuf_tensor("g_" + n, shape, dt))
        src = sb("src", [P, 4, NT, D])
        sqr = sb("sqr", [P, NT, D])
        xw1 = sb("xw1", [P, KD, T])
        h_tm = sb("h", [P, NT, D])
        red = sb("red", [P, 4, 3, N2])
        tiny = sb("tiny", [P, 4, 3, N2])
        st = sb("st", [P, N2, 32])
        stT = sb("stT", [P, T])
        h1 = sb("h1", [P, KD, H, T])
        lg = sb("lg", [P, N2, 4])
        pr = sb("pr", [P, N2, 4])
        sm = sb("sm", [P, 6, N2])
        oT = sb("oT", [P, KD, T])
        stats = sb("stats", [P, NT, 6])
        mv = sb("mv", [P, NT, 2])
        rstd = sb("rstd", [P, 3, NT])
        xn = sb("xn", [P, NT, D])
        xnT = sb("xnT", [P, KD, T])
        ex = sb("ex", [P, KD, T])
        eT = sb("eT", [P, NT, D])
        at = sb("at", [P, 8, KD])
        cx = sb("cx", [P, KD, D])
        cxT = sb("cxT", [P, KD, D])
        zm = sb("zm", [P, KD, D])

        flat = lambda a: a.rearrange("p t (h n) -> p (t h) n", h=H)
        bank2 = lambda b0: K["psum"][:, b0:b0 + 2, :].rearrange("p k n -> p (k n)")
        mixw = lambda i: pr[:, :, i:i + 1].to_broadcast([P, N2, DH])
        MIX, LONG, DELTA, VAL = 0, 1, 2, 3

        @block.sync
        def _(sp):
            with sp.Fori(0, NB) as b:
                tiles = bass.ds(b * NT, NT)
                sp.wait_ge(S["on"], b)
                for i, n in enumerate((dram["fir"][0], dram["fir"][1], dram["delta"], dram["v"])):
                    sp.dma_start(src[:, i, :, :], n[:, tiles, :]).then_inc(S["src_loaded"], 16)
                sp.wait_ge(S["pre_sb"], b * 4)
                sp.dma_start(xw1[:], dram["xw1"][:, bass.ds(b * KD, KD), :]).then_inc(S["xw1_loaded"], 16)
                sp.wait_ge(S["h2_stored"], b * 16)
                sp.dma_start(h_tm[:], dram["h"][:, tiles, :]).then_inc(S["h_loaded"], 16)
                sp.wait_ge(S["xt_sb"], b * 4 + 4)
                sp.dma_start(dram["xn2T"][:, bass.ds(b * KD, KD), :], xnT[:]).then_inc(S["xt_stored"], 16)
                sp.wait_ge(S["h2b"], b + 1)
                sp.dma_start(dram["h2"][:, tiles, :], h_tm[:]).then_inc(S["h2_stored"], 16)
            sp.wait_ge(S["xt_stored"], 16 * NB)
            sp.wait_ge(S["h2_stored"], 16 * NB)

        @block.gpsimd
        def _(pool):
            with pool.Fori(0, NB) as b:
                pool.wait_ge(S["sm"], b * 11 + 11)
                f = flat(src[:, LONG, :, :])
                nc.gpsimd.tensor_tensor(f, f, mixw(1), ALU.mult).then_inc(S["pool_mix"], 1)
                g = flat(src[:, VAL, :, :])
                nc.gpsimd.tensor_tensor(g, g, mixw(3), ALU.mult).then_inc(S["pool_mix"], 1)
                pool.wait_ge(S["pool_mix"], b * 3 + 2)
                nc.gpsimd.tensor_tensor(f, f, g, ALU.add).then_inc(S["pool_mix"], 1)
                pool.wait_ge(S["xn_done"], b * NT + NT)
                nc.gpsimd.tensor_tensor(h_tm[:], h_tm[:], K["cbo"][:].unsqueeze(1).to_broadcast([P, NT, D]), ALU.add).then_inc(S["h2b"], 1)

        @block.tensor
        def _(pe):
            ident = K["ident"][:]
            with pe.Fori(0, NB) as b:
                pe.wait_ge(S["st_step"], b * 4 + 4)
                pe.wait_ge(S["st_root"], b + 1)
                pe.wait_ge(S["pad"], 1)
                for n in range(2):
                    for q in range(4):
                        t = 4 * n + q
                        last = nc.tensor.transpose(ps[n][:, q * P:(q + 1) * P], st[:, t * H:(t + 1) * H, :].rearrange("p h j -> p (h j)"), ident)
                    last.then_inc(S["st_ps"], 1)
                pe.wait_ge(S["st_sb"], b * 2 + 2)
                for n in range(4):
                    m, c = n // 2, n % 2
                    if n >= 2:
                        pe.wait_ge(S["pre_sb"], b * 4 + n - 1)
                    for h in range(H):
                        last = nc.tensor.matmul(ps[4 * (1 - n % 2) + h][:], K["W1s"][32 * h:32 * h + 16, m * P:(m + 1) * P],
                                                stT[32 * h:32 * h + 16, c * 512:(c + 1) * 512], start=True, stop=True)
                    last.then_inc(S["pre_ps"], 1)
                pe.wait_ge(S["pre_sb"], b * 4 + 3)
                pe.wait_ge(S["gelu"], b * 4 + 4)
                for t in range(NT):
                    for h in range(H):
                        for m in range(KD):
                            last = nc.tensor.matmul(ps[4][:, (t * H + h) * 4:(t * H + h + 1) * 4], h1[:, m, h, t * P:(t + 1) * P], K["W2"][:, m, :],
                                                    start=(m == 0), stop=(m == KD - 1))
                last.then_inc(S["lg_ps"], 1)
                pe.wait_ge(S["pre_sb"], b * 4 + 4)
                pe.wait_ge(S["on"], b + 1)
                for n in range(4):
                    half, k = n // 2, n % 2
                    for q in range(4):
                        last = nc.tensor.transpose(ps[n][:, q * P:(q + 1) * P], src[:, MIX, 4 * half + q, k * P:(k + 1) * P], ident)
                    last.then_inc(S["ot_ps"], 1)
                for n in range(4):
                    pe.wait_ge(S["ot_sb"], b * 4 + (2 if n < 2 else 4))
                    for q in range(2):
                        t = 2 * n + q
                        for k in range(KD):
                            last = nc.tensor.matmul(ps[4 + n][:, q * D:(q + 1) * D], oT[:, k, t * P:(t + 1) * P], K["Wo"][:, k, :],
                                                    start=(k == 0), stop=(k == KD - 1))
                    last.then_inc(S["h2_ps"], 1)
                for n in range(4):
                    half, k = n // 2, n % 2
                    pe.wait_ge(S["xn_done"], b * NT + 4 * half + 4)
                    for q in range(4):
                        last = nc.tensor.transpose(ps[n][:, q * P:(q + 1) * P], xn[:, 4 * half + q, k * P:(k + 1) * P], ident)
                    last.then_inc(S["xt_ps"], 1)
                pe.wait_ge(S["xt_sb"], b * 4 + 4)
                for m in range(KD):
                    for c in range(2):
                        for k in range(KD):
                            last = nc.tensor.matmul(ps[4 + 2 * m + c][:], K["Md"][:, k, m * P:(m + 1) * P], xnT[:, k, c * 512:(c + 1) * 512],
                                                    start=(k == 0), stop=(k == KD - 1))
                    last.then_inc(S["sc_ps"], 1)
                pe.wait_ge(S["sc_exp"], b * KD + KD)
                for n in range(4):
                    for q in range(4):
                        t, m = 2 * n + q // 2, q % 2
                        last = nc.tensor.transpose(ps[n][:, q * P:(q + 1) * P], ex[:, m, t * P:(t + 1) * P], ident)
                    last.then_inc(S["et_ps"], 1)
                pe.wait_ge(S["et_sb"], b * 4 + 4)
                for m in range(KD):
                    for t in range(NT):
                        last = nc.tensor.matmul(ps[4 + m][:, 0:D], eT[:, t, m * P:(m + 1) * P], xn[:, t, :], start=(t == 0), stop=(t == NT - 1))
                    last.then_inc(S["ctx_ps"], 1)
                pe.wait_ge(S["ctx_sb"], b * KD + KD)
                for k in range(KD):
                    for m in range(KD):
                        last = nc.tensor.transpose(ps[0][:, k * D + m * P:k * D + (m + 1) * P], cx[:, m, k * P:(k + 1) * P], ident)
                last.then_inc(S["ctxT_ps"], 1)
                pe.wait_ge(S["ctxT_sb"], b + 1)
                for m in range(KD):
                    for k in range(KD):
                        last = nc.tensor.matmul(ps[1][:, m * D:(m + 1) * D], cxT[:, k, m * P:(m + 1) * P], K["dWv"][:, k, :],
                                                start=(k == 0), stop=(k == KD - 1))
                last.then_inc(S["z_ps"], 1)
                pe.wait_ge(S["z_sb"], b * KD + KD)
                for c in range(KD):
                    for m in range(KD):
                        last = nc.tensor.matmul(ps[6][:, c * NS:(c + 1) * NS], zm[:, m, c * P:(c + 1) * P], K["qsel"][:], start=(m == 0), stop=(m == KD - 1))
                last.then_inc(S["o_ps"], 1)
                pe.wait_ge(S["o_sb"], b * KD + KD)

        @block.scalar
        def _(act):
            copy = lambda o, i: nc.scalar.activation(o, i, ACT.Copy)
            with act.Fori(0, NB) as b:
                act.wait_ge(S["src_loaded"], b * 64 + 64)
                for i in range(4):
                    if i:
                        act.wait_ge(S["red"], b * 12 + 3 * i)
                    else:
                        act.wait_ge(S["red"], b * 12)
                    nc.scalar.activation(sqr[:], src[:, i, :, :], ACT.Square).then_inc(S["square"], 1)
                act.wait_ge(S["red"], b * 12 + 12)
                nc.scalar.activation(st[:, :, 3:16:4].rearrange("p n s -> p s n"), red[:, :, 2, :], ACT.Sqrt).then_inc(S["st_root"], 1)
                for n in range(2):
                    act.wait_ge(S["st_ps"], b * 2 + n + 1)
                    copy(stT[:, n * 512:(n + 1) * 512], ps[n][:]).then_inc(S["st_sb"], 1)
                for n in range(4):
                    m, c = n // 2, n % 2
                    act.wait_ge(S["pre_sb"], b * 4 + n + 1)
                    g = h1[:, m, :, c * 512:(c + 1) * 512]
                    nc.scalar.activation(g, g, ACT.Gelu, bias=K["b1"][:, m, :]).then_inc(S["gelu"], 1)
                act.wait_ge(S["sm"], b * 11 + 4)
                nc.scalar.activation(pr[:], lg[:], ACT.Exp).then_inc(S["sm_exp"], 1)
                act.wait_ge(S["mix"], b * 4 + 4)
                nc.scalar.activation(sqr[:], src[:, MIX, :, :], ACT.Square).then_inc(S["osq"], 1)
                act.wait_ge(S["rms"], b * 2 + 1)
                nc.scalar.activation(sm[:, 4, :], sm[:, 3, :], ACT.Sqrt).then_inc(S["rms_root"], 1)
                for n in range(4):
                    act.wait_ge(S["ot_ps"], b * 4 + n + 1)
                    copy(oT[:, n % 2, n // 2 * 512:(n // 2 + 1) * 512], ps[n][:]).then_inc(S["ot_sb"], 1)
                act.wait_ge(S["ln_eps"], b + 1)
                nc.scalar.activation(rstd[:, 1, :], rstd[:, 0, :], ACT.Sqrt).then_inc(S["ln_std"], 1)
                act.wait_ge(S["xt_stored"], b * 16)
                for n in range(4):
                    act.wait_ge(S["xt_ps"], b * 4 + n + 1)
                    copy(xnT[:, n % 2, n // 2 * 512:(n // 2 + 1) * 512], ps[n][:]).then_inc(S["xt_sb"], 1)
                for m in range(KD):
                    act.wait_ge(S["sc_max"], b * 6 + 3 * m + 3)
                    nc.scalar.activation(ex[:, m, :], bank2(4 + 2 * m), ACT.Exp, bias=at[:, 2, m:m + 1], scale=0.25, accum_out=at[:, 3, m:m + 1])\
                        .then_inc(S["sc_exp"], 1)
                for n in range(4):
                    act.wait_ge(S["et_ps"], b * 4 + n + 1)
                    copy(eT[:, 2 * n:2 * n + 2, :], ps[n][:].rearrange("p (t n) -> p t n", t=2)).then_inc(S["et_sb"], 1)
                act.wait_ge(S["ctxT_ps"], b + 1)
                copy(cxT[:], ps[0][:].rearrange("p (k n) -> p k n", k=KD)).then_inc(S["ctxT_sb"], 1)
                act.wait_ge(S["o_ps"], b + 1)
                for c in range(KD):
                    nc.scalar.activation(K["OT"][:, c, bass.ds(b * NS, NS)], ps[6][:, c * NS:(c + 1) * NS], ACT.Identity,
                                         bias=K["vecs"][:, 4 + c:5 + c]).then_inc(S["o_sb"], 1)

        @block.vector
        def _(v):
            nc.vector.memset(st[:], 0.0).then_inc(S["pad"], 1)
            v.wait_ge(S["pad"], 1)
            with v.Fori(0, NB) as b:
                v.wait_ge(S["src_loaded"], b * 64 + 64)
                for i in range(4):
                    f = flat(src[:, i, :, :])
                    nc.vector.tensor_reduce(red[:, i, 0, :], f, AX.X, ALU.add).then_inc(S["red"], 1)
                    nc.vector.tensor_reduce(red[:, i, 1, :], f, AX.X, ALU.add, apply_absolute_value=True).then_inc(S["red"], 1)
                    v.wait_ge(S["square"], b * 4 + i + 1)
                    nc.vector.tensor_reduce(red[:, i, 2, :], flat(sqr[:]), AX.X, ALU.add).then_inc(S["red"], 1)
                v.wait_ge(S["red"], b * 12 + 12)
                col = lambda j: st[:, :, j:16:4].rearrange("p n s -> p s n")
                nc.vector.tensor_scalar(col(0), red[:, :, 0, :], 1.0 / DH, None, ALU.mult).then_inc(S["st_step"], 1)
                nc.vector.tensor_scalar(col(2), red[:, :, 1, :], 1.0 / DH, None, ALU.mult).then_inc(S["st_step"], 1)
                v.wait_ge(S["st_step"], b * 4 + 1)
                nc.vector.tensor_tensor(tiny[:, :, 0, :], col(0), col(0), ALU.mult).then_inc(S["st_step"], 1)
                v.wait_ge(S["st_step"], b * 4 + 3)
                nc.vector.scalar_tensor_tensor(col(1), red[:, :, 2, :], 1.0 / DH, tiny[:, :, 0, :], ALU.mult, ALU.subtract)\
                    .then_inc(S["st_step"], 1)
                v.wait_ge(S["xw1_loaded"], b * 16 + 16)
                for n in range(4):
                    m, c = n // 2, n % 2
                    v.wait_ge(S["pre_ps"], b * 4 + n + 1)
                    bk = 4 * (1 - n % 2)
                    nc.vector.tensor_tensor(h1[:, m, :, c * 512:(c + 1) * 512], K["psum"][:, bk:bk + 4, :],
                                            xw1[:, m, c * 512:(c + 1) * 512].unsqueeze(1).to_broadcast([P, H, 512]), ALU.add).then_inc(S["pre_sb"], 1)
                k = [0]

                def step(ins):
                    ins.then_inc(S["sm"], 1)
                    k[0] += 1
                    v.wait_ge(S["sm"], b * 11 + k[0])

                last4 = lambda a: a.unsqueeze(2).to_broadcast([P, N2, 4])
                by_t = lambda a: a.rearrange("p (t h) j -> p t (h j)", h=H)
                v.wait_ge(S["lg_ps"], b + 1)
                step(nc.vector.tensor_tensor(by_t(lg[:]), ps[4][:, 0:4 * N2].rearrange("p (t n) -> p t n", t=NT),
                                             K["lbias"][:].unsqueeze(1).to_broadcast([P, NT, 16]), ALU.add))
                step(nc.vector.tensor_tensor(by_t(lg[:]), by_t(lg[:]), K["itemp16"][:].unsqueeze(1).to_broadcast([P, NT, 16]), ALU.mult))
                step(nc.vector.tensor_reduce(sm[:, 0, :], lg[:], AX.X, ALU.max))
                step(nc.vector.tensor_tensor(lg[:], lg[:], last4(sm[:, 0, :]), ALU.subtract))
                v.wait_ge(S["sm_exp"], b + 1)
                step(nc.vector.tensor_reduce(sm[:, 1, :], pr[:], AX.X, ALU.add))
                step(nc.vector.reciprocal(sm[:, 2, :], sm[:, 1, :]))
                step(nc.vector.tensor_tensor(lg[:], pr[:], last4(sm[:, 2, :]), ALU.mult))
                nc.vector.tensor_scalar(pr[:, :, 0:2], lg[:, :, 0:2], 0.05, None, ALU.max).then_inc(S["floor"], 1)
                nc.vector.tensor_scalar(pr[:, :, 2:4], lg[:, :, 2:4], 0.0, None, ALU.max).then_inc(S["floor"], 1)
                v.wait_ge(S["floor"], b * 2 + 2)
                step(nc.vector.tensor_reduce(sm[:, 1, :], pr[:], AX.X, ALU.add))
                step(nc.vector.reciprocal(sm[:, 2, :], sm[:, 1, :]))
                step(nc.vector.tensor_tensor(pr[:], pr[:], last4(sm[:, 2, :]), ALU.mult))
                p0 = pr[:, :, 0].rearrange("p (t h) -> p t h", h=H)
                step(nc.vector.tensor_tensor(p0, p0, K["halfsig"][:].unsqueeze(1).to_broadcast([P, NT, H]), ALU.add))
                assert k[0] == 11
                f, g = flat(src[:, MIX, :, :]), flat(src[:, DELTA, :, :])
                nc.vector.tensor_tensor(f, f, mixw(0), ALU.mult).then_inc(S["mix"], 1)
                nc.vector.tensor_tensor(g, g, mixw(2), ALU.mult).then_inc(S["mix"], 1)
                v.wait_ge(S["mix"], b * 4 + 2)
                nc.vector.tensor_tensor(f, f, g, ALU.add).then_inc(S["mix"], 1)
                v.wait_ge(S["mix"], b * 4 + 3)
                v.wait_ge(S["pool_mix"], b * 3 + 3)
                nc.vector.tensor_tensor(f, f, flat(src[:, LONG, :, :]), ALU.add).then_inc(S["mix"], 1)
                v.wait_ge(S["osq"], b + 1)
                nc.vector.tensor_reduce(sm[:, 5, :], flat(sqr[:]), AX.X, ALU.add).then_inc(S["sq_sum"], 1)
                v.wait_ge(S["sq_sum"], b + 1)
                nc.vector.tensor_scalar(sm[:, 3, :], sm[:, 5, :], 1.0 / DH, 1e-5, ALU.mult, ALU.add).then_inc(S["rms"], 1)
                v.wait_ge(S["rms_root"], b + 1)
                nc.vector.reciprocal(sm[:, 5, :], sm[:, 4, :]).then_inc(S["rms"], 1)
                v.wait_ge(S["rms"], b * 2 + 2)
                nc.vector.tensor_tensor(f, f, sm[:, 5, :].unsqueeze(2).to_broadcast([P, N2, DH]), ALU.mult).then_inc(S["on"], 1)
                v.wait_ge(S["h_loaded"], b * 16 + 16)
                for n in range(4):
                    v.wait_ge(S["h2_ps"], b * 4 + n + 1)
                    t2 = h_tm[:, 2 * n:2 * n + 2, :]
                    nc.vector.tensor_tensor(t2, ps[4 + n][:].rearrange("p (t n) -> p t n", t=2), t2, ALU.add).then_inc(S["h2_sb"], 1)
                for t in range(NT):
                    v.wait_ge(S["h2_sb"], b * 4 + t // 2 + 1)
                    nc.vector.bn_stats(stats[:, t, :], h_tm[:, t, :]).then_inc(S["ln_stats"], 1)
                v.wait_ge(S["ln_stats"], b * NT + NT).then_inc(S["ln_go"], 1)
                for t in range(NT):
                    nc.vector.bn_aggr(mv[:, t, :], stats[:, t, :]).then_inc(S["ln_aggr"], 1)
                v.wait_ge(S["ln_aggr"], b * NT + NT)
                nc.vector.tensor_scalar(rstd[:, 0, :], mv[:, :, 1], 1e-5, None, ALU.add).then_inc(S["ln_eps"], 1)
                v.wait_ge(S["ln_std"], b + 1)
                nc.vector.reciprocal(rstd[:, 2, :], rstd[:, 1, :]).then_inc(S["ln_rstd"], 1)
                v.wait_ge(S["ln_rstd"], b + 1)
                for t in range(NT):
                    nc.vector.tensor_scalar(xn[:, t, :], h_tm[:, t, :], mv[:, t, 0:1], rstd[:, 2, t:t + 1], ALU.subtract, ALU.mult)\
                        .then_inc(S["xn_done"], 1)
                for m in range(KD):
                    v.wait_ge(S["sc_ps"], b * KD + m + 1)
                    nc.vector.tensor_reduce(at[:, 0, m:m + 1], bank2(4 + 2 * m), AX.X, ALU.max).then_inc(S["sc_max"], 1)
                    v.wait_ge(S["sc_max"], b * 6 + 3 * m + 1)
                    nc.vector.scalar_tensor_tensor(at[:, 1, m:m + 1], at[:, 0, m:m + 1], 0.25, K["drow"][:, m:m + 1], ALU.mult, ALU.add)\
                        .then_inc(S["sc_max"], 1)
                    v.wait_ge(S["sc_max"], b * 6 + 3 * m + 2)
                    nc.vector.tensor_tensor(at[:, 2, m:m + 1], K["drow"][:, m:m + 1], at[:, 1, m:m + 1], ALU.subtract).then_inc(S["sc_max"], 1)
                v.wait_ge(S["sc_exp"], b * KD + KD)
                nc.vector.reciprocal(at[:, 4, :], at[:, 3, :]).then_inc(S["sum_inv"], 1)
                v.wait_ge(S["sum_inv"], b + 1)
                for m in range(KD):
                    v.wait_ge(S["ctx_ps"], b * KD + m + 1)
                    nc.vector.tensor_scalar(cx[:, m, :], ps[4 + m][:, 0:D], at[:, 4, m:m + 1], None, ALU.mult).then_inc(S["ctx_sb"], 1)
                v.wait_ge(S["z_ps"], b + 1)
                for m in range(KD):
                    nc.vector.tensor_tensor(zm[:, m, :].rearrange("p (g n) -> p g n", g=AH), ps[1][:, m * D:(m + 1) * D].rearrange("p (g n) -> p g n", g=AH),
                                            K["hmask"][:, m, :].unsqueeze(2).to_broadcast([P, AH, AD]), ALU.mult).then_inc(S["z_sb"], 1)

    nc.clear_and_free_semaphores(list(S.values()))
    nc.all_engine_barrier()


def expert_phase(nc, ctx, A, K, dram, ps):
    sem = lambda n: ctx.enter_context(nc.semaphore("e_" + n))
    NB = A["x"].shape[0]
    NR = NB * NS
    NF = FF // P
    NW = 3
    NE = NS
    ld, vst, pe_c, root, bias_sb = sem("loaded"), sem("vector_step"), sem("pe_group"), sem("root"), sem("bias_step")
    w_loaded = [sem(f"w{q}_loaded") for q in range(NW)]
    u_ps, u_pre, u_act, ug_sb, y_ps, o2_sb, kv_ps, kv_sb = (sem(n) for n in ("u_ps", "u_pre", "u_act", "ug_sb", "y_ps", "o2_sb", "kv_ps", "kv_sb"))
    with ExitStack() as tmp, nc.Block() as block:
        sb = lambda n, shape, dt=F32: tmp.enter_context(nc.sbuf_tensor("e_" + n, shape, dt))
        dWo = sb("dWo", [P, KD, D])
        cWk = sb("cWk", [P, KD, D])
        cWv = sb("cWv", [P, KD, D])
        slotb = sb("slotb", [P, D])
        bo = sb("bo", [P, D])
        lng = sb("lng", [P, D])
        lnb = sb("lnb", [P, D])
        brow = [sb(f"brow{q}", [NE * NF, P]) for q in range(2)]
        b2row = sb("b2row", [NE * KD, P])
        b1c = sb("b1c", [P, 2, NE, NF])
        b2c = sb("b2c", [P, NE, KD])
        W1 = [sb(f"W1_{q}", [P, KD, FF]) for q in range(NW)]
        Wg = [sb(f"Wg_{q}", [P, KD, FF]) for q in range(NW)]
        W2 = [sb(f"W2_{q}", [P, NF, D]) for q in range(NW)]
        o1 = sb("o1", [P, D])
        stats = sb("stats", [P, 6])
        mv = sb("mv", [P, 2])
        rs = sb("rs", [P, 4])
        hl = sb("hl", [P, D])
        hT = sb("hT", [P, KD, NR])
        o1T = sb("o1T", [P, KD, NR])
        o2T = sb("o2T", [P, KD, NR])
        ub = [sb(f"ub{q}", [P, 2, NF, NB]) for q in range(2)]
        ug = [sb(f"ug{q}", [P, NF, NB]) for q in range(2)]
        NLOAD = 3 + 3 * NB + 1 + 2 + 1

        @block.sync
        def _(sp):
            def load(e):
                q = e % NW
                if e >= NW:
                    sp.wait_ge(y_ps, e - NW + 1)
                sp.dma_start(W1[q][:], A["L0_ffn_e_W1"][e].rearrange("(k p) f -> p k f", p=P)).then_inc(w_loaded[q], 16)
                sp.dma_start(Wg[q][:], A["L0_ffn_e_Wg"][e].rearrange("(k p) f -> p k f", p=P)).then_inc(w_loaded[q], 16)
                sp.dma_start(W2[q][:], A["L0_ffn_e_W2"][e].rearrange("(k p) n -> p k n", p=P)).then_inc(w_loaded[q], 16)

            for e in range(NE):
                load(e)

        @block.scalar
        def _(act):
            for t, n in ((dWo, "d_Wo"), (cWk, "c_Wk"), (cWv, "c_Wv")):
                act.dma_start(t[:], A["L0_ffn_" + n].rearrange("(k p) n -> p k n", p=P)).then_inc(ld, 16)
            for b in range(NB):
                act.dma_start(slotb[b * NS:(b + 1) * NS, :], A["L0_ffn_slot_query"][0]).then_inc(ld, 16)
                act.dma_start(lng[b * NS:(b + 1) * NS, :], A["L0_ffn_e_ln_g"]).then_inc(ld, 16)
                act.dma_start(lnb[b * NS:(b + 1) * NS, :], A["L0_ffn_e_ln_b"]).then_inc(ld, 16)
            act.dma_start(bo[:], bass.AP(A["L0_ffn_d_bo"].tensor, 0, [[0, P], [1, D]])).then_inc(ld, 16)
            for q, n in enumerate(("e_b1", "e_bg")):
                act.dma_start(brow[q][:], A["L0_ffn_" + n].rearrange("e (f p) -> (e f) p", p=P)).then_inc(ld, 16)
            act.dma_start(b2row[:], A["L0_ffn_e_b2"].rearrange("e (k p) -> (e k) p", p=P)).then_inc(ld, 16)
            act.wait_ge(vst, 4)
            nc.scalar.activation(rs[0:NR, 1:2], rs[0:NR, 0:1], ACT.Sqrt).then_inc(root, 1)
            for e in range(NE):
                act.wait_ge(u_pre, e + 1)
                nc.scalar.activation(ub[e % 2][:], ub[e % 2][:], ACT.Silu).then_inc(u_act, 1)

        @block.tensor
        def _(pe):
            ident = K["ident"]
            pe.wait_ge(ld, 16 * NLOAD)
            for q in range(2):
                nc.tensor.transpose(ps[q][:, 0:P], brow[q][:], ident[:])
            nc.tensor.transpose(ps[2][:, 0:NE * KD], b2row[:], ident[0:NE * KD, 0:NE * KD]).then_inc(pe_c, 1)
            for k in range(KD):
                last = nc.tensor.matmul(ps[3][0:NR, 0:D], K["OT"][:, k, :], dWo[:, k, :], start=(k == 0), stop=(k == KD - 1))
            last.then_inc(pe_c, 1)
            pe.wait_ge(vst, 8)
            for k in range(KD):
                nc.tensor.transpose(ps[4][:, k * P:k * P + NR], hl[0:NR, k * P:(k + 1) * P], ident[0:NR, 0:NR])
                last = nc.tensor.transpose(ps[5][:, k * P:k * P + NR], o1[0:NR, k * P:(k + 1) * P], ident[0:NR, 0:NR])
            last.then_inc(pe_c, 1)

            def up(e):
                q, bank = e % NW, 6 + e % 2
                pe.wait_ge(w_loaded[q], 48 * (e // NW + 1))
                if e >= 2:
                    pe.wait_ge(u_pre, e - 1)
                for g, w in ((0, W1[q]), (1, Wg[q])):
                    for f in range(NF):
                        at = (g * NF + f) * NB
                        for k in range(KD):
                            last = nc.tensor.matmul(ps[bank][:, at:at + NB], w[:, k, f * P:(f + 1) * P], hT[:, k, e:NR:NE],
                                                    start=(k == 0), stop=(k == KD - 1))
                last.then_inc(u_ps, 1)

            def down(e):
                q, bank = e % NW, e % 2
                pe.wait_ge(ug_sb, e + 1)
                if e >= 2:
                    pe.wait_ge(o2_sb, e - 1)
                for c in range(KD):
                    for f in range(NF):
                        last = nc.tensor.matmul(ps[bank][:, c * NB:(c + 1) * NB], W2[q][:, f, c * P:(c + 1) * P], ug[e % 2][:, f, :],
                                                start=(f == 0), stop=(f == NF - 1))
                last.then_inc(y_ps, 1)

            pe.wait_ge(vst, 9)
            pe.wait_ge(bias_sb, 3)
            for e in range(NE + 1):
                if e < NE:
                    up(e)
                if e:
                    down(e - 1)
            pe.wait_ge(o2_sb, NE)
            for w, wt in enumerate((cWk, cWv)):
                for c in range(KD):
                    for k in range(KD):
                        last = nc.tensor.matmul(ps[2 + w][:, c * P:c * P + NR], wt[:, k, c * P:(c + 1) * P], o2T[:, k, :], start=(k == 0), stop=(k == KD - 1))
            last.then_inc(kv_ps, 1)

        @block.vector
        def _(v):
            n = [0]

            def step(ins):
                ins.then_inc(vst, 1)
                n[0] += 1
                v.wait_ge(vst, n[0])

            R = slice(0, NR)
            v.wait_ge(ld, 16 * NLOAD)
            v.wait_ge(pe_c, 2)
            step(nc.vector.tensor_tensor(o1[R, :], ps[3][R, 0:D], slotb[R, :], ALU.add))
            step(nc.vector.tensor_tensor(o1[R, :], o1[R, :], bo[R, :], ALU.add))
            step(nc.vector.bn_stats(stats[R, :], o1[R, :]))
            nc.vector.bn_aggr(mv[R, :], stats[R, :]).then_inc(kv_sb, 1)
            v.wait_ge(kv_sb, 1)
            step(nc.vector.tensor_scalar(rs[R, 0:1], mv[R, 1:2], 1e-5, None, ALU.add))
            v.wait_ge(root, 1)
            step(nc.vector.reciprocal(rs[R, 2:3], rs[R, 1:2]))
            step(nc.vector.tensor_scalar(hl[R, :], o1[R, :], mv[R, 0:1], rs[R, 2:3], ALU.subtract, ALU.mult))
            step(nc.vector.tensor_tensor(hl[R, :], hl[R, :], lng[R, :], ALU.mult))
            step(nc.vector.tensor_tensor(hl[R, :], hl[R, :], lnb[R, :], ALU.add))
            for q in range(2):
                nc.vector.tensor_copy(b1c[:, q, :, :].rearrange("p e f -> p (e f)"), ps[q][:, 0:P]).then_inc(bias_sb, 1)
            nc.vector.tensor_copy(b2c[:].rearrange("p e k -> p (e k)"), ps[2][:, 0:NE * KD]).then_inc(bias_sb, 1)
            v.wait_ge(bias_sb, 3)
            v.wait_ge(pe_c, 3)
            nr = lambda bank: ps[bank][:, 0:KD * P].rearrange("p (k n) -> p k n", k=KD)[:, :, 0:NR]
            step(nc.vector.tensor_copy(hT[:], nr(4)))
            step(nc.vector.tensor_copy(o1T[:], nr(5)))
            for k in range(KD):
                o = o1T[:, k, :].rearrange("p (b e) -> p b e", e=NE)
                step(nc.vector.tensor_tensor(o, o, b2c[:, :, k].unsqueeze(1).to_broadcast([P, NB, NE]), ALU.add))

            def pre(e):
                v.wait_ge(u_ps, e + 1)
                nc.vector.tensor_tensor(ub[e % 2][:], ps[6 + e % 2][:, 0:2 * NF * NB].rearrange("p (g f b) -> p g f b", g=2, f=NF),
                                        b1c[:, :, e, :].unsqueeze(3).to_broadcast([P, 2, NF, NB]), ALU.add).then_inc(u_pre, 1)
                v.wait_ge(u_act, e + 1)
                nc.vector.tensor_tensor(ug[e % 2][:], ub[e % 2][:, 0, :, :], ub[e % 2][:, 1, :, :], ALU.mult).then_inc(ug_sb, 1)

            def post(e):
                v.wait_ge(y_ps, e + 1)
                nc.vector.tensor_tensor(o2T[:, :, e:NR:NE], ps[e % 2][:, 0:KD * NB].rearrange("p (k b) -> p k b", k=KD), o1T[:, :, e:NR:NE],
                                        ALU.add).then_inc(o2_sb, 1)

            for e in range(NE + 1):
                if e < NE:
                    pre(e)
                if e:
                    post(e - 1)
            v.wait_ge(kv_ps, 1)
            for w, dst in enumerate((K["kT"], K["vT"])):
                for c in range(KD):
                    nc.vector.tensor_scalar(dst[:, c, :], ps[2 + w][:, c * P:c * P + NR], K["vecs"][:, 8 + 2 * w + c:9 + 2 * w + c], None, ALU.add)\
                        .then_inc(kv_sb, 1)
            v.wait_ge(kv_sb, 5)


def final_phase(nc, ctx, A, K, dram, ps, out):
    sem = lambda n: ctx.enter_context(nc.semaphore("t_" + n))
    NB = A["x"].shape[0]
    names = ["cwo", "xt0_loaded", "xt1_loaded", "h0_loaded", "h1_loaded", "kblk", "vblk", "m_ps", "m_sb", "row_sb", "vo_ps", "vo_sb", "sc_ps",
             "mx", "dif", "exp", "sum", "rec", "attn", "at_ps", "at_sb", "o_ps", "o_sb", "out0_stored", "out1_stored"]
    S = {n: sem(n) for n in names}
    with ExitStack() as tmp, nc.Block() as block:
        sb = lambda n, shape, dt=F32: tmp.enter_context(nc.sbuf_tensor("t_" + n, shape, dt))
        cWo = sb("cWo", [P, KD, D])
        xT = [sb(f"xT{q}", [P, KD, T]) for q in range(2)]
        h = [sb(f"h{q}", [P, NT, D]) for q in range(2)]
        kb = sb("kb", [P, KD, AH, NS])
        vb = sb("vb", [P, KD, AH, NS])
        Mc = sb("Mc", [P, KD, D])
        crow = sb("crow", [1, D])
        VW = sb("VW", [P, KD, D])
        sc = [sb(f"sc{q}", [P, 32, NS]) for q in range(2)]
        ex = [sb(f"ex{q}", [P, 32, NS]) for q in range(2)]
        at = [sb(f"at{q}", [P, 2, D]) for q in range(2)]
        aT = [sb(f"aT{q}", [P, 2, KD, P]) for q in range(2)]
        mx = sb("mx", [P, 4, 3, 32])
        blk = lambda a: a.rearrange("p h q -> p (h q)")
        outv = out.rearrange("b (t p) d -> b p t d", p=P)
        GR = NT // 2

        @block.sync
        def _(sp):
            sp.dma_start(cWo[:], A["L0_ffn_c_Wo"].rearrange("(k p) n -> p k n", p=P)).then_inc(S["cwo"], 16)
            with sp.Fori(0, NB // 2) as c:
                for q in range(2):
                    sp.wait_ge(S["sc_ps"], c * 2 * GR)
                    sp.dma_start(xT[q][:], dram["xn2T"][:, bass.ds((c * 2 + q) * KD, KD), :]).then_inc(S[f"xt{q}_loaded"], 16)
                    sp.wait_ge(S[f"out{q}_stored"], c * 16)
                    sp.dma_start(h[q][:], dram["h2"][:, bass.ds((c * 2 + q) * NT, NT), :]).then_inc(S[f"h{q}_loaded"], 16)

        @block.gpsimd
        def _(pool):
            hm = lambda k: K["hmask"][:, k, :].unsqueeze(2).to_broadcast([P, AH, NS])
            with pool.Fori(0, NB // 2) as c:
                for q in range(2):
                    b = c * 2 + q
                    pool.wait_ge(S["m_ps"], b)
                    pool.wait_ge(S["vo_ps"], b)
                    for k in range(KD):
                        nc.gpsimd.tensor_tensor(kb[:, k, :, :], K["kT"][:, k, bass.ds(b * NS, NS)].unsqueeze(1).to_broadcast([P, AH, NS]), hm(k), ALU.mult)\
                            .then_inc(S["kblk"], 1)
                    for k in range(KD):
                        nc.gpsimd.tensor_tensor(vb[:, k, :, :], K["vT"][:, k, bass.ds(b * NS, NS)].unsqueeze(1).to_broadcast([P, AH, NS]), hm(k), ALU.mult)\
                            .then_inc(S["vblk"], 1)
                    for g in range(GR):
                        n = b * GR + g
                        pool.wait_ge(S["rec"], n + 1)
                        if g >= 2:
                            pool.wait_ge(S["at_ps"], n - 1)
                        nc.gpsimd.tensor_tensor(at[g % 2][:].rearrange("p t (h s) -> p (t h) s", s=NS), ex[g % 2][:],
                                                mx[:, g, 2, :].unsqueeze(2).to_broadcast([P, 32, NS]), ALU.mult).then_inc(S["attn"], 1)

        @block.tensor
        def _(pe):
            def scores(b, q, g):
                n = b * GR + g
                if g >= 2:
                    pe.wait_ge(S["dif"], n - 1)
                bank = g % 2
                for j in range(2):
                    t = 2 * g + j
                    o = ps[bank][:, j * D:(j + 1) * D]
                    for k in range(KD):
                        nc.tensor.matmul(o, xT[q][:, k, t * P:(t + 1) * P], Mc[:, k, :], start=(k == 0), stop=False)
                    last = nc.tensor.matmul(o, K["ones"][0:1, :], crow[0:1, :], start=False, stop=True)
                last.then_inc(S["sc_ps"], 1)

            def values(b, q, g):
                n = b * GR + g
                pe.wait_ge(S["attn"], n + 1)
                if g >= 2:
                    pe.wait_ge(S["at_sb"], n - 1)
                    pe.wait_ge(S["o_sb"], n - 1)
                for j in range(2):
                    for m in range(KD):
                        last = nc.tensor.transpose(ps[2 + g % 2][:, (j * KD + m) * P:(j * KD + m + 1) * P], at[g % 2][:, j, m * P:(m + 1) * P], K["ident"][:])
                last.then_inc(S["at_ps"], 1)
                pe.wait_ge(S["at_sb"], n + 1)
                for j in range(2):
                    for m in range(KD):
                        last = nc.tensor.matmul(ps[4 + g % 2][:, j * D:(j + 1) * D], aT[g % 2][:, j, m, :], VW[:, m, :], start=(m == 0), stop=(m == KD - 1))
                last.then_inc(S["o_ps"], 1)

            pe.wait_ge(S["cwo"], 16)
            with pe.Fori(0, NB // 2) as c:
                for q in range(2):
                    b = c * 2 + q
                    pe.wait_ge(S["kblk"], b * 2 + 2)
                    for d in range(KD):
                        for k in range(KD):
                            last = nc.tensor.matmul(ps[6][:, d * D:(d + 1) * D], K["cWqT"][:, k, d * P:(d + 1) * P], blk(kb[:, k, :, :]), start=(k == 0), stop=(k == KD - 1))
                    pe.wait_ge(S["dif"], b * GR)
                    for k in range(KD):
                        last = nc.tensor.matmul(ps[0][0:1, 0:D], K["vecs"][:, 6 + k:7 + k], blk(kb[:, k, :, :]), start=(k == 0), stop=(k == KD - 1))
                    last.then_inc(S["m_ps"], 1)
                    pe.wait_ge(S["vblk"], b * 2 + 2)
                    for m in range(KD):
                        for k in range(KD):
                            last = nc.tensor.matmul(ps[7][:, m * D:(m + 1) * D], blk(vb[:, k, :, :])[:, m * P:(m + 1) * P], cWo[:, k, :], start=(k == 0), stop=(k == KD - 1))
                    last.then_inc(S["vo_ps"], 1)
                    pe.wait_ge(S["m_sb"], b + 1)
                    pe.wait_ge(S["row_sb"], b + 1)
                    pe.wait_ge(S["vo_sb"], b + 1)
                    pe.wait_ge(S["o_sb"], b * GR)
                    pe.wait_ge(S[f"xt{q}_loaded"], c * 16 + 16)
                    for g in range(GR + 1):
                        if g < GR:
                            scores(b, q, g)
                        if g:
                            values(b, q, g - 1)

        @block.scalar
        def _(act):
            copy = lambda o, i: nc.scalar.activation(o, i, ACT.Copy)
            with act.Fori(0, NB // 2) as c:
                for q in range(2):
                    b = c * 2 + q
                    act.wait_ge(S["m_ps"], b + 1)
                    act.wait_ge(S["at_ps"], b * GR)
                    copy(Mc[:], ps[6][:].rearrange("p (k n) -> p k n", k=KD)).then_inc(S["m_sb"], 1)
                    copy(crow[:], ps[0][0:1, 0:D]).then_inc(S["row_sb"], 1)
                    act.wait_ge(S["vo_ps"], b + 1)
                    copy(VW[:], ps[7][:].rearrange("p (k n) -> p k n", k=KD)).then_inc(S["vo_sb"], 1)
                    for g in range(GR + 1):
                        n = b * GR + g
                        if g < GR:
                            act.wait_ge(S["dif"], n + 1)
                            if g >= 2:
                                act.wait_ge(S["attn"], n - 1)
                            nc.scalar.activation(ex[g % 2][:], sc[g % 2][:], ACT.Exp, scale=0.25).then_inc(S["exp"], 1)
                        if g:
                            act.wait_ge(S["at_ps"], n)
                            copy(aT[(g - 1) % 2][:].rearrange("p j m n -> p (j m n)"), ps[2 + (g - 1) % 2][:]).then_inc(S["at_sb"], 1)
                            act.wait_ge(S["o_sb"], n)
                            if g == GR:
                                act.dma_start(outv[bass.ds(b, 1), :, :, :].rearrange("b p t d -> (b p) t d"), h[q][:]).then_inc(S[f"out{q}_stored"], 16)
            for q in range(2):
                act.wait_ge(S[f"out{q}_stored"], 16 * (NB // 2))

        @block.vector
        def _(v):
            with v.Fori(0, NB // 2) as c:
                for q in range(2):
                    b = c * 2 + q
                    for g in range(GR + 1):
                        n = b * GR + g
                        if g < GR:
                            s3 = ps[g % 2][:].rearrange("p (n s) -> p n s", s=NS)
                            b3 = lambda a: a.unsqueeze(2).to_broadcast([P, 32, NS])
                            v.wait_ge(S["sc_ps"], n + 1)
                            nc.vector.tensor_reduce(mx[:, g, 0, :], s3, AX.X, ALU.max).then_inc(S["mx"], 1)
                            v.wait_ge(S["mx"], n + 1)
                            if g >= 2:
                                v.wait_ge(S["exp"], n - 1)
                            nc.vector.tensor_tensor(sc[g % 2][:], s3, b3(mx[:, g, 0, :]), ALU.subtract).then_inc(S["dif"], 1)
                        if g < GR:
                            v.wait_ge(S["exp"], n + 1)
                            nc.vector.tensor_reduce(mx[:, g, 1, :], ex[g % 2][:], AX.X, ALU.add).then_inc(S["sum"], 1)
                            v.wait_ge(S["sum"], n + 1)
                            nc.vector.reciprocal(mx[:, g, 2, :], mx[:, g, 1, :]).then_inc(S["rec"], 1)
                        if g:
                            if g == 1:
                                v.wait_ge(S[f"h{q}_loaded"], c * 16 + 16)
                            v.wait_ge(S["o_ps"], n)
                            h2 = h[q][:, 2 * g - 2:2 * g, :]
                            nc.vector.tensor_tensor(h2, ps[4 + (g - 1) % 2][:].rearrange("p (t n) -> p t n", t=2), h2, ALU.add).then_inc(S["o_sb"], 1)


def tower(nc, A, out):
    NB = A["x"].shape[0]
    with ExitStack() as ctx:
        dram = scratch(nc, NB)
        K = constants(nc, ctx, NB)
        K["psum"] = ctx.enter_context(nc.psum_tensor("psum", [P, 8, 512], F32))
        ps = [K["psum"][:, i, :] for i in range(8)]
        setup(nc, ctx, A, K, dram, ps)
        delta_phase(nc, ctx, A, K, dram, ps)
        filter_phase(nc, ctx, A, K, dram, ps)
        slot_setup(nc, ctx, A, K, dram, ps)
        gate_phase(nc, ctx, A, K, dram, ps)
        expert_phase(nc, ctx, A, K, dram, ps)
        final_phase(nc, ctx, A, K, dram, ps, out)


_ATTN = ("Wq", "Wk", "Wv", "Wb", "conv_q", "conv_k", "conv_v", "fir_long", "fir_short", "W1", "b1", "W2", "b2", "log_temp",
         "base_bias", "conv_residual_logit", "rms_w", "Wo")
_FFN = ("slot_query", "d_Wq", "d_Wk", "d_Wv", "d_Wo", "d_bq", "d_bk", "d_bv", "d_bo", "c_Wq", "c_Wk", "c_Wv", "c_Wo", "c_bq", "c_bk",
        "c_bv", "c_bo", "e_ln_g", "e_ln_b", "e_W1", "e_b1", "e_Wg", "e_bg", "e_W2", "e_b2")
_INS = ["x"] + [f"L0_tok_{n}{i}" for i in range(3) for n in ("emb", "w")] + ["L0_attn_" + n for n in _ATTN] + ["L0_ffn_" + n for n in _FFN]


def kernel(**inputs):
    import numpy as _np
    import concourse.bacc as _bacc
    from concourse import mybir as _mybir
    from concourse.bass_utils import run_bass_kernel_spmd as _run

    nc = _bacc.Bacc("TRN2", target_bir_lowering=False, num_devices=1)
    arrays, args = {}, {}
    for name in _INS:
        a = _np.ascontiguousarray(inputs[name])
        arrays[f"in_{name}_dram"] = a
        args[name] = nc.dram_tensor(f"in_{name}_dram", a.shape, _mybir.dt.from_np(a.dtype), kind="ExternalInput").ap()
    shape = tuple(inputs["x"].shape) + (D,)
    out = nc.dram_tensor("out_0_dram", shape, F32, kind="ExternalOutput").ap()
    tower(nc, args, out)
    r = _run(nc, [arrays], core_ids=[0])
    return r.results[0]["out_0_dram"]
```

```python
from contextlib import ExitStack
from math import sqrt

import concourse.bass as bass
from concourse import mybir

F32 = mybir.dt.float32
I32 = mybir.dt.int32
U32 = mybir.dt.uint32
BF16 = mybir.dt.bfloat16
ALU = mybir.AluOpType
ACT = mybir.ActivationFunctionType
AX = mybir.AxisListType

P = 128
D = 256
KD = D // P
T = 1024
NT = T // P
EDGES = (0, 5000, 10000, 50257)
EMB_W = (256, 64, 64)
KE = sum(EMB_W) // P
H, DH = 4, 64
TAPS = 4
FIR = (5, 64)
FPAD = 320
FW = (132, 192)
BS = 32
NBLK = P // BS
NST = 16
LEVELS = 2
AH, AD = 16, 16
NS = 16
FF = 1024


def rows_of(h):
    r = 64 * (h % 2)
    return slice(r, r + 64), h // 2


def setup(nc, ctx, A, K, dram, ps):
    sem = lambda n: ctx.enter_context(nc.semaphore(n))
    wl, cl, fl = sem("weights_loaded"), sem("consts_loaded"), sem("filters_loaded")
    pool_c, vst, pe_c, pad_st = sem("pool_consts"), sem("setup_vector_step"), sem("setup_pe_group"), sem("padded_stored")
    act_c = sem("setup_scalar_step")
    NB = A["x"].shape[0]
    NTT = NB * NT
    with ExitStack() as tmp, nc.Block() as block:
        sb = lambda n, shape, dt=F32: tmp.enter_context(nc.sbuf_tensor(n, shape, dt))
        wcat = sb("wcat", [P, KD, KE * P])
        ids_row = sb("ids_row", [NTT, P], I32)
        ids_rf = sb("ids_rf", [NTT, P])
        idf = sb("idf", [P, NTT])
        t1 = sb("t1", [P, NTT])
        t2 = sb("t2", [P, NTT])
        firw = [sb(f"firw{f}", [P, KD, FIR[f]]) for f in range(2)]
        padded = [sb(f"padded{f}", [P, KD, FPAD]) for f in range(2)]
        lt = sb("lt", [P, 8, 4])

        @block.sync
        def _(sp):
            col = 0
            for i, w in enumerate(EMB_W):
                sp.dma_start(wcat[:, :, col:col + w], A[f"L0_tok_w{i}"].rearrange("(k p) n -> p k n", p=P)).then_inc(wl, 16)
                col += w
            sp.dma_start(ids_row[:], A["x"].rearrange("b (t p) -> (b t) p", p=P)).then_inc(wl, 16)
            for f, n in enumerate(("L0_attn_fir_short", "L0_attn_fir_long")):
                sp.dma_start(firw[f][:], A[n].rearrange("h d t -> (h d) t").rearrange("(k p) t -> p k t", p=P)).then_inc(fl, 16)
            for n in ("Wq", "Wk", "Wv", "Wo"):
                sp.dma_start(K[n][:], A["L0_attn_" + n].rearrange("(k p) n -> p k n", p=P)).then_inc(cl, 16)
            sp.dma_start(K["W1x"][:], A["L0_attn_W1"][0:D, :].rearrange("(k p) n -> p k n", p=P)).then_inc(cl, 16)
            sp.dma_start(K["W1s"][:], A["L0_attn_W1"][D:D + NST, :]).then_inc(cl, 16)
            sp.dma_start(K["W2"][:], A["L0_attn_W2"].rearrange("(k p) n -> p k n", p=P)).then_inc(cl, 16)
            sp.dma_start(K["Wb"][:], A["L0_attn_Wb"].rearrange("(k p) n -> p k n", p=P)).then_inc(cl, 16)
            sp.wait_ge(vst, 20)
            for f in range(2):
                sp.dma_start(dram["fpad"][f].rearrange("(k p) t -> p k t", p=P), padded[f][:]).then_inc(pad_st, 16)
            sp.wait_ge(pad_st, 32)
            sp.wait_ge(cl, 16 * 14)

        @block.scalar
        def _(act):
            for j, n in enumerate(("conv_v", "conv_k", "conv_q")):
                act.dma_start(K["convw"][:, 2 * j:2 * j + 2, :], A["L0_attn_" + n].rearrange("(k p) t -> p k t", p=P)).then_inc(cl, 16)
            act.dma_start(K["b1"][:], A["L0_attn_b1"].rearrange("(k p o) -> p k o", p=P, o=1), allow_slow_non_contiguous=True).then_inc(cl, 16)
            for r in range(2):
                act.dma_start(K["rmsw"][64 * r:64 * r + 64, :], A["L0_attn_rms_w"].rearrange("(p o) -> p o", o=1)).then_inc(cl, 16)
            rowb = lambda ap, n: bass.AP(ap.tensor, 0, [[0, P], [1, n]])
            act.dma_start(K["lbias"][:], rowb(A["L0_attn_base_bias"], 16)).then_inc(fl, 16)
            act.dma_start(lt[:, 0, :], rowb(A["L0_attn_b2"], 4)).then_inc(fl, 16)
            act.dma_start(lt[:, 1, :], rowb(A["L0_attn_log_temp"], 4)).then_inc(fl, 16)
            act.dma_start(lt[:, 2, :], rowb(A["L0_attn_conv_residual_logit"], 4)).then_inc(fl, 16)
            act.wait_ge(fl, 16 * 6)
            nc.scalar.activation(lt[:, 3, :], lt[:, 1, :], ACT.Abs).then_inc(act_c, 1)
            act.wait_ge(act_c, 1)
            nc.scalar.activation(lt[:, 4, :], lt[:, 3, :], ACT.Exp, scale=-1.0).then_inc(act_c, 1)
            nc.scalar.activation(lt[:, 5, :], lt[:, 2, :], ACT.Exp, scale=-1.0).then_inc(act_c, 1)
            act.wait_ge(vst, 22)
            nc.scalar.activation(lt[:, 4, :], lt[:, 4, :], ACT.Ln).then_inc(act_c, 1)

        @block.gpsimd
        def _(pool):
            n = [0]

            def keep(where, cmp, fill, base, pattern, mult, before=None):
                pool.wait_ge(pool_c, n[0])
                nc.gpsimd.affine_select(out=where, in_=where, compare_op=cmp, fill=fill, base=base,
                                        pattern=pattern, channel_multiplier=mult).then_inc(pool_c, 1)
                n[0] += 1
                return n[0]

            def fill(where, value):
                if n[0]:
                    pool.wait_ge(pool_c, n[0])
                nc.gpsimd.memset(where, value).then_inc(pool_c, 1)
                n[0] += 1
                return n[0]

            keep(K["ident"][:], ALU.not_equal, 1.0, 0, [[-1, P]], 1, fill(K["ident"][:], 0.0))
            keep(K["up_strict"][:], ALU.is_gt, 0.0, 0, [[1, P]], -1, fill(K["up_strict"][:], 1.0))
            keep(K["up_incl"][:], ALU.is_ge, 0.0, 0, [[1, P]], -1, fill(K["up_incl"][:], 1.0))
            keep(K["anti"][:], ALU.not_equal, 1.0, 1 - P, [[1, P]], 1, fill(K["anti"][:], 0.0))
            at = fill(K["sel2"][:], 0.0)
            pool.wait_ge(pool_c, at)
            fill(K["sel2"][0:64, 0:1], 1.0)
            fill(K["sel2"][64:128, 1:2], 1.0)
            for l in range(LEVELS):
                m = BS << l
                w = K["wmask"][:, l, :]
                v = w.rearrange("i (g two m) -> i g two m", two=2, m=m)
                at = fill(w, 0.0)
                pool.wait_ge(pool_c, at)
                at = fill(v[:, :, 0, :], -1.0)
                at = keep(v[:, :, 0, :], ALU.is_ge, 0.0, -m, [[-2 * m, P // (2 * m)], [0, m]], 1, at)
                at = keep(v[:, :, 0, :], ALU.is_ge, 0.0, 2 * m - 1, [[2 * m, P // (2 * m)], [0, m]], -1, at)
                keep(w, ALU.not_equal, 1.0, 0, [[-1, P]], 1, at)
            at = fill(K["bmask"][:], 1.0)
            at = keep(K["bmask"][:], ALU.is_ge, 0.0, 0, [[-BS, NBLK]], 1, at)
            keep(K["bmask"][:], ALU.is_ge, 0.0, BS - 1, [[BS, NBLK]], -1, at)
            hm = K["hmask"]
            at = fill(hm[:], 1.0)
            for k in range(KD):
                at = keep(hm[:, k, :], ALU.is_ge, 0.0, k * P, [[-AD, AH]], 1, at)
                at = keep(hm[:, k, :], ALU.is_ge, 0.0, AD - 1 - k * P, [[AD, AH]], -1, at)
            fill(K["qsel"][:], 0.0)
            for g in range(P // NS):
                keep(K["qsel"][:], ALU.not_equal, 1.0, -NS * g, [[-1, NS]], 1)
            fill(K["ones"][:], 1.0)
            pool.wait_ge(pool_c, n[0])

        @block.tensor
        def _(pe):
            pe.wait_ge(pool_c, 2)
            pe.wait_ge(wl, 64)
            for k in range(KE):
                for dh in range(KD):
                    n = k * KD + dh
                    last = nc.tensor.transpose(ps[n // 4][:, (n % 4) * P:(n % 4 + 1) * P], wcat[:, dh, k * P:(k + 1) * P], K["ident"][:])
            last.then_inc(pe_c, 1)
            pe.wait_ge(vst, 1)
            nc.tensor.transpose(ps[2][:, 0:NTT], ids_rf[:], K["ident"][0:NTT, 0:NTT]).then_inc(pe_c, 1)

        @block.vector
        def _(v):
            n = [0]

            def step(ins, fence=True):
                ins.then_inc(vst, 1)
                n[0] += 1
                if fence:
                    v.wait_ge(vst, n[0])

            v.wait_ge(wl, 64)
            step(nc.vector.tensor_copy(ids_rf[:], ids_row[:]))
            v.wait_ge(pe_c, 1)
            step(nc.vector.tensor_copy(K["WcT"][:, 0:2, :], ps[0][:].rearrange("p (k n) -> p k n", k=2)), False)
            step(nc.vector.tensor_copy(K["WcT"][:, 2, :], ps[1][:, 0:D]), False)
            v.wait_ge(pe_c, 2)
            step(nc.vector.tensor_copy(idf[:], ps[2][:, 0:NTT]))
            for i in range(3):
                lo, hi = EDGES[i], EDGES[i + 1]
                step(nc.vector.tensor_scalar(t1[:], idf[:], float(-lo), 0.0, ALU.add, ALU.max), False)
                step(nc.vector.tensor_scalar(t2[:], idf[:], float(lo), None, ALU.is_ge))
                step(nc.vector.tensor_scalar(K["rows"][:, i, :], t1[:], float(hi - lo - 1), None, ALU.min), False)
                step(nc.vector.scalar_tensor_tensor(K["mask"][:, i, :], idf[:], float(hi), t2[:], ALU.is_lt, ALU.mult))
            assert n[0] == 16
            v.wait_ge(fl, 16 * 6)
            for f in range(2):
                step(nc.vector.memset(padded[f][:], 0.0))
                a = firw[f][:]
                back = bass.AP(a.tensor, a.offset + FIR[f] - 1, [a.ap[0], [FIR[f], KD], [-1, FIR[f]]])
                step(nc.vector.tensor_copy(padded[f][:, :, P - 1:P - 1 + FIR[f]], back))
            assert n[0] == 20
            v.wait_ge(act_c, 3)
            step(nc.vector.tensor_scalar(lt[:, 5, :], lt[:, 5, :], 1.0, None, ALU.add))
            step(nc.vector.tensor_scalar(lt[:, 4, :], lt[:, 4, :], 1.0, None, ALU.add))
            v.wait_ge(act_c, 4)
            step(nc.vector.tensor_scalar(lt[:, 6, :], lt[:, 1, :], 0.0, 1e-4, ALU.max, ALU.add))
            step(nc.vector.tensor_tensor(lt[:, 6, :], lt[:, 6, :], lt[:, 4, :], ALU.add))
            step(nc.vector.reciprocal(K["itemp"][:], lt[:, 6, :]))
            step(nc.vector.tensor_copy(K["itemp16"][:].rearrange("p (h j) -> p h j", h=H), K["itemp"][:].unsqueeze(2).to_broadcast([P, H, 4])))
            step(nc.vector.reciprocal(lt[:, 7, :], lt[:, 5, :]))
            step(nc.vector.tensor_scalar(K["halfsig"][:], lt[:, 7, :], 0.5, None, ALU.mult))
            step(nc.vector.tensor_tensor(K["lbias"][:].rearrange("p (h j) -> p h j", h=H), K["lbias"][:].rearrange("p (h j) -> p h j", h=H),
                                         lt[:, 0, :].unsqueeze(1).to_broadcast([P, H, 4]), ALU.add))
            v.wait_ge(cl, 16 * 14)
            for k in range(KD):
                step(nc.vector.tensor_scalar(K["Wo"][:, k, :], K["Wo"][:, k, :], K["rmsw"][:, 0:1], None, ALU.mult), False)
            v.wait_ge(vst, n[0])


def delta_phase(nc, ctx, A, K, dram, ps):
    NB = A["x"].shape[0]
    names = ["gathered", "rows_copied", "rows_masked", "gt_ps", "gt_sb", "h_ps", "h_sb", "h_stored", "ln_stats", "ln_aggr", "ln_eps",
             "ln_std", "ln_rstd", "xn_done", "xt_ps", "xt_sb", "pj_ps", "pj_sb", "conv_step", "silu_done", "sq_done", "ss_ps",
             "norm_eps", "norm_root", "norm_inv", "gamma_sq", "gamma_done", "tm_ps", "tm_sb", "vk_done", "v_stored", "xw1_stored",
             "gk_ps", "qk_ps", "at_sb", "qk_sb", "qkt_done", "a1_sb", "x1t_sb", "x1_ps", "p_ps", "q_sb", "x_ps", "x_sb", "xt2_ps", "xt2_sb",
             "blocks_stored", "blocks_loaded", "unit_set", "subst", "inverses_stored", "inverses_loaded",
             "ks_ps", "r_sb", "y_ps", "z_sb", "ds_ps", "s_sb", "o_ps", "o_sb", "delta_stored", "pads", "gather_go", "ln_go"]
    S = {n: nc.alloc_semaphore(name=n) for n in names}

    with ExitStack() as tmp, nc.Block() as block:
        sb = lambda n, shape, dt=F32: tmp.enter_context(nc.sbuf_tensor(n, shape, dt))
        rowsb = sb("rowsb", [P, 3, NT], U32)
        G = sb("G", [P, NT, KE * P])
        GT = sb("GT", [P, KE, T])
        h_tm = sb("h_tm", [P, NT, D])
        stats = sb("stats", [P, NT, 6])
        mv = sb("mv", [P, NT, 2])
        rstd = sb("rstd", [P, 3, NT])
        xn = sb("xn", [P, NT, D])
        xnT = sb("xnT", [P, KD, T])
        raw = sb("raw", [P, 6, TAPS - 1 + T])
        cm = sb("cm", [P, 6, T])
        beta = sb("beta", [P, NT * H])
        nrm = sb("nrm", [P, 2, NT * H])
        inv = sb("inv", [P, 2, NT * H])
        gam = sb("gam", [P, 2, NT * H])
        xw1 = sb("xw1", [P, KD, T])
        v_tm = sb("v_tm", [P, NT, D])
        k_tm = sb("k_tm", [P, NT, D])
        vk = xn
        dl = h_tm
        A1T = sb("A1T", [P, NT, H, P])
        gt_flat = GT[:].rearrange("p k t -> p (k t)")
        AB, XB, XC = [gt_flat[:, i * BS * BS:(i + 1) * BS * BS].rearrange("p (j i) -> p j i", i=BS) for i in range(3)]
        prod = sb("prod", [P, BS * BS // 4])
        X = [sb(f"X{j}", [P, H, P]) for j in range(2)]
        Q = [sb(f"Q{j}", [P, H, P]) for j in range(2)]
        XT = [sb(f"XT{j}", [P, H, P]) for j in range(4)]
        QKT = sb("QKT", [P, NT, H, P])
        St = sb("St", [P, 2, 2, DH])
        R = sb("R", [P, D])
        z = sb("z", [P, D])

        sq = raw[:, 2:6, TAPS - 1:]
        g4 = lambda bank: ps[bank][:].rearrange("p (h n) -> p h n", h=H)
        h4 = lambda bank: ps[bank][:, 0:D].rearrange("p (h n) -> p h n", h=H)
        per_head = lambda a, t, n: a[:, t * H:(t + 1) * H].unsqueeze(2).to_broadcast([P, H, n])
        by_head = lambda a: a.rearrange("p (h n) -> p h n", h=H)
        over_heads = lambda m: m.unsqueeze(1).to_broadcast([P, H, P])
        ORDER = (2, 3, 0, 1, 4, 5)
        C = 2 * LEVELS
        CT = C * NT // 2

        @block.gpsimd
        def _(pool):
            def gather(b):
                pool.wait_ge(S["gathered"], b * (3 * NT * 16))
                pool.wait_ge(S["gt_ps"], b * 6)
                nc.gpsimd.tensor_copy(rowsb[:], K["rows"][:, :, bass.ds(b * NT, NT)]).then_inc(S["rows_copied"], 1)
                pool.wait_ge(S["rows_copied"], b + 1).then_inc(S["gather_go"], 1)
                for t in range(NT):
                    col = 0
                    for i in range(3):
                        nc.gpsimd.indirect_dma_start(G[:, t, col:col + EMB_W[i]], None, A[f"L0_tok_emb{i}"],
                                                     bass.IndirectOffsetOnAxis(ap=rowsb[:, i, t:t + 1], axis=0)).then_inc(S["gathered"], 16)
                        col += EMB_W[i]

            def sequence(b, more):
                if more:
                    gather(b + 1)
                for t in range(NT):
                    pool.wait_ge(S["at_sb"], b * H * NT + H * t + H)
                    nc.gpsimd.tensor_tensor(A1T[:, t], A1T[:, t], over_heads(K["ident"][:]), ALU.add).then_inc(S["a1_sb"], 1)
                pool.wait_ge(S["norm_root"], b * 2 + 1)
                pool.wait_ge(S["tm_sb"], b * 8 + 4)
                nc.gpsimd.tensor_tensor(vk[:].rearrange("p t (h n) -> p (t h) n", h=H), v_tm[:].rearrange("p t (h n) -> p (t h) n", h=H),
                                        nrm[:, 0, :].unsqueeze(2).to_broadcast([P, NT * H, DH]), ALU.mult).then_inc(S["vk_done"], 1)
                for p in range(NT // 2):
                    pool.wait_ge(S["qk_sb"], b * NT + 2 * p + 2)
                    for t in (2 * p, 2 * p + 1):
                        nc.gpsimd.tensor_tensor(QKT[:, t], QKT[:, t], over_heads(K["up_incl"][:]), ALU.mult).then_inc(S["qkt_done"], 1)
                pool.wait_ge(S["inverses_loaded"], b * 16 * NBLK + 16 * NBLK)
                for t in range(NT):
                    if t >= 4:
                        pool.wait_ge(S["y_ps"], b * NT + t - 3)
                    nc.gpsimd.tensor_tensor(XT[t % 4][:].rearrange("p h (g j) -> p h g j", j=BS),
                                            XC[:, t * H:(t + 1) * H, :].unsqueeze(2).to_broadcast([P, H, NBLK, BS]),
                                            K["bmask"][:].unsqueeze(1).unsqueeze(3).to_broadcast([P, H, NBLK, BS]), ALU.mult).then_inc(S["x1t_sb"], 1)

            gather(0)
            with pool.Fori(0, NB - 1) as b:
                sequence(b, True)
            sequence(NB - 1, False)

        @block.sync
        def _(sp):
            with sp.Fori(0, NB) as b:
                sp.wait_ge(S["h_sb"], b * 4 + 4)
                sp.dma_start(dram["h"][:, bass.ds(b * NT, NT), :], h_tm[:]).then_inc(S["h_stored"], 16)
                sp.wait_ge(S["a1_sb"], b * NT + NT)
                for g in range(NBLK):
                    rows = slice(g * BS, (g + 1) * BS)
                    sp.dma_start(bass.AP(dram["blocks"].tensor, g * BS * BS, [[BS, BS], [NBLK * BS * BS, NT * H], [1, BS]]),
                                 A1T[rows, :, :, rows].rearrange("p t h n -> p (t h) n")).then_inc(S["blocks_stored"], 16)
                sp.wait_ge(S["blocks_stored"], b * 16 * NBLK + 16 * NBLK)
                sp.dma_start(AB.rearrange("p j i -> p (j i)"), dram["blocks"][:, :]).then_inc(S["blocks_loaded"], 16)
                sp.wait_ge(S["pj_sb"], b * 17 + 17)
                sp.dma_start(dram["xw1"][:, bass.ds(b * KD, KD), :], xw1[:]).then_inc(S["xw1_stored"], 16)
                sp.wait_ge(S["tm_sb"], b * 8 + 4)
                sp.dma_start(dram["v"][:, bass.ds(b * NT, NT), :], v_tm[:]).then_inc(S["v_stored"], 16)
                sp.wait_ge(S["subst"], b * 2 * (BS - 1) + 2 * (BS - 1))
                sp.dma_start(dram["inverses"][:, :], XB.rearrange("p j i -> p (j i)")).then_inc(S["inverses_stored"], 16)
                sp.wait_ge(S["inverses_stored"], b * 16 + 16)
                for g in range(NBLK):
                    sp.dma_start(XC[g * BS:(g + 1) * BS, :, :], bass.AP(dram["inverses"].tensor, g * BS * BS, [[BS, BS], [NBLK * BS * BS, NT * H], [1, BS]]))\
                        .then_inc(S["inverses_loaded"], 16)
                sp.wait_ge(S["o_sb"], b * 2 * NT + 2 * NT)
                sp.dma_start(dram["delta"][:, bass.ds(b * NT, NT), :], dl[:]).then_inc(S["delta_stored"], 16)
            for n in ("h_stored", "xw1_stored", "v_stored", "delta_stored"):
                sp.wait_ge(S[n], 16 * NB)

        @block.tensor
        def _(pe):
            ident = K["ident"][:]

            def inverse(b, p, s):
                tiles = (2 * p, 2 * p + 1)
                if s == 0:
                    if p:
                        pe.wait_ge(S["xt2_sb"], b * CT + p * C)
                    for t in tiles:
                        j = t % 2
                        pe.wait_ge(S["x1t_sb"], b * NT + t + 1)
                        for h in range(H):
                            last = nc.tensor.transpose(g4(4 + j)[:, h, :], XT[t % 4][:, h, :], ident)
                        last.then_inc(S["x1_ps"], 1)
                    return
                l = s - 1
                for t in tiles:
                    j = t % 2
                    pe.wait_ge(S["x_sb"], b * CT + p * C + 2 * l + j + 1)
                    if l:
                        pe.wait_ge(S["xt2_sb"], b * CT + p * C + 2 * l + j - 1)
                    for h in range(H):
                        last = nc.tensor.matmul(g4(j)[:, h, :], A1T[:, t, h, :], X[j][:, h, :], start=True, stop=True)
                    last.then_inc(S["p_ps"], 1)

            def inverse_rest(b, p, s):
                l = s - 1
                for t in (2 * p, 2 * p + 1):
                    j = t % 2
                    pe.wait_ge(S["q_sb"], b * CT + p * C + 2 * l + j + 1)
                    if l < LEVELS - 1:
                        for h in range(H):
                            last = nc.tensor.matmul(g4(2 + j)[:, h, :], XT[t % 4][:, h, :], Q[j][:, h, :], start=True, stop=True)
                        last.then_inc(S["x_ps"], 1)
                    for h in range(H):
                        last = nc.tensor.matmul(g4(4 + j)[:, h, :], Q[j][:, h, :], XT[t % 4][:, h, :], start=True, stop=True)
                    last.then_inc(S["xt2_ps"], 1)

            def scan(b, p, s):
                t = 2 * p + s // 3
                tk = slice(t * P, (t + 1) * P)
                if s % 3 == 0:
                    pe.wait_ge(S["s_sb"], b * (NT + 1) + t + 1)
                    pe.wait_ge(S["o_sb"], b * 2 * NT + 2 * t)
                    for h in range(H):
                        rows, i = rows_of(h)
                        last = nc.tensor.matmul(h4(6 + h % 2)[:, i, :], cm[rows, 2 + i, tk], St[rows, t % 2, i, :], start=True, stop=True)
                    last.then_inc(S["ks_ps"], 1)
                elif s % 3 == 1:
                    pe.wait_ge(S["r_sb"], b * 2 * NT + 2 * t + 2)
                    pe.wait_ge(S["xt2_sb"], b * CT + C * p + C)
                    for h in range(H):
                        last = nc.tensor.matmul(h4(6)[:, h, :], XT[t % 4][:, h, :], R[:, h * DH:(h + 1) * DH], start=True, stop=True)
                    last.then_inc(S["y_ps"], 1)
                else:
                    pe.wait_ge(S["z_sb"], b * NT + t + 1)
                    for h in range(H):
                        rows, i = rows_of(h)
                        last = nc.tensor.matmul(ps[7][rows, i * DH:(i + 1) * DH], k_tm[:, t, h * DH:(h + 1) * DH], z[:, h * DH:(h + 1) * DH],
                                                start=True, stop=True)
                    last.then_inc(S["ds_ps"], 1)
                    for h in (0, 2, 1, 3):
                        rows, i = rows_of(h)
                        if h == 1:
                            pe.wait_ge(S["s_sb"], b * (NT + 1) + t + 2)
                        nc.tensor.matmul(h4(6 + h % 2)[:, i, :], cm[rows, 4 + i, tk], St[rows, t % 2, i, :], start=True, stop=False)
                        last = nc.tensor.matmul(h4(6 + h % 2)[:, i, :], QKT[:, t, h, :], z[:, h * DH:(h + 1) * DH], start=False, stop=True)
                    last.then_inc(S["o_ps"], 1)

            with pe.Fori(0, NB) as b:
                pe.wait_ge(S["rows_masked"], b * 3 + 3)
                pe.wait_ge(S["xt2_sb"], b * CT)
                for n in range(6):
                    if n >= 4:
                        pe.wait_ge(S["gt_sb"], b * 6 + n - 3)
                    half, k = n // 3, n % 3
                    for q in range(4):
                        last = nc.tensor.transpose(ps[n % 4][:, q * P:(q + 1) * P], G[:, 4 * half + q, k * P:(k + 1) * P], ident)
                    last.then_inc(S["gt_ps"], 1)
                pe.wait_ge(S["o_sb"], b * 2 * NT)
                for n in range(4):
                    pe.wait_ge(S["gt_sb"], b * 6 + (3 if n < 2 else 6))
                    for q in range(2):
                        t = 2 * n + q
                        for k in range(KE):
                            last = nc.tensor.matmul(ps[4 + n][:, q * D:(q + 1) * D], GT[:, k, t * P:(t + 1) * P], K["WcT"][:, k, :],
                                                    start=(k == 0), stop=(k == KE - 1))
                    last.then_inc(S["h_ps"], 1)
                for n in range(4):
                    half, k = n // 2, n % 2
                    pe.wait_ge(S["xn_done"], b * NT + 4 * half + 4)
                    for q in range(4):
                        last = nc.tensor.transpose(ps[n][:, q * P:(q + 1) * P], xn[:, 4 * half + q, k * P:(k + 1) * P], ident)
                    last.then_inc(S["xt_ps"], 1)
                pe.wait_ge(S["h_sb"], b * 4 + 4)
                pe.wait_ge(S["xt_sb"], b * 4 + 4)
                for t in range(NT):
                    for k in range(KD):
                        last = nc.tensor.matmul(ps[4][:, t * H:(t + 1) * H], xnT[:, k, t * P:(t + 1) * P], K["Wb"][:, k, :],
                                                start=(k == 0), stop=(k == KD - 1))
                last.then_inc(S["pj_ps"], 1)
                def project(ns):
                    for n in ns:
                        if n >= 4:
                            pe.wait_ge(S["pj_sb"], b * 17 + n - 3)
                        w, m, c = (n - 1) // 4, (n - 1) // 2 % 2, (n - 1) % 2
                        for k in range(KD):
                            last = nc.tensor.matmul(ps[4 + n % 4][:], K[("Wk", "Wv", "Wq", "W1x")[w]][:, k, m * P:(m + 1) * P],
                                                    xnT[:, k, c * 512:(c + 1) * 512], start=(k == 0), stop=(k == KD - 1))
                        last.then_inc(S["pj_ps"], 1)

                def squares(w, bank):
                    pe.wait_ge(S["sq_done"], b * 4 + 2 * w + 2)
                    for i in range(2):
                        for t in range(NT):
                            last = nc.tensor.matmul(ps[bank][:, t * H + 2 * i:t * H + 2 * i + 2], sq[:, 2 * w + i, t * P:(t + 1) * P], K["sel2"][:],
                                                    start=True, stop=True)
                    last.then_inc(S["ss_ps"], 1)

                def gram(p, w, done):
                    for t in (2 * p, 2 * p + 1):
                        tk = slice(t * P, (t + 1) * P)
                        for h in range(H):
                            rows, i = rows_of(h)
                            last = nc.tensor.matmul(g4(2 * (p % 2) + h % 2)[:, 2 * (t % 2) + i, :], cm[rows, 2 + i, tk], cm[rows, w + i, tk],
                                                    start=True, stop=True)
                    last.then_inc(S[done], 1)

                project(range(1, 13))
                squares(0, 2)
                for p in range(NT // 2):
                    if p == 1:
                        pe.wait_ge(S["norm_eps"], b * 2 + 1)
                    if p >= 2:
                        pe.wait_ge(S["at_sb"], b * NT * H + 2 * H * (p - 1))
                    gram(p, 2, "gk_ps")
                project(range(13, 17))
                for n in range(8):
                    i, half = n // 2, n % 2
                    pe.wait_ge(S["silu_done"], b * 6 + (3 + i if i < 2 else 4))
                    if n < 4:
                        pe.wait_ge(S["pj_sb"], b * 17 + 14 + n)
                    else:
                        pe.wait_ge(S["tm_sb"], b * 8 + n - 3)
                    bank = (5, 6, 7, 4)[n % 4]
                    for q in range(4):
                        t = 4 * half + q
                        last = nc.tensor.transpose(ps[bank][:, q * P:(q + 1) * P], cm[:, i, t * P:(t + 1) * P], ident)
                    last.then_inc(S["tm_ps"], 1)
                pe.wait_ge(S["silu_done"], b * 6 + 6)
                for p in range(NT // 2):
                    if p < 2:
                        pe.wait_ge(S["at_sb"], b * NT * H + 2 * H * (p + 3))
                    else:
                        pe.wait_ge(S["qk_sb"], b * NT + 2 * (p - 1))
                    gram(p, 4, "qk_ps")
                pe.wait_ge(S["tm_sb"], b * 8 + 8)
                squares(1, 6)
                pe.wait_ge(S["qk_sb"], b * NT + NT)
                for p in range(NT // 2 + 1):
                    for s in range(6):
                        if p < NT // 2 and s % 2 == 0:
                            inverse(b, p, s // 2)
                        if p:
                            if p == 1 and s == 0:
                                pe.wait_ge(S["norm_eps"], b * 2 + 2)
                            if s == 0:
                                pe.wait_ge(S["qkt_done"], b * NT + 2 * p)
                            scan(b, p - 1, s)
                        if p < NT // 2 and s in (2, 4):
                            inverse_rest(b, p, s // 2)

        @block.scalar
        def _(act):
            ident_copy = lambda o, i: nc.scalar.activation(o, i, ACT.Copy)
            with act.Fori(0, NB) as b:
                for n in range(6):
                    act.wait_ge(S["gt_ps"], b * 6 + n + 1)
                    ident_copy(GT[:, n % 3, n // 3 * 512:(n // 3 + 1) * 512], ps[n % 4][:]).then_inc(S["gt_sb"], 1)
                act.wait_ge(S["delta_stored"], b * 16)
                for n in range(4):
                    act.wait_ge(S["h_ps"], b * 4 + n + 1)
                    ident_copy(h_tm[:, 2 * n:2 * n + 2, :], ps[4 + n][:].rearrange("p (t n) -> p t n", t=2)).then_inc(S["h_sb"], 1)
                act.wait_ge(S["ln_eps"], b + 1)
                nc.scalar.activation(rstd[:, 1, :], rstd[:, 0, :], ACT.Sqrt).then_inc(S["ln_std"], 1)
                for n in range(4):
                    act.wait_ge(S["xt_ps"], b * 4 + n + 1)
                    ident_copy(xnT[:, n % 2, n // 2 * 512:(n // 2 + 1) * 512], ps[n][:]).then_inc(S["xt_sb"], 1)
                act.wait_ge(S["pj_ps"], b * 17 + 1)
                nc.scalar.activation(beta[:], ps[4][:, 0:NT * H], ACT.Sigmoid).then_inc(S["pj_sb"], 1)
                act.wait_ge(S["pads"], 1)
                def projected(ns):
                    for n in ns:
                        act.wait_ge(S["pj_ps"], b * 17 + n + 1)
                        i, c = (n - 1) // 2, (n - 1) % 2
                        if i < 6:
                            ident_copy(raw[:, ORDER[i], TAPS - 1 + c * 512:TAPS - 1 + (c + 1) * 512], ps[4 + n % 4][:]).then_inc(S["pj_sb"], 1)
                        else:
                            if n == 13:
                                act.wait_ge(S["xw1_stored"], b * 16)
                            ident_copy(xw1[:, i - 6, c * 512:(c + 1) * 512], ps[4 + n % 4][:]).then_inc(S["pj_sb"], 1)

                def silu(w):
                    for i in range(2):
                        act.wait_ge(S["conv_step"], b * 24 + 8 * w + 7 + i)
                        nc.scalar.activation(cm[:, ORDER[2 * w + i], :], cm[:, ORDER[2 * w + i], :], ACT.Silu).then_inc(S["silu_done"], 1)

                def norms(w):
                    act.wait_ge(S["silu_done"], b * 6 + (2, 6)[w])
                    for i in range(2):
                        nc.scalar.activation(sq[:, 2 * w + i, :], cm[:, 2 + 2 * w + i, :], ACT.Square).then_inc(S["sq_done"], 1)
                    act.wait_ge(S["norm_eps"], b * 2 + w + 1)
                    nc.scalar.activation(nrm[:, w, :], nrm[:, w, :], ACT.Sqrt).then_inc(S["norm_root"], 1)

                projected(range(1, 13))
                silu(0)
                norms(0)
                projected(range(13, 17))
                silu(1)
                act.wait_ge(S["v_stored"], b * 16)
                act.wait_ge(S["vk_done"], b)
                for n in range(8):
                    i, half = n // 2, n % 2
                    act.wait_ge(S["tm_ps"], b * 8 + n + 1)
                    dst = (v_tm, k_tm)[i // 2][:, 4 * half:4 * half + 4, (i % 2) * P:(i % 2 + 1) * P]
                    ident_copy(dst, ps[(5, 6, 7, 4)[n % 4]][:].rearrange("p (t n) -> p t n", t=4)).then_inc(S["tm_sb"], 1)
                silu(2)
                for p in range(NT // 2):
                    act.wait_ge(S["qk_ps"], b * (NT // 2) + p + 1)
                    for r in range(2):
                        ident_copy(QKT[:, 2 * p:2 * p + 2, r::2, :].rearrange("p t i n -> p (t i) n"), g4(2 * (p % 2) + r)).then_inc(S["qk_sb"], 1)
                norms(1)
                for p in range(NT // 2):
                    for t in (2 * p, 2 * p + 1):
                        act.wait_ge(S["x1_ps"], b * NT + t + 1)
                        ident_copy(X[t % 2][:], g4(4 + t % 2)).then_inc(S["x_sb"], 1)
                    for l in range(LEVELS):
                        for t in (2 * p, 2 * p + 1):
                            if l < LEVELS - 1:
                                act.wait_ge(S["x_ps"], b * (CT - NT) + p * (C - 2) + 2 * l + t % 2 + 1)
                                ident_copy(X[t % 2][:], g4(2 + t % 2)).then_inc(S["x_sb"], 1)
                            act.wait_ge(S["xt2_ps"], b * CT + p * C + 2 * l + t % 2 + 1)
                            ident_copy(XT[t % 4][:], g4(4 + t % 2)).then_inc(S["xt2_sb"], 1)

        @block.vector
        def _(v):
            nc.vector.memset(raw[:, :, 0:TAPS - 1], 0.0).then_inc(S["pads"], 1)
            with v.Fori(0, NB) as b:
                v.wait_ge(S["gathered"], b * (3 * NT * 16) + 3 * NT * 16)
                col = 0
                for i in range(3):
                    g = G[:, :, col:col + EMB_W[i]]
                    nc.vector.tensor_tensor(g, g, K["mask"][:, i, bass.ds(b * NT, NT)].unsqueeze(2).to_broadcast([P, NT, EMB_W[i]]),
                                            ALU.mult).then_inc(S["rows_masked"], 1)
                    col += EMB_W[i]
                for t in range(NT):
                    v.wait_ge(S["h_sb"], b * 4 + t // 2 + 1)
                    nc.vector.bn_stats(stats[:, t, :], h_tm[:, t, :]).then_inc(S["ln_stats"], 1)
                v.wait_ge(S["ln_stats"], b * NT + NT).then_inc(S["ln_go"], 1)
                for t in range(NT):
                    nc.vector.bn_aggr(mv[:, t, :], stats[:, t, :]).then_inc(S["ln_aggr"], 1)
                v.wait_ge(S["ln_aggr"], b * NT + NT)
                nc.vector.tensor_scalar(rstd[:, 0, :], mv[:, :, 1], 1e-5, None, ALU.add).then_inc(S["ln_eps"], 1)
                v.wait_ge(S["ln_std"], b + 1)
                nc.vector.reciprocal(rstd[:, 2, :], rstd[:, 1, :]).then_inc(S["ln_rstd"], 1)
                v.wait_ge(S["ln_rstd"], b + 1)
                for t in range(NT):
                    nc.vector.tensor_scalar(xn[:, t, :], h_tm[:, t, :], mv[:, t, 0:1], rstd[:, 2, t:t + 1], ALU.subtract, ALU.mult)\
                        .then_inc(S["xn_done"], 1)
                def conv(w):
                    for n in range(2 * TAPS):
                        j, i = n // 2, ORDER[2 * w + n % 2]
                        if j == 0:
                            v.wait_ge(S["pj_sb"], b * 17 + 3 + 2 * (2 * w + n % 2))
                            nc.vector.tensor_scalar(cm[:, i, :], raw[:, i, 0:T], K["convw"][:, i, 0:1], None, ALU.mult).then_inc(S["conv_step"], 1)
                        else:
                            v.wait_ge(S["conv_step"], b * 24 + 8 * w + n - 1)
                            nc.vector.scalar_tensor_tensor(cm[:, i, :], raw[:, i, j:j + T], K["convw"][:, i, j:j + 1], cm[:, i, :],
                                                           ALU.mult, ALU.add).then_inc(S["conv_step"], 1)

                def norms(w, bank):
                    v.wait_ge(S["ss_ps"], b * 2 + w + 1)
                    nc.vector.tensor_scalar(nrm[:, w, :], ps[bank][:, 0:NT * H], 1e-6, None, ALU.add).then_inc(S["norm_eps"], 1)
                    v.wait_ge(S["norm_root"], b * 2 + w + 1)
                    nc.vector.reciprocal(inv[:, w, :], nrm[:, w, :]).then_inc(S["norm_inv"], 1)
                    v.wait_ge(S["norm_inv"], b * 2 + w + 1)

                conv(0)
                conv(1)
                norms(0, 2)
                nc.vector.tensor_tensor(gam[:, 1, :], inv[:, 0, :], inv[:, 0, :], ALU.mult).then_inc(S["gamma_sq"], 1)
                v.wait_ge(S["gamma_sq"], b + 1)
                nc.vector.tensor_tensor(gam[:, 0, :], gam[:, 1, :], beta[:], ALU.mult).then_inc(S["gamma_done"], 1)
                v.wait_ge(S["gamma_done"], b + 1)
                nc.vector.memset(St[:, 0, :, :], 0.0).then_inc(S["s_sb"], 1)
                for p in range(NT // 2):
                    v.wait_ge(S["gk_ps"], b * (NT // 2) + p + 1)
                    for t in (2 * p, 2 * p + 1):
                        for h in range(H):
                            nc.vector.scalar_tensor_tensor(A1T[:, t, h, :], g4(2 * (p % 2) + h % 2)[:, 2 * (t % 2) + h // 2, :],
                                                           gam[:, 0, t * H + h:t * H + h + 1], K["up_strict"][:], ALU.mult, ALU.mult)\
                                .then_inc(S["at_sb"], 1)
                conv(2)
                nc.vector.memset(XB, 0.0).then_inc(S["unit_set"], 1)
                v.wait_ge(S["unit_set"], b * 2 + 1)
                nc.vector.memset(gt_flat[:, BS * BS:2 * BS * BS:BS + 1], 1.0).then_inc(S["unit_set"], 1)
                v.wait_ge(S["blocks_loaded"], b * 16 + 16)
                v.wait_ge(S["unit_set"], b * 2 + 2)
                for n, r in enumerate(range(BS - 1, 0, -1)):
                    w = BS - r
                    pr = prod[:, 0:r * w].rearrange("p (j c) -> p j c", c=w)
                    if n:
                        v.wait_ge(S["subst"], b * 2 * (BS - 1) + 2 * n)
                    nc.vector.tensor_tensor(pr, AB[:, 0:r, r:r + 1].to_broadcast([P, r, w]), XB[:, r:r + 1, r:].to_broadcast([P, r, w]), ALU.mult)\
                        .then_inc(S["subst"], 1)
                    v.wait_ge(S["subst"], b * 2 * (BS - 1) + 2 * n + 1)
                    nc.vector.tensor_tensor(XB[:, 0:r, r:], XB[:, 0:r, r:], pr, ALU.subtract).then_inc(S["subst"], 1)
                norms(1, 6)

                def inverse(p, s):
                    for j in range(2):
                        v.wait_ge(S["p_ps"], b * CT + p * C + 2 * (s - 1) + j + 1)
                        nc.vector.tensor_tensor(Q[j][:], g4(j), over_heads(K["wmask"][:, s - 1, :]), ALU.mult).then_inc(S["q_sb"], 1)

                def scan(p, s):
                    t = 2 * p + s // 3
                    if s % 3 == 0:
                        v.wait_ge(S["ks_ps"], b * NT + t + 1)
                        v.wait_ge(S["vk_done"], b + 1)
                        for r in range(2):
                            nc.vector.tensor_tensor(by_head(R[:])[:, r::2, :], by_head(vk[:, t, :])[:, r::2, :], h4(6 + r)[:, 0:2, :],
                                                    ALU.subtract).then_inc(S["r_sb"], 1)
                    elif s % 3 == 1:
                        v.wait_ge(S["y_ps"], b * NT + t + 1)
                        nc.vector.tensor_tensor(z[:].rearrange("p (h n) -> p h n", h=H), h4(6), per_head(gam[:, 0, :], t, DH), ALU.mult)\
                            .then_inc(S["z_sb"], 1)
                    else:
                        v.wait_ge(S["ds_ps"], b * NT + t + 1)
                        nc.vector.tensor_tensor(St[:, (t + 1) % 2, :, :], St[:, t % 2, :, :], ps[7][:, 0:P].rearrange("p (i n) -> p i n", i=2),
                                                ALU.add).then_inc(S["s_sb"], 1)
                        v.wait_ge(S["o_ps"], b * NT + t + 1)
                        if t == 0:
                            v.wait_ge(S["h_stored"], b * 16 + 16)
                        for r in range(2):
                            nc.vector.tensor_tensor(by_head(dl[:, t, :])[:, r::2, :], h4(6 + r)[:, 0:2, :],
                                                    per_head(inv[:, 1, :], t, DH)[:, r::2, :], ALU.mult).then_inc(S["o_sb"], 1)

                for p in range(NT // 2 + 1):
                    for s in range(6):
                        if p < NT // 2 and s in (2, 4):
                            inverse(p, s // 2)
                        if p:
                            scan(p - 1, s)


def constants(nc, ctx, NB):
    shapes = {"ident": [P, P], "up_strict": [P, P], "up_incl": [P, P], "anti": [P, P], "bmask": [P, NBLK], "wmask": [P, LEVELS, P], "sel2": [P, 2],
              "hmask": [P, KD, AH], "vecs": [P, 12], "cbo": [P, D], "dWv": [P, KD, D], "cWqT": [P, KD, D], "Md": [P, KD, D],
              "drow": [P, KD], "OT": [P, KD, NB * NS], "kT": [P, KD, NB * NS], "vT": [P, KD, NB * NS], "ones": [P, P], "WcT": [P, KE, D], "Wq": [P, KD, D], "Wk": [P, KD, D], "Wv": [P, KD, D],
              "Wo": [P, KD, D], "W1x": [P, KD, D], "W1s": [NST, D], "W2": [P, KD, 4], "Wb": [P, KD, H], "convw": [P, 6, TAPS],
              "b1": [P, KD, 1], "rmsw": [P, 1], "lbias": [P, 4 * H], "itemp": [P, H], "itemp16": [P, 4 * H], "qsel": [P, NS], "halfsig": [P, H], "mask": [P, 3, NB * NT]}
    K = {n: ctx.enter_context(nc.sbuf_tensor("k_" + n, s, F32)) for n, s in shapes.items()}
    K["rows"] = ctx.enter_context(nc.sbuf_tensor("k_rows", [P, 3, NB * NT], U32))
    return K


def scratch(nc, NB, kind="Internal"):
    t = lambda n, shape: nc.dram_tensor("scr_" + n, shape, F32, kind=kind).ap()
    return {"fpad": [t(f"fpad{f}", (D, FPAD)) for f in range(2)],
            "h": t("h", (P, NB * NT, D)), "v": t("v", (P, NB * NT, D)), "delta": t("delta", (P, NB * NT, D)),
            "xw1": t("xw1", (P, NB * KD, T)), "fir": [t(f"fir{f}", (P, NB * NT, D)) for f in range(2)],
            "blocks": t("blocks", (P, BS * BS)), "inverses": t("inverses", (P, BS * BS)), "h2": t("h2", (P, NB * NT, D)), "xn2T": t("xn2T", (P, NB * KD, T))}


def filter_phase(nc, ctx, A, K, dram, ps):
    NB = A["x"].shape[0]
    CG = 8
    NG = DH // CG
    NL = 4
    NTT = NB * NT
    VT = NTT * DH // 512
    sem = lambda n: ctx.enter_context(nc.semaphore(n))
    v_loaded, zeroed, vr_ps, vr_sb = sem("vh_loaded"), sem("vh_zeroed"), sem("vrev_ps"), sem("vrev_sb")
    t_loaded = [[sem(f"toeplitz{f}{q}_loaded") for q in range(NL)] for f in range(2)]
    f_ps = [sem(f"fir{f}_ps") for f in range(2)]
    f_sb = [sem(f"fir{f}_sb") for f in range(2)]
    f_stored = [sem(f"fir{f}_stored") for f in range(2)]
    with ExitStack() as tmp, nc.Block() as block:
        sb = lambda n, shape, dt=F32: tmp.enter_context(nc.sbuf_tensor(n, shape, dt))
        V = sb("Vh", [P, NTT, DH])
        VR = [sb(f"Vrev{q}", [P, DH, NB, 1 + NT]) for q in range(2)]
        TB = [sb(f"TB{f}", [P, NL, CG, FW[f]]) for f in range(2)]
        F = [sb(f"F{f}", [P, NTT, DH]) for f in range(2)]

        @block.sync
        def _(sp):
            for hd in range(H):
                for g in range(NG):
                    n = hd * NG + g
                    for f in range(2):
                        if n >= NL:
                            sp.wait_ge(f_ps[f], n - NL + 1)
                        src = bass.AP(dram["fpad"][f].tensor, (hd * DH + g * CG) * FPAD, [[1, P], [FPAD, CG], [1, FW[f]]])
                        sp.dma_start(TB[f][:, n % NL, :, :], src).then_inc(t_loaded[f][n % NL], 16)

        @block.gpsimd
        def _(pool):
            def load_v(hd):
                if hd:
                    pool.wait_ge(vr_ps, hd * VT)
                pool.dma_start(V[:], dram["v"][:, :, hd * DH:(hd + 1) * DH]).then_inc(v_loaded, 16)

            load_v(0)
            for q in range(2):
                nc.gpsimd.memset(VR[q][:, :, :, 0], 0.0).then_inc(zeroed, 1)
            load_v(1)
            for hd in range(H):
                for f in range(2):
                    pool.wait_ge(f_sb[f], (hd + 1) * NG)
                    pool.dma_start(dram["fir"][f][:, :, hd * DH:(hd + 1) * DH], F[f][:]).then_inc(f_stored[f], 16)
                if hd + 2 < H:
                    load_v(hd + 2)
            for f in range(2):
                pool.wait_ge(f_stored[f], 16 * H)

        @block.tensor
        def _(pe):
            def turn(hd):
                pe.wait_ge(v_loaded, 16 * (hd + 1))
                v2 = V[:].rearrange("p n c -> p (n c)")
                for i in range(VT):
                    n = hd * VT + i
                    if n >= 2:
                        pe.wait_ge(vr_sb, n - 1)
                    nc.tensor.matmul(ps[6 + n % 2][:], K["anti"][:], v2[:, i * 512:(i + 1) * 512], start=True, stop=True).then_inc(vr_ps, 1)

            pe.wait_ge(zeroed, 2)
            turn(0)
            for hd in range(H):
                pe.wait_ge(vr_sb, (hd + 1) * VT)
                for g in range(NG):
                    n = hd * NG + g
                    for f in range(2):
                        bank = 3 * f + n % 3
                        pe.wait_ge(t_loaded[f][n % NL], 16 * (n // NL + 1))
                        if n >= 3:
                            pe.wait_ge(f_sb[f], n - 2)
                        for c in range(CG):
                            cols = slice(c * NTT, (c + 1) * NTT)
                            v3 = VR[hd % 2][:, g * CG + c, :, :]
                            nc.tensor.matmul(ps[bank][:, cols], TB[f][:, n % NL, c, 0:P], v3[:, :, 1:], start=True, stop=False,
                                             skip_group_check=True)
                            last = nc.tensor.matmul(ps[bank][0:FW[f] - P, cols], TB[f][:, n % NL, c, P:FW[f]], v3[:, :, 0:NT],
                                                    start=False, stop=True, skip_group_check=True)
                        last.then_inc(f_ps[f], 1)
                    if g == NG // 2 and hd + 1 < H:
                        turn(hd + 1)

        def turned(hd, i):
            n = hd * VT + i
            return VR[hd % 2][:, :, i, 1:], ps[6 + n % 2][:].rearrange("p (t c) -> p c t", c=DH)

        def evacuate(eng, f, copy):
            def turns(hd):
                for i in range(VT):
                    if i % 2 == f:
                        eng.wait_ge(vr_ps, hd * VT + i + 1)
                        o, s = turned(hd, i)
                        if hd * VT + i:
                            eng.wait_ge(vr_sb, hd * VT + i)
                        copy(o, s).then_inc(vr_sb, 1)

            turns(0)
            for hd in range(H):
                if hd:
                    eng.wait_ge(f_stored[f], 16 * hd)
                for g in range(NG):
                    n = hd * NG + g
                    eng.wait_ge(f_ps[f], n + 1)
                    copy(F[f][:, :, g * CG:(g + 1) * CG].rearrange("p n c -> p c n"),
                         ps[3 * f + n % 3][:, 0:CG * NTT].rearrange("p (c n) -> p c n", c=CG)).then_inc(f_sb[f], 1)
                    if g == NG // 2 and hd + 1 < H:
                        turns(hd + 1)

        @block.scalar
        def _(act):
            evacuate(act, 0, lambda o, i: nc.scalar.activation(o, i, ACT.Copy))

        @block.vector
        def _(v):
            evacuate(v, 1, lambda o, i: nc.vector.tensor_copy(o, i))


def slot_setup(nc, ctx, A, K, dram, ps):
    sem = lambda n: ctx.enter_context(nc.semaphore(n))
    ld, pe_c, vst, act_c = sem("slot_loaded"), sem("slot_pe_group"), sem("slot_vector_step"), sem("slot_scalar_step")
    VECS = ("d_bq", "d_bk", "d_bv", "c_bq", "c_bk", "c_bv")
    with ExitStack() as tmp, nc.Block() as block:
        sb = lambda n, shape, dt=F32: tmp.enter_context(nc.sbuf_tensor(n, shape, dt))
        vrow = sb("vrow", [2 * len(VECS), P])
        slot = sb("slot", [NS, D])
        slotT = sb("slotT", [P, KD, NS])
        wqs = sb("wqs", [P, KD, D])
        wks = sb("wks", [P, KD, D])
        wkT = sb("wkT", [P, KD, D])
        qT = sb("qT", [P, KD, NS])
        qblk = sb("qblk", [P, KD, AH, NS])
        cwq = sb("cwq", [P, KD, D])

        @block.sync
        def _(sp):
            for i, n in enumerate(VECS):
                sp.dma_start(vrow[2 * i:2 * i + 2, :], A["L0_ffn_" + n].rearrange("(k p) -> k p", p=P)).then_inc(ld, 16)
            sp.dma_start(slot[:], A["L0_ffn_slot_query"][0]).then_inc(ld, 16)
            for t, n in ((wqs, "d_Wq"), (wks, "d_Wk"), (cwq, "c_Wq"), (K["dWv"], "d_Wv")):
                sp.dma_start(t[:], A["L0_ffn_" + n].rearrange("(k p) n -> p k n", p=P)).then_inc(ld, 16)
            sp.dma_start(K["cbo"][:], bass.AP(A["L0_ffn_c_bo"].tensor, 0, [[0, P], [1, D]])).then_inc(ld, 16)
            sp.wait_ge(ld, 16 * (len(VECS) + 6))

        @block.tensor
        def _(pe):
            ident = K["ident"]
            pe.wait_ge(ld, 16 * (len(VECS) + 6))
            nc.tensor.transpose(ps[0][:, 0:12], vrow[:], ident[0:12, 0:12]).then_inc(pe_c, 1)
            for k in range(KD):
                last = nc.tensor.transpose(ps[1][:, k * NS:(k + 1) * NS], slot[:, k * P:(k + 1) * P], ident[0:NS, 0:NS])
            last.then_inc(pe_c, 1)
            for w, src in ((2, wks), (3, cwq)):
                for c in range(KD):
                    for k in range(KD):
                        last = nc.tensor.transpose(ps[w][:, c * D + k * P:c * D + (k + 1) * P], src[:, k, c * P:(c + 1) * P], ident[:])
            last.then_inc(pe_c, 1)
            pe.wait_ge(vst, 4)
            for c in range(KD):
                for k in range(KD):
                    last = nc.tensor.matmul(ps[4][:, c * NS:(c + 1) * NS], wqs[:, k, c * P:(c + 1) * P], slotT[:, k, :], start=(k == 0), stop=(k == KD - 1))
            last.then_inc(pe_c, 1)
            pe.wait_ge(vst, 8)
            for c in range(KD):
                for k in range(KD):
                    last = nc.tensor.matmul(ps[5][:, c * D:(c + 1) * D], wkT[:, k, c * P:(c + 1) * P], qblk[:, k, :, :].rearrange("p h q -> p (h q)"),
                                            start=(k == 0), stop=(k == KD - 1))
            for m in range(KD):
                for k in range(KD):
                    last = nc.tensor.matmul(ps[6][:, m:m + 1], qblk[:, k, :, :].rearrange("p h q -> p (h q)")[:, m * P:(m + 1) * P],
                                            K["vecs"][:, 2 + k:3 + k], start=(k == 0), stop=(k == KD - 1))
            last.then_inc(pe_c, 1)

        @block.vector
        def _(v):
            n = [0]

            def step(ins, fence=True):
                ins.then_inc(vst, 1)
                n[0] += 1
                if fence:
                    v.wait_ge(vst, n[0])

            v.wait_ge(pe_c, 3)
            step(nc.vector.tensor_copy(K["vecs"][:], ps[0][:, 0:12]))
            step(nc.vector.tensor_copy(slotT[:], ps[1][:, 0:KD * NS].rearrange("p (k n) -> p k n", k=KD)))
            step(nc.vector.tensor_copy(wkT[:], ps[2][:].rearrange("p (k n) -> p k n", k=KD)))
            step(nc.vector.tensor_copy(K["cWqT"][:], ps[3][:].rearrange("p (k n) -> p k n", k=KD)))
            v.wait_ge(pe_c, 4)
            for c in range(KD):
                step(nc.vector.tensor_scalar(qT[:, c, :], ps[4][:, c * NS:(c + 1) * NS], K["vecs"][:, c:c + 1], None, ALU.add))
            for c in range(KD):
                step(nc.vector.tensor_tensor(qblk[:, c, :, :], qT[:, c, :].unsqueeze(1).to_broadcast([P, AH, NS]),
                                             K["hmask"][:, c, :].unsqueeze(2).to_broadcast([P, AH, NS]), ALU.mult))
            v.wait_ge(pe_c, 5)
            step(nc.vector.tensor_copy(K["Md"][:], ps[5][:].rearrange("p (k n) -> p k n", k=KD)))
            step(nc.vector.tensor_scalar(K["drow"][:], ps[6][:, 0:KD], 0.25, None, ALU.mult))


def gate_phase(nc, ctx, A, K, dram, ps):
    NB = A["x"].shape[0]
    names = ["ln_go", "src0_loaded", "src1_loaded", "xw1_loaded", "h_loaded", "square", "red", "st_step", "st_root", "pad", "w_split", "w8_loaded", "st_ps", "st_sb", "pre_ps", "pre_sb",
             "gelu", "lg_ps", "sm", "sm_exp", "pool_mix", "mix", "osq", "rms", "rms_root", "on", "ot_ps", "ot_sb", "h2_ps", "h2_sb",
             "ln_stats", "ln_aggr", "ln_eps", "ln_std", "ln_rstd", "xn_done", "h2b", "h2_stored", "xt_ps", "xt_sb", "xt_stored",
             "sc_ps", "sc_max", "sc_exp", "sum_inv", "sq_sum", "floor", "et_ps", "et_sb", "ctx_ps", "ctx_sb", "ctxT_ps", "ctxT_sb", "z_ps", "z_sb", "o_ps", "o_sb"]
    S = {n: nc.alloc_semaphore(name="g_" + n) for n in names}
    N2 = NT * H
    with ExitStack() as tmp, nc.Block() as block:
        sb = lambda n, shape, dt=F32: tmp.enter_context(nc.sbuf_tensor("g_" + n, shape, dt))
        srcs = [sb(f"src{q}", [P, 4, NT, D]) for q in range(2)]
        sqr = sb("sqr", [P, NT, D])
        xw1 = sb("xw1", [P, KD, T])
        h_tm = sb("h", [P, NT, D])
        red = sb("red", [P, 4, 3, N2])
        tiny = sb("tiny", [P, 4, 3, N2])
        st = sb("st", [P, N2, NST])
        st8 = sb("st8", [P, N2, 8, NST], BF16)
        stT = sb("stT", [P, H, T], BF16)
        w8 = sb("w8", [P, D], BF16)
        w3 = sb("w3", [NST, 3, D], BF16)
        wr = sb("wr", [NST, D])
        identb = sb("identb", [P, P], BF16)
        h1 = sb("h1", [P, KD, H, T])
        lg = sb("lg", [P, N2, 4])
        pr = sb("pr", [P, N2, 4])
        sm = sb("sm", [P, 6, N2])
        oT = sb("oT", [P, KD, T])
        stats = sb("stats", [P, NT, 6])
        mv = sb("mv", [P, NT, 2])
        rstd = sb("rstd", [P, 3, NT])
        xn = sb("xn", [P, NT, D])
        xnT = sb("xnT", [P, KD, T])
        ex = oT
        eT = sqr
        at = sb("at", [P, 8, KD])
        cx = sb("cx", [P, KD, D])
        cxT = sb("cxT", [P, KD, D])
        zm = sb("zm", [P, KD, D])

        flat = lambda a: a.rearrange("p t (h n) -> p (t h) n", h=H)
        bank2 = lambda b0: K["psum"][:, b0:b0 + 2, :].rearrange("p k n -> p (k n)")
        mixw = lambda i: pr[:, :, i:i + 1].to_broadcast([P, N2, DH])
        MIX, LONG, DELTA, VAL = 0, 1, 2, 3

        def over_sequences(eng, body):
            if NB > 2:
                with eng.Fori(0, NB // 2 - 1) as c:
                    body(c * 2, 0, True, True)
                    body(c * 2 + 1, 1, True, True)
            body(NB - 2, 0, True, False)
            body(NB - 1, 1, False, False)

        @block.sync
        def _(sp):
            def load_src(b, q):
                for i, n in enumerate((dram["fir"][0], dram["fir"][1], dram["delta"], dram["v"])):
                    sp.dma_start(srcs[q][:, i, :, :], n[:, bass.ds(b * NT, NT), :]).then_inc(S[f"src{q}_loaded"], 16)

            def load_xw1(b):
                sp.dma_start(xw1[:], dram["xw1"][:, bass.ds(b * KD, KD), :]).then_inc(S["xw1_loaded"], 16)

            def load_h(b):
                sp.dma_start(h_tm[:], dram["h"][:, bass.ds(b * NT, NT), :]).then_inc(S["h_loaded"], 16)

            def body(b, q, more, far):
                if more:
                    sp.wait_ge(S["pre_sb"], b * 4 + 4)
                    load_xw1(b + 1)
                if far:
                    sp.wait_ge(S["ot_ps"], b * 4 + 4)
                    load_src(b + 2, q)
                sp.wait_ge(S["xt_sb"], b * 4 + 4)
                sp.dma_start(dram["xn2T"][:, bass.ds(b * KD, KD), :], xnT[:]).then_inc(S["xt_stored"], 16)
                sp.wait_ge(S["h2b"], b + 1)
                sp.dma_start(dram["h2"][:, bass.ds(b * NT, NT), :], h_tm[:]).then_inc(S["h2_stored"], 16)
                if more:
                    sp.wait_ge(S["h2_stored"], b * 16 + 16)
                    load_h(b + 1)

            load_src(0, 0)
            sp.wait_ge(S["w_split"], 5)
            for r, part in enumerate((0, 1, 2, 0, 1, 2, 0, 1)):
                sp.dma_start(w8[r * NST:(r + 1) * NST, :], w3[:, part, :]).then_inc(S["w8_loaded"], 16)
            load_xw1(0)
            load_h(0)
            load_src(1, 1)
            over_sequences(sp, body)
            sp.wait_ge(S["xt_stored"], 16 * NB)
            sp.wait_ge(S["h2_stored"], 16 * NB)

        @block.gpsimd
        def _(pool):
            def body(b, q, more, far):
                src = srcs[q]
                pool.wait_ge(S["sm"], b * 11 + 11)
                f = flat(src[:, VAL, :, :])
                nc.gpsimd.tensor_tensor(f, f, mixw(3), ALU.mult).then_inc(S["pool_mix"], 1)
                pool.wait_ge(S["xn_done"], b * NT + NT)
                nc.gpsimd.tensor_tensor(h_tm[:], h_tm[:], K["cbo"][:].unsqueeze(1).to_broadcast([P, NT, D]), ALU.add).then_inc(S["h2b"], 1)

            over_sequences(pool, body)

        @block.tensor
        def _(pe):
            ident = K["ident"][:]
            def hidden(b, later):
                pe.wait_ge(S["st_step"], b * 9 + 9)
                for c in range(2):
                    if later and c:
                        pe.wait_ge(S["h2_sb"], b * 4)
                    for h in range(H):
                        for q in range(4):
                            last = nc.tensor.matmul(ps[4 * c + h][:, q * P:(q + 1) * P],
                                                    st8[:, (4 * c + q) * H + h].rearrange("p r j -> p (r j)"), identb[:], start=True, stop=True)
                    last.then_inc(S["st_ps"], 1)
                for n in range(4):
                    m, c = n // 2, n % 2
                    if n < 2:
                        pe.wait_ge(S["st_sb"], b * 2 + n + 1)
                    else:
                        pe.wait_ge(S["pre_sb"], b * 4 + n - 1)
                    for h in range(H):
                        last = nc.tensor.matmul(ps[4 * c + h][:], w8[:, m * P:(m + 1) * P], stT[:, h, c * 512:(c + 1) * 512], start=True, stop=True)
                    last.then_inc(S["pre_ps"], 1)

            def logits(b):
                pe.wait_ge(S["pre_sb"], b * 4 + 4)
                pe.wait_ge(S["gelu"], b * 4 + 4)
                for t in range(NT):
                    for h in range(H):
                        for m in range(KD):
                            last = nc.tensor.matmul(ps[3][:, (t * H + h) * 4:(t * H + h + 1) * 4], h1[:, m, h, t * P:(t + 1) * P], K["W2"][:, m, :],
                                                    start=(m == 0), stop=(m == KD - 1))
                last.then_inc(S["lg_ps"], 1)

            def body(b, q, more, far):
                src = srcs[q]
                pe.wait_ge(S["on"], b + 1)
                for n in range(4):
                    half, k = n // 2, n % 2
                    for g in range(4):
                        last = nc.tensor.transpose(ps[n][:, g * P:(g + 1) * P], src[:, MIX, 4 * half + g, k * P:(k + 1) * P], ident)
                    last.then_inc(S["ot_ps"], 1)
                for n in range(4):
                    pe.wait_ge(S["ot_sb"], b * 4 + (2 if n < 2 else 4))
                    for q in range(2):
                        t = 2 * n + q
                        for k in range(KD):
                            last = nc.tensor.matmul(ps[4 + n][:, q * D:(q + 1) * D], oT[:, k, t * P:(t + 1) * P], K["Wo"][:, k, :],
                                                    start=(k == 0), stop=(k == KD - 1))
                    last.then_inc(S["h2_ps"], 1)
                if more:
                    hidden(b + 1, True)
                    pe.wait_ge(S["pre_sb"], b * 4 + 8)
                for n in range(4):
                    half, k = n // 2, n % 2
                    pe.wait_ge(S["xn_done"], b * NT + 4 * half + 4)
                    for q in range(4):
                        last = nc.tensor.transpose(ps[n][:, q * P:(q + 1) * P], xn[:, 4 * half + q, k * P:(k + 1) * P], ident)
                    last.then_inc(S["xt_ps"], 1)
                pe.wait_ge(S["xt_sb"], b * 4 + 4)
                for m in range(KD):
                    for c in range(2):
                        for k in range(KD):
                            last = nc.tensor.matmul(ps[4 + 2 * m + c][:], K["Md"][:, k, m * P:(m + 1) * P], xnT[:, k, c * 512:(c + 1) * 512],
                                                    start=(k == 0), stop=(k == KD - 1))
                    last.then_inc(S["sc_ps"], 1)
                if more:
                    logits(b + 1)
                pe.wait_ge(S["sc_exp"], b * KD + KD)
                for n in range(4):
                    if n == 3:
                        pe.wait_ge(S["et_sb"], b * 4 + 1)
                    for q in range(4):
                        t, m = 2 * n + q // 2, q % 2
                        last = nc.tensor.transpose(ps[n % 3][:, q * P:(q + 1) * P], ex[:, m, t * P:(t + 1) * P], ident)
                    last.then_inc(S["et_ps"], 1)
                pe.wait_ge(S["et_sb"], b * 4 + 4)
                for m in range(KD):
                    for t in range(NT):
                        last = nc.tensor.matmul(ps[4 + m][:, 0:D], eT[:, t, m * P:(m + 1) * P], xn[:, t, :], start=(t == 0), stop=(t == NT - 1))
                    last.then_inc(S["ctx_ps"], 1)
                pe.wait_ge(S["ctx_sb"], b * KD + KD)
                for k in range(KD):
                    for m in range(KD):
                        last = nc.tensor.transpose(ps[6][:, k * D + m * P:k * D + (m + 1) * P], cx[:, m, k * P:(k + 1) * P], ident)
                last.then_inc(S["ctxT_ps"], 1)
                pe.wait_ge(S["ctxT_sb"], b + 1)
                for m in range(KD):
                    for k in range(KD):
                        last = nc.tensor.matmul(ps[7][:, m * D:(m + 1) * D], cxT[:, k, m * P:(m + 1) * P], K["dWv"][:, k, :],
                                                start=(k == 0), stop=(k == KD - 1))
                last.then_inc(S["z_ps"], 1)
                pe.wait_ge(S["z_sb"], b * KD + KD)
                for c in range(KD):
                    for m in range(KD):
                        last = nc.tensor.matmul(ps[4][:, c * NS:(c + 1) * NS], zm[:, m, c * P:(c + 1) * P], K["qsel"][:], start=(m == 0), stop=(m == KD - 1))
                last.then_inc(S["o_ps"], 1)
                pe.wait_ge(S["o_sb"], b * KD + KD)

            pe.wait_ge(S["w8_loaded"], 16 * 8)
            pe.wait_ge(S["pad"], 1)
            hidden(0, False)
            logits(0)
            over_sequences(pe, body)

        @block.scalar
        def _(act):
            copy = lambda o, i: nc.scalar.activation(o, i, ACT.Copy)
            def squares(b, q, later):
                act.wait_ge(S[f"src{q}_loaded"], b * 32 + (64 - 32 * q))
                for i in range(4):
                    if i:
                        act.wait_ge(S["red"], b * 12 + 3 * i)
                    elif later:
                        act.wait_ge(S["sq_sum"], b - 1)
                    nc.scalar.activation(sqr[:], srcs[q][:, i, :, :], ACT.Square).then_inc(S["square"], 1)
                act.wait_ge(S["red"], b * 12 + 12)
                nc.scalar.activation(st[:, :, 3:NST:4].rearrange("p n s -> p s n"), red[:, :, 2, :], ACT.Sqrt).then_inc(S["st_root"], 1)

            def turned(b):
                for n in range(2):
                    act.wait_ge(S["st_ps"], b * 2 + n + 1)
                    copy(stT[:, :, n * 512:(n + 1) * 512], K["psum"][:, 4 * n:4 * n + 4, :]).then_inc(S["st_sb"], 1)

            def gelus(b):
                for n in range(4):
                    m, c = n // 2, n % 2
                    act.wait_ge(S["pre_sb"], b * 4 + n + 1)
                    g = h1[:, m, :, c * 512:(c + 1) * 512]
                    nc.scalar.activation(g, g, ACT.Gelu, bias=K["b1"][:, m, :]).then_inc(S["gelu"], 1)

            def exps(b):
                act.wait_ge(S["sm"], b * 11 + 4)
                nc.scalar.activation(pr[:], lg[:], ACT.Exp).then_inc(S["sm_exp"], 1)

            def body(b, q, more, far):
                act.wait_ge(S["mix"], b * 6 + 6)
                nc.scalar.activation(sqr[:], srcs[q][:, MIX, :, :], ACT.Square).then_inc(S["osq"], 1)
                act.wait_ge(S["rms"], b * 2 + 1)
                nc.scalar.activation(sm[:, 4, :], sm[:, 3, :], ACT.Sqrt).then_inc(S["rms_root"], 1)
                for n in range(4):
                    act.wait_ge(S["ot_ps"], b * 4 + n + 1)
                    copy(oT[:, n % 2, n // 2 * 512:(n // 2 + 1) * 512], ps[n][:]).then_inc(S["ot_sb"], 1)
                if more:
                    turned(b + 1)
                act.wait_ge(S["ln_eps"], b + 1)
                nc.scalar.activation(rstd[:, 1, :], rstd[:, 0, :], ACT.Sqrt).then_inc(S["ln_std"], 1)
                if more:
                    gelus(b + 1)
                for n in range(4):
                    act.wait_ge(S["xt_ps"], b * 4 + n + 1)
                    copy(xnT[:, n % 2, n // 2 * 512:(n // 2 + 1) * 512], ps[n][:]).then_inc(S["xt_sb"], 1)
                for m in range(KD):
                    act.wait_ge(S["sc_max"], b * 6 + 3 * m + 3)
                    nc.scalar.activation(ex[:, m, :], bank2(4 + 2 * m), ACT.Exp, bias=at[:, 2, m:m + 1], scale=0.25, accum_out=at[:, 3, m:m + 1])\
                        .then_inc(S["sc_exp"], 1)
                if far:
                    squares(b + 2, q, True)
                for n in range(4):
                    act.wait_ge(S["et_ps"], b * 4 + n + 1)
                    copy(eT[:, 2 * n:2 * n + 2, :], ps[n % 3][:].rearrange("p (t n) -> p t n", t=2)).then_inc(S["et_sb"], 1)
                if more:
                    exps(b + 1)
                act.wait_ge(S["ctxT_ps"], b + 1)
                copy(cxT[:], ps[6][:].rearrange("p (k n) -> p k n", k=KD)).then_inc(S["ctxT_sb"], 1)
                act.wait_ge(S["o_ps"], b + 1)
                for c in range(KD):
                    nc.scalar.activation(K["OT"][:, c, bass.ds(b * NS, NS)], ps[4][:, c * NS:(c + 1) * NS], ACT.Identity,
                                         bias=K["vecs"][:, 4 + c:5 + c]).then_inc(S["o_sb"], 1)
                act.wait_ge(S["xt_stored"], b * 16 + 16)

            squares(0, 0, False)
            turned(0)
            gelus(0)
            squares(1, 1, False)
            exps(0)
            over_sequences(act, body)

        @block.vector
        def _(v):
            nc.vector.tensor_copy(identb[:], K["ident"][:]).then_inc(S["pad"], 1)
            for i in range(3):
                nc.vector.tensor_copy(w3[:, i, :], wr[:] if i else K["W1s"][:]).then_inc(S["w_split"], 1)
                if i < 2:
                    v.wait_ge(S["w_split"], 2 * i + 1)
                    nc.vector.tensor_tensor(wr[:], wr[:] if i else K["W1s"][:], w3[:, i, :], ALU.subtract).then_inc(S["w_split"], 1)
                    v.wait_ge(S["w_split"], 2 * i + 2)
            def statistics(b, q):
                src = srcs[q]
                v.wait_ge(S[f"src{q}_loaded"], b * 32 + (64 - 32 * q))
                for i in range(4):
                    f = flat(src[:, i, :, :])
                    nc.vector.tensor_reduce(red[:, i, 0, :], f, AX.X, ALU.add).then_inc(S["red"], 1)
                    nc.vector.tensor_reduce(red[:, i, 1, :], f, AX.X, ALU.add, apply_absolute_value=True).then_inc(S["red"], 1)
                    v.wait_ge(S["square"], b * 4 + i + 1)
                    nc.vector.tensor_reduce(red[:, i, 2, :], flat(sqr[:]), AX.X, ALU.add).then_inc(S["red"], 1)
                v.wait_ge(S["red"], b * 12 + 12)
                col = lambda j: st[:, :, j:NST:4].rearrange("p n s -> p s n")
                nc.vector.tensor_scalar(col(0), red[:, :, 0, :], 1.0 / DH, None, ALU.mult).then_inc(S["st_step"], 1)
                nc.vector.tensor_scalar(col(2), red[:, :, 1, :], 1.0 / DH, None, ALU.mult).then_inc(S["st_step"], 1)
                v.wait_ge(S["st_step"], b * 9 + 1)
                nc.vector.tensor_tensor(tiny[:, :, 0, :], col(0), col(0), ALU.mult).then_inc(S["st_step"], 1)
                v.wait_ge(S["st_step"], b * 9 + 3)
                nc.vector.scalar_tensor_tensor(col(1), red[:, :, 2, :], 1.0 / DH, tiny[:, :, 0, :], ALU.mult, ALU.subtract)\
                    .then_inc(S["st_step"], 1)
                v.wait_ge(S["st_step"], b * 9 + 4)
                v.wait_ge(S["st_root"], b + 1)
                for i, (at_, rows) in enumerate(((0, 3), (3, 3), (6, 2))):
                    nc.vector.tensor_copy(st8[:, :, at_:at_ + rows, :], st[:].unsqueeze(2).to_broadcast([P, N2, rows, NST])).then_inc(S["st_step"], 1)
                    if i < 2:
                        v.wait_ge(S["st_step"], b * 9 + 5 + 2 * i)
                        nc.vector.tensor_tensor(st[:], st[:], st8[:, :, at_, :], ALU.subtract).then_inc(S["st_step"], 1)
                        v.wait_ge(S["st_step"], b * 9 + 6 + 2 * i)

            def hidden(b):
                v.wait_ge(S["xw1_loaded"], b * 16 + 16)
                for n in range(4):
                    m, c = n // 2, n % 2
                    v.wait_ge(S["pre_ps"], b * 4 + n + 1)
                    bk = 4 * c
                    nc.vector.tensor_tensor(h1[:, m, :, c * 512:(c + 1) * 512], K["psum"][:, bk:bk + 4, :],
                                            xw1[:, m, c * 512:(c + 1) * 512].unsqueeze(1).to_broadcast([P, H, 512]), ALU.add).then_inc(S["pre_sb"], 1)

            def softmax(b):
                k = [0]

                def step(ins):
                    ins.then_inc(S["sm"], 1)
                    k[0] += 1
                    v.wait_ge(S["sm"], b * 11 + k[0])

                last4 = lambda a: a.unsqueeze(2).to_broadcast([P, N2, 4])
                by_t = lambda a: a.rearrange("p (t h) j -> p t (h j)", h=H)
                v.wait_ge(S["lg_ps"], b + 1)
                step(nc.vector.tensor_tensor(by_t(lg[:]), ps[3][:, 0:4 * N2].rearrange("p (t n) -> p t n", t=NT),
                                             K["lbias"][:].unsqueeze(1).to_broadcast([P, NT, 16]), ALU.add))
                step(nc.vector.tensor_tensor(by_t(lg[:]), by_t(lg[:]), K["itemp16"][:].unsqueeze(1).to_broadcast([P, NT, 16]), ALU.mult))
                step(nc.vector.tensor_reduce(sm[:, 0, :], lg[:], AX.X, ALU.max))
                step(nc.vector.tensor_tensor(lg[:], lg[:], last4(sm[:, 0, :]), ALU.subtract))
                v.wait_ge(S["sm_exp"], b + 1)
                step(nc.vector.tensor_reduce(sm[:, 1, :], pr[:], AX.X, ALU.add))
                step(nc.vector.reciprocal(sm[:, 2, :], sm[:, 1, :]))
                step(nc.vector.tensor_tensor(lg[:], pr[:], last4(sm[:, 2, :]), ALU.mult))
                nc.vector.tensor_scalar(pr[:, :, 0:2], lg[:, :, 0:2], 0.05, None, ALU.max).then_inc(S["floor"], 1)
                nc.vector.tensor_scalar(pr[:, :, 2:4], lg[:, :, 2:4], 0.0, None, ALU.max).then_inc(S["floor"], 1)
                v.wait_ge(S["floor"], b * 2 + 2)
                step(nc.vector.tensor_reduce(sm[:, 1, :], pr[:], AX.X, ALU.add))
                step(nc.vector.reciprocal(sm[:, 2, :], sm[:, 1, :]))
                step(nc.vector.tensor_tensor(pr[:], pr[:], last4(sm[:, 2, :]), ALU.mult))
                p0 = pr[:, :, 0].rearrange("p (t h) -> p t h", h=H)
                step(nc.vector.tensor_tensor(p0, p0, K["halfsig"][:].unsqueeze(1).to_broadcast([P, NT, H]), ALU.add))
                assert k[0] == 11

            def body(b, q, more, far):
                src = srcs[q]
                f = flat(src[:, MIX, :, :])
                for n, i in enumerate((MIX, LONG, DELTA)):
                    w = flat(src[:, i, :, :])
                    nc.vector.tensor_tensor(w, w, mixw(i), ALU.mult).then_inc(S["mix"], 1)
                for n, i in enumerate((LONG, DELTA, VAL)):
                    v.wait_ge(S["mix"], b * 6 + 3 + n)
                    if i == VAL:
                        v.wait_ge(S["pool_mix"], b + 1)
                    nc.vector.tensor_tensor(f, f, flat(src[:, i, :, :]), ALU.add).then_inc(S["mix"], 1)
                v.wait_ge(S["osq"], b + 1)
                nc.vector.tensor_reduce(sm[:, 5, :], flat(sqr[:]), AX.X, ALU.add).then_inc(S["sq_sum"], 1)
                v.wait_ge(S["sq_sum"], b + 1)
                nc.vector.tensor_scalar(sm[:, 3, :], sm[:, 5, :], 1.0 / DH, 1e-5, ALU.mult, ALU.add).then_inc(S["rms"], 1)
                v.wait_ge(S["rms_root"], b + 1)
                nc.vector.reciprocal(sm[:, 5, :], sm[:, 4, :]).then_inc(S["rms"], 1)
                v.wait_ge(S["rms"], b * 2 + 2)
                nc.vector.tensor_tensor(f, f, sm[:, 5, :].unsqueeze(2).to_broadcast([P, N2, DH]), ALU.mult).then_inc(S["on"], 1)
                v.wait_ge(S["h_loaded"], b * 16 + 16)
                for n in range(4):
                    v.wait_ge(S["h2_ps"], b * 4 + n + 1)
                    t2 = h_tm[:, 2 * n:2 * n + 2, :]
                    nc.vector.tensor_tensor(t2, ps[4 + n][:].rearrange("p (t n) -> p t n", t=2), t2, ALU.add).then_inc(S["h2_sb"], 1)
                for t in range(NT):
                    v.wait_ge(S["h2_sb"], b * 4 + t // 2 + 1)
                    nc.vector.bn_stats(stats[:, t, :], h_tm[:, t, :]).then_inc(S["ln_stats"], 1)
                v.wait_ge(S["ln_stats"], b * NT + NT).then_inc(S["ln_go"], 1)
                for t in range(NT):
                    nc.vector.bn_aggr(mv[:, t, :], stats[:, t, :]).then_inc(S["ln_aggr"], 1)
                v.wait_ge(S["ln_aggr"], b * NT + NT)
                nc.vector.tensor_scalar(rstd[:, 0, :], mv[:, :, 1], 1e-5, None, ALU.add).then_inc(S["ln_eps"], 1)
                v.wait_ge(S["ln_std"], b + 1)
                nc.vector.reciprocal(rstd[:, 2, :], rstd[:, 1, :]).then_inc(S["ln_rstd"], 1)
                v.wait_ge(S["ln_rstd"], b + 1)
                for t in range(NT):
                    nc.vector.tensor_scalar(xn[:, t, :], h_tm[:, t, :], mv[:, t, 0:1], rstd[:, 2, t:t + 1], ALU.subtract, ALU.mult)\
                        .then_inc(S["xn_done"], 1)
                if more:
                    hidden(b + 1)
                for m in range(KD):
                    v.wait_ge(S["sc_ps"], b * KD + m + 1)
                    nc.vector.tensor_reduce(at[:, 0, m:m + 1], bank2(4 + 2 * m), AX.X, ALU.max).then_inc(S["sc_max"], 1)
                    v.wait_ge(S["sc_max"], b * 6 + 3 * m + 1)
                    nc.vector.scalar_tensor_tensor(at[:, 1, m:m + 1], at[:, 0, m:m + 1], 0.25, K["drow"][:, m:m + 1], ALU.mult, ALU.add)\
                        .then_inc(S["sc_max"], 1)
                    v.wait_ge(S["sc_max"], b * 6 + 3 * m + 2)
                    nc.vector.tensor_tensor(at[:, 2, m:m + 1], K["drow"][:, m:m + 1], at[:, 1, m:m + 1], ALU.subtract).then_inc(S["sc_max"], 1)
                if far:
                    statistics(b + 2, q)
                if more:
                    softmax(b + 1)
                v.wait_ge(S["sc_exp"], b * KD + KD)
                nc.vector.reciprocal(at[:, 4, :], at[:, 3, :]).then_inc(S["sum_inv"], 1)
                v.wait_ge(S["sum_inv"], b + 1)
                for m in range(KD):
                    v.wait_ge(S["ctx_ps"], b * KD + m + 1)
                    nc.vector.tensor_scalar(cx[:, m, :], ps[4 + m][:, 0:D], at[:, 4, m:m + 1], None, ALU.mult).then_inc(S["ctx_sb"], 1)
                v.wait_ge(S["z_ps"], b + 1)
                for m in range(KD):
                    nc.vector.tensor_tensor(zm[:, m, :].rearrange("p (g n) -> p g n", g=AH), ps[7][:, m * D:(m + 1) * D].rearrange("p (g n) -> p g n", g=AH),
                                            K["hmask"][:, m, :].unsqueeze(2).to_broadcast([P, AH, AD]), ALU.mult).then_inc(S["z_sb"], 1)

            statistics(0, 0)
            hidden(0)
            statistics(1, 1)
            softmax(0)
            over_sequences(v, body)

    nc.clear_and_free_semaphores(list(S.values()))
    nc.all_engine_barrier()


def expert_phase(nc, ctx, A, K, dram, ps):
    sem = lambda n: ctx.enter_context(nc.semaphore("e_" + n))
    NB = A["x"].shape[0]
    NR = NB * NS
    NF = FF // P
    NW = 3
    NE = NS
    ld, vst, pe_c, root, bias_sb = sem("loaded"), sem("vector_step"), sem("pe_group"), sem("root"), sem("bias_step")
    w_loaded = [sem(f"w{q}_loaded") for q in range(NW)]
    u_ps, u_pre, u_act, ug_sb, y_ps, o2_sb, kv_ps, kv_sb = (sem(n) for n in ("u_ps", "u_pre", "u_act", "ug_sb", "y_ps", "o2_sb", "kv_ps", "kv_sb"))
    with ExitStack() as tmp, nc.Block() as block:
        sb = lambda n, shape, dt=F32: tmp.enter_context(nc.sbuf_tensor("e_" + n, shape, dt))
        dWo = sb("dWo", [P, KD, D])
        cWk = sb("cWk", [P, KD, D])
        cWv = sb("cWv", [P, KD, D])
        slotb = sb("slotb", [P, D])
        bo = sb("bo", [P, D])
        lng = sb("lng", [P, D])
        lnb = sb("lnb", [P, D])
        brow = [sb(f"brow{q}", [NE * NF, P]) for q in range(2)]
        b2row = sb("b2row", [NE * KD, P])
        b1c = sb("b1c", [P, 2, NE, NF])
        b2c = sb("b2c", [P, NE, KD])
        W1 = [sb(f"W1_{q}", [P, KD, FF]) for q in range(NW)]
        Wg = [sb(f"Wg_{q}", [P, KD, FF]) for q in range(NW)]
        W2 = [sb(f"W2_{q}", [P, NF, D]) for q in range(NW)]
        o1 = sb("o1", [P, D])
        stats = sb("stats", [P, 6])
        mv = sb("mv", [P, 2])
        rs = sb("rs", [P, 4])
        hl = sb("hl", [P, D])
        hT = sb("hT", [P, KD, NR])
        o1T = sb("o1T", [P, KD, NR])
        o2T = sb("o2T", [P, KD, NR])
        ub = [sb(f"ub{q}", [P, 2, NF, NB]) for q in range(2)]
        ug = [sb(f"ug{q}", [P, NF, NB]) for q in range(2)]
        NLOAD = 3 + 3 * NB + 1 + 2 + 1

        @block.sync
        def _(sp):
            def load(e):
                q = e % NW
                if e >= NW:
                    sp.wait_ge(y_ps, e - NW + 1)
                sp.dma_start(W1[q][:], A["L0_ffn_e_W1"][e].rearrange("(k p) f -> p k f", p=P)).then_inc(w_loaded[q], 16)
                sp.dma_start(Wg[q][:], A["L0_ffn_e_Wg"][e].rearrange("(k p) f -> p k f", p=P)).then_inc(w_loaded[q], 16)
                sp.dma_start(W2[q][:], A["L0_ffn_e_W2"][e].rearrange("(k p) n -> p k n", p=P)).then_inc(w_loaded[q], 16)

            for e in range(NE):
                load(e)

        @block.scalar
        def _(act):
            for t, n in ((dWo, "d_Wo"), (cWk, "c_Wk"), (cWv, "c_Wv")):
                act.dma_start(t[:], A["L0_ffn_" + n].rearrange("(k p) n -> p k n", p=P)).then_inc(ld, 16)
            for b in range(NB):
                act.dma_start(slotb[b * NS:(b + 1) * NS, :], A["L0_ffn_slot_query"][0]).then_inc(ld, 16)
                act.dma_start(lng[b * NS:(b + 1) * NS, :], A["L0_ffn_e_ln_g"]).then_inc(ld, 16)
                act.dma_start(lnb[b * NS:(b + 1) * NS, :], A["L0_ffn_e_ln_b"]).then_inc(ld, 16)
            act.dma_start(bo[:], bass.AP(A["L0_ffn_d_bo"].tensor, 0, [[0, P], [1, D]])).then_inc(ld, 16)
            for q, n in enumerate(("e_b1", "e_bg")):
                act.dma_start(brow[q][:], A["L0_ffn_" + n].rearrange("e (f p) -> (e f) p", p=P)).then_inc(ld, 16)
            act.dma_start(b2row[:], A["L0_ffn_e_b2"].rearrange("e (k p) -> (e k) p", p=P)).then_inc(ld, 16)
            act.wait_ge(vst, 4)
            nc.scalar.activation(rs[0:NR, 1:2], rs[0:NR, 0:1], ACT.Sqrt).then_inc(root, 1)
            for e in range(NE):
                act.wait_ge(u_pre, e + 1)
                nc.scalar.activation(ub[e % 2][:], ub[e % 2][:], ACT.Silu).then_inc(u_act, 1)

        @block.tensor
        def _(pe):
            ident = K["ident"]
            pe.wait_ge(ld, 16 * NLOAD)
            for q in range(2):
                nc.tensor.transpose(ps[q][:, 0:P], brow[q][:], ident[:])
            nc.tensor.transpose(ps[2][:, 0:NE * KD], b2row[:], ident[0:NE * KD, 0:NE * KD]).then_inc(pe_c, 1)
            for k in range(KD):
                last = nc.tensor.matmul(ps[3][0:NR, 0:D], K["OT"][:, k, :], dWo[:, k, :], start=(k == 0), stop=(k == KD - 1))
            last.then_inc(pe_c, 1)
            pe.wait_ge(vst, 8)
            for k in range(KD):
                nc.tensor.transpose(ps[4][:, k * P:k * P + NR], hl[0:NR, k * P:(k + 1) * P], ident[0:NR, 0:NR])
                last = nc.tensor.transpose(ps[5][:, k * P:k * P + NR], o1[0:NR, k * P:(k + 1) * P], ident[0:NR, 0:NR])
            last.then_inc(pe_c, 1)

            def up(e):
                q, bank = e % NW, 6 + e % 2
                pe.wait_ge(w_loaded[q], 48 * (e // NW + 1))
                if e >= 2:
                    pe.wait_ge(u_pre, e - 1)
                for g, w in ((0, W1[q]), (1, Wg[q])):
                    for f in range(NF):
                        at = (g * NF + f) * NB
                        for k in range(KD):
                            last = nc.tensor.matmul(ps[bank][:, at:at + NB], w[:, k, f * P:(f + 1) * P], hT[:, k, e:NR:NE],
                                                    start=(k == 0), stop=(k == KD - 1))
                last.then_inc(u_ps, 1)

            def down(e):
                q, bank = e % NW, e % 2
                pe.wait_ge(ug_sb, e + 1)
                if e >= 2:
                    pe.wait_ge(o2_sb, e - 1)
                for c in range(KD):
                    for f in range(NF):
                        last = nc.tensor.matmul(ps[bank][:, c * NB:(c + 1) * NB], W2[q][:, f, c * P:(c + 1) * P], ug[e % 2][:, f, :],
                                                start=(f == 0), stop=(f == NF - 1))
                last.then_inc(y_ps, 1)

            pe.wait_ge(vst, 9)
            pe.wait_ge(bias_sb, 3)
            for e in range(NE + 1):
                if e < NE:
                    up(e)
                if e:
                    down(e - 1)
            pe.wait_ge(o2_sb, NE)
            for w, wt in enumerate((cWk, cWv)):
                for c in range(KD):
                    for k in range(KD):
                        last = nc.tensor.matmul(ps[2 + w][:, c * P:c * P + NR], wt[:, k, c * P:(c + 1) * P], o2T[:, k, :], start=(k == 0), stop=(k == KD - 1))
            last.then_inc(kv_ps, 1)

        @block.vector
        def _(v):
            n = [0]

            def step(ins):
                ins.then_inc(vst, 1)
                n[0] += 1
                v.wait_ge(vst, n[0])

            R = slice(0, NR)
            v.wait_ge(ld, 16 * NLOAD)
            v.wait_ge(pe_c, 2)
            step(nc.vector.tensor_tensor(o1[R, :], ps[3][R, 0:D], slotb[R, :], ALU.add))
            step(nc.vector.tensor_tensor(o1[R, :], o1[R, :], bo[R, :], ALU.add))
            step(nc.vector.bn_stats(stats[R, :], o1[R, :]))
            nc.vector.bn_aggr(mv[R, :], stats[R, :]).then_inc(kv_sb, 1)
            v.wait_ge(kv_sb, 1)
            step(nc.vector.tensor_scalar(rs[R, 0:1], mv[R, 1:2], 1e-5, None, ALU.add))
            v.wait_ge(root, 1)
            step(nc.vector.reciprocal(rs[R, 2:3], rs[R, 1:2]))
            step(nc.vector.tensor_scalar(hl[R, :], o1[R, :], mv[R, 0:1], rs[R, 2:3], ALU.subtract, ALU.mult))
            step(nc.vector.tensor_tensor(hl[R, :], hl[R, :], lng[R, :], ALU.mult))
            step(nc.vector.tensor_tensor(hl[R, :], hl[R, :], lnb[R, :], ALU.add))
            for q in range(2):
                nc.vector.tensor_copy(b1c[:, q, :, :].rearrange("p e f -> p (e f)"), ps[q][:, 0:P]).then_inc(bias_sb, 1)
            nc.vector.tensor_copy(b2c[:].rearrange("p e k -> p (e k)"), ps[2][:, 0:NE * KD]).then_inc(bias_sb, 1)
            v.wait_ge(bias_sb, 3)
            v.wait_ge(pe_c, 3)
            nr = lambda bank: ps[bank][:, 0:KD * P].rearrange("p (k n) -> p k n", k=KD)[:, :, 0:NR]
            step(nc.vector.tensor_copy(hT[:], nr(4)))
            step(nc.vector.tensor_copy(o1T[:], nr(5)))
            for k in range(KD):
                o = o1T[:, k, :].rearrange("p (b e) -> p b e", e=NE)
                step(nc.vector.tensor_tensor(o, o, b2c[:, :, k].unsqueeze(1).to_broadcast([P, NB, NE]), ALU.add))

            def pre(e):
                v.wait_ge(u_ps, e + 1)
                nc.vector.tensor_tensor(ub[e % 2][:], ps[6 + e % 2][:, 0:2 * NF * NB].rearrange("p (g f b) -> p g f b", g=2, f=NF),
                                        b1c[:, :, e, :].unsqueeze(3).to_broadcast([P, 2, NF, NB]), ALU.add).then_inc(u_pre, 1)
                v.wait_ge(u_act, e + 1)
                nc.vector.tensor_tensor(ug[e % 2][:], ub[e % 2][:, 0, :, :], ub[e % 2][:, 1, :, :], ALU.mult).then_inc(ug_sb, 1)

            def post(e):
                v.wait_ge(y_ps, e + 1)
                nc.vector.tensor_tensor(o2T[:, :, e:NR:NE], ps[e % 2][:, 0:KD * NB].rearrange("p (k b) -> p k b", k=KD), o1T[:, :, e:NR:NE],
                                        ALU.add).then_inc(o2_sb, 1)

            for e in range(NE + 1):
                if e < NE:
                    pre(e)
                if e:
                    post(e - 1)
            v.wait_ge(kv_ps, 1)
            for w, dst in enumerate((K["kT"], K["vT"])):
                for c in range(KD):
                    nc.vector.tensor_scalar(dst[:, c, :], ps[2 + w][:, c * P:c * P + NR], K["vecs"][:, 8 + 2 * w + c:9 + 2 * w + c], None, ALU.add)\
                        .then_inc(kv_sb, 1)
            v.wait_ge(kv_sb, 5)


def final_phase(nc, ctx, A, K, dram, ps, out):
    sem = lambda n: ctx.enter_context(nc.semaphore("t_" + n))
    NB = A["x"].shape[0]
    names = ["cwo", "xt0_loaded", "xt1_loaded", "h0_loaded", "h1_loaded", "kblk", "vblk", "m_ps", "m_sb", "row_sb", "vo_ps", "vo_sb", "sc_ps",
             "mx", "dif", "exp", "sum", "rec", "attn", "at_ps", "at_sb", "o_ps", "o_sb", "out0_stored", "out1_stored"]
    S = {n: sem(n) for n in names}
    with ExitStack() as tmp, nc.Block() as block:
        sb = lambda n, shape, dt=F32: tmp.enter_context(nc.sbuf_tensor("t_" + n, shape, dt))
        cWo = sb("cWo", [P, KD, D])
        xT = [sb(f"xT{q}", [P, KD, T]) for q in range(2)]
        h = [sb(f"h{q}", [P, NT, D]) for q in range(2)]
        kb = sb("kb", [P, KD, AH, NS])
        vb = sb("vb", [P, KD, AH, NS])
        Mc = sb("Mc", [P, KD, D])
        crow = sb("crow", [1, D])
        VW = sb("VW", [P, KD, D])
        sc = [sb(f"sc{q}", [P, 32, NS]) for q in range(2)]
        ex = [sb(f"ex{q}", [P, 32, NS]) for q in range(2)]
        at = [sb(f"at{q}", [P, 2, D]) for q in range(2)]
        aT = [sb(f"aT{q}", [P, 2, KD, P]) for q in range(2)]
        mx = sb("mx", [P, 4, 3, 32])
        blk = lambda a: a.rearrange("p h q -> p (h q)")
        outv = out.rearrange("b (t p) d -> b p t d", p=P)
        GR = NT // 2

        @block.sync
        def _(sp):
            sp.dma_start(cWo[:], A["L0_ffn_c_Wo"].rearrange("(k p) n -> p k n", p=P)).then_inc(S["cwo"], 16)
            with sp.Fori(0, NB // 2) as c:
                for q in range(2):
                    sp.wait_ge(S["sc_ps"], c * 2 * GR)
                    sp.dma_start(xT[q][:], dram["xn2T"][:, bass.ds((c * 2 + q) * KD, KD), :]).then_inc(S[f"xt{q}_loaded"], 16)
                    sp.wait_ge(S[f"out{q}_stored"], c * 16)
                    sp.dma_start(h[q][:], dram["h2"][:, bass.ds((c * 2 + q) * NT, NT), :]).then_inc(S[f"h{q}_loaded"], 16)

        @block.gpsimd
        def _(pool):
            hm = lambda k: K["hmask"][:, k, :].unsqueeze(2).to_broadcast([P, AH, NS])
            with pool.Fori(0, NB // 2) as c:
                for q in range(2):
                    b = c * 2 + q
                    pool.wait_ge(S["m_ps"], b)
                    pool.wait_ge(S["vo_ps"], b)
                    for k in range(KD):
                        nc.gpsimd.tensor_tensor(kb[:, k, :, :], K["kT"][:, k, bass.ds(b * NS, NS)].unsqueeze(1).to_broadcast([P, AH, NS]), hm(k), ALU.mult)\
                            .then_inc(S["kblk"], 1)
                    for k in range(KD):
                        nc.gpsimd.tensor_tensor(vb[:, k, :, :], K["vT"][:, k, bass.ds(b * NS, NS)].unsqueeze(1).to_broadcast([P, AH, NS]), hm(k), ALU.mult)\
                            .then_inc(S["vblk"], 1)
                    for g in range(GR):
                        n = b * GR + g
                        pool.wait_ge(S["rec"], n + 1)
                        if g >= 2:
                            pool.wait_ge(S["at_ps"], n - 1)
                        nc.gpsimd.tensor_tensor(at[g % 2][:].rearrange("p t (h s) -> p (t h) s", s=NS), ex[g % 2][:],
                                                mx[:, g, 2, :].unsqueeze(2).to_broadcast([P, 32, NS]), ALU.mult).then_inc(S["attn"], 1)

        @block.tensor
        def _(pe):
            def scores(b, q, g):
                n = b * GR + g
                if g >= 2:
                    pe.wait_ge(S["dif"], n - 1)
                bank = g % 2
                for j in range(2):
                    t = 2 * g + j
                    o = ps[bank][:, j * D:(j + 1) * D]
                    for k in range(KD):
                        nc.tensor.matmul(o, xT[q][:, k, t * P:(t + 1) * P], Mc[:, k, :], start=(k == 0), stop=False)
                    last = nc.tensor.matmul(o, K["ones"][0:1, :], crow[0:1, :], start=False, stop=True)
                last.then_inc(S["sc_ps"], 1)

            def values(b, q, g):
                n = b * GR + g
                pe.wait_ge(S["attn"], n + 1)
                if g >= 2:
                    pe.wait_ge(S["at_sb"], n - 1)
                    pe.wait_ge(S["o_sb"], n - 1)
                for j in range(2):
                    for m in range(KD):
                        last = nc.tensor.transpose(ps[2 + g % 2][:, (j * KD + m) * P:(j * KD + m + 1) * P], at[g % 2][:, j, m * P:(m + 1) * P], K["ident"][:])
                last.then_inc(S["at_ps"], 1)
                pe.wait_ge(S["at_sb"], n + 1)
                for j in range(2):
                    for m in range(KD):
                        last = nc.tensor.matmul(ps[4 + g % 2][:, j * D:(j + 1) * D], aT[g % 2][:, j, m, :], VW[:, m, :], start=(m == 0), stop=(m == KD - 1))
                last.then_inc(S["o_ps"], 1)

            pe.wait_ge(S["cwo"], 16)
            with pe.Fori(0, NB // 2) as c:
                for q in range(2):
                    b = c * 2 + q
                    pe.wait_ge(S["kblk"], b * 2 + 2)
                    for d in range(KD):
                        for k in range(KD):
                            last = nc.tensor.matmul(ps[6][:, d * D:(d + 1) * D], K["cWqT"][:, k, d * P:(d + 1) * P], blk(kb[:, k, :, :]), start=(k == 0), stop=(k == KD - 1))
                    pe.wait_ge(S["dif"], b * GR)
                    for k in range(KD):
                        last = nc.tensor.matmul(ps[0][0:1, 0:D], K["vecs"][:, 6 + k:7 + k], blk(kb[:, k, :, :]), start=(k == 0), stop=(k == KD - 1))
                    last.then_inc(S["m_ps"], 1)
                    pe.wait_ge(S["vblk"], b * 2 + 2)
                    for m in range(KD):
                        for k in range(KD):
                            last = nc.tensor.matmul(ps[7][:, m * D:(m + 1) * D], blk(vb[:, k, :, :])[:, m * P:(m + 1) * P], cWo[:, k, :], start=(k == 0), stop=(k == KD - 1))
                    last.then_inc(S["vo_ps"], 1)
                    pe.wait_ge(S["m_sb"], b + 1)
                    pe.wait_ge(S["row_sb"], b + 1)
                    pe.wait_ge(S["vo_sb"], b + 1)
                    pe.wait_ge(S["o_sb"], b * GR)
                    pe.wait_ge(S[f"xt{q}_loaded"], c * 16 + 16)
                    for g in range(GR + 1):
                        if g < GR:
                            scores(b, q, g)
                        if g:
                            values(b, q, g - 1)

        @block.scalar
        def _(act):
            copy = lambda o, i: nc.scalar.activation(o, i, ACT.Copy)
            with act.Fori(0, NB // 2) as c:
                for q in range(2):
                    b = c * 2 + q
                    act.wait_ge(S["m_ps"], b + 1)
                    act.wait_ge(S["at_ps"], b * GR)
                    copy(Mc[:], ps[6][:].rearrange("p (k n) -> p k n", k=KD)).then_inc(S["m_sb"], 1)
                    copy(crow[:], ps[0][0:1, 0:D]).then_inc(S["row_sb"], 1)
                    act.wait_ge(S["vo_ps"], b + 1)
                    copy(VW[:], ps[7][:].rearrange("p (k n) -> p k n", k=KD)).then_inc(S["vo_sb"], 1)
                    for g in range(GR + 1):
                        n = b * GR + g
                        if g < GR:
                            act.wait_ge(S["dif"], n + 1)
                            if g >= 2:
                                act.wait_ge(S["attn"], n - 1)
                            nc.scalar.activation(ex[g % 2][:], sc[g % 2][:], ACT.Exp, scale=0.25).then_inc(S["exp"], 1)
                        if g:
                            act.wait_ge(S["at_ps"], n)
                            copy(aT[(g - 1) % 2][:].rearrange("p j m n -> p (j m n)"), ps[2 + (g - 1) % 2][:]).then_inc(S["at_sb"], 1)
                            act.wait_ge(S["o_sb"], n)
                            if g == GR:
                                act.dma_start(outv[bass.ds(b, 1), :, :, :].rearrange("b p t d -> (b p) t d"), h[q][:]).then_inc(S[f"out{q}_stored"], 16)
            for q in range(2):
                act.wait_ge(S[f"out{q}_stored"], 16 * (NB // 2))

        @block.vector
        def _(v):
            with v.Fori(0, NB // 2) as c:
                for q in range(2):
                    b = c * 2 + q
                    for g in range(GR + 1):
                        n = b * GR + g
                        if g < GR:
                            s3 = ps[g % 2][:].rearrange("p (n s) -> p n s", s=NS)
                            b3 = lambda a: a.unsqueeze(2).to_broadcast([P, 32, NS])
                            v.wait_ge(S["sc_ps"], n + 1)
                            nc.vector.tensor_reduce(mx[:, g, 0, :], s3, AX.X, ALU.max).then_inc(S["mx"], 1)
                            v.wait_ge(S["mx"], n + 1)
                            if g >= 2:
                                v.wait_ge(S["exp"], n - 1)
                            nc.vector.tensor_tensor(sc[g % 2][:], s3, b3(mx[:, g, 0, :]), ALU.subtract).then_inc(S["dif"], 1)
                        if g < GR:
                            v.wait_ge(S["exp"], n + 1)
                            nc.vector.tensor_reduce(mx[:, g, 1, :], ex[g % 2][:], AX.X, ALU.add).then_inc(S["sum"], 1)
                            v.wait_ge(S["sum"], n + 1)
                            nc.vector.reciprocal(mx[:, g, 2, :], mx[:, g, 1, :]).then_inc(S["rec"], 1)
                        if g:
                            if g == 1:
                                v.wait_ge(S[f"h{q}_loaded"], c * 16 + 16)
                            v.wait_ge(S["o_ps"], n)
                            h2 = h[q][:, 2 * g - 2:2 * g, :]
                            nc.vector.tensor_tensor(h2, ps[4 + (g - 1) % 2][:].rearrange("p (t n) -> p t n", t=2), h2, ALU.add).then_inc(S["o_sb"], 1)


def tower(nc, A, out):
    NB = A["x"].shape[0]
    with ExitStack() as ctx:
        dram = scratch(nc, NB)
        K = constants(nc, ctx, NB)
        K["psum"] = ctx.enter_context(nc.psum_tensor("psum", [P, 8, 512], F32))
        ps = [K["psum"][:, i, :] for i in range(8)]
        setup(nc, ctx, A, K, dram, ps)
        delta_phase(nc, ctx, A, K, dram, ps)
        filter_phase(nc, ctx, A, K, dram, ps)
        slot_setup(nc, ctx, A, K, dram, ps)
        gate_phase(nc, ctx, A, K, dram, ps)
        expert_phase(nc, ctx, A, K, dram, ps)
        final_phase(nc, ctx, A, K, dram, ps, out)


_ATTN = ("Wq", "Wk", "Wv", "Wb", "conv_q", "conv_k", "conv_v", "fir_long", "fir_short", "W1", "b1", "W2", "b2", "log_temp",
         "base_bias", "conv_residual_logit", "rms_w", "Wo")
_FFN = ("slot_query", "d_Wq", "d_Wk", "d_Wv", "d_Wo", "d_bq", "d_bk", "d_bv", "d_bo", "c_Wq", "c_Wk", "c_Wv", "c_Wo", "c_bq", "c_bk",
        "c_bv", "c_bo", "e_ln_g", "e_ln_b", "e_W1", "e_b1", "e_Wg", "e_bg", "e_W2", "e_b2")
_INS = ["x"] + [f"L0_tok_{n}{i}" for i in range(3) for n in ("emb", "w")] + ["L0_attn_" + n for n in _ATTN] + ["L0_ffn_" + n for n in _FFN]


def kernel(**inputs):
    import numpy as _np
    import concourse.bacc as _bacc
    from concourse import mybir as _mybir
    from concourse.bass_utils import run_bass_kernel_spmd as _run

    nc = _bacc.Bacc("TRN2", target_bir_lowering=False, num_devices=1)
    arrays, args = {}, {}
    for name in _INS:
        a = _np.ascontiguousarray(inputs[name])
        arrays[f"in_{name}_dram"] = a
        args[name] = nc.dram_tensor(f"in_{name}_dram", a.shape, _mybir.dt.from_np(a.dtype), kind="ExternalInput").ap()
    shape = tuple(inputs["x"].shape) + (D,)
    out = nc.dram_tensor("out_0_dram", shape, F32, kind="ExternalOutput").ap()
    tower(nc, args, out)
    r = _run(nc, [arrays], core_ids=[0])
    return r.results[0]["out_0_dram"]
```

```python
from contextlib import ExitStack
from math import sqrt

import concourse.bass as bass
from concourse import mybir

F32 = mybir.dt.float32
I32 = mybir.dt.int32
U32 = mybir.dt.uint32
BF16 = mybir.dt.bfloat16
ALU = mybir.AluOpType
ACT = mybir.ActivationFunctionType
AX = mybir.AxisListType

P = 128
D = 256
KD = D // P
T = 1024
NT = T // P
EDGES = (0, 5000, 10000, 50257)
EMB_W = (256, 64, 64)
KE = sum(EMB_W) // P
H, DH = 4, 64
TAPS = 4
FIR = (5, 64)
FPAD = 320
FW = 192
BS = 32
NBLK = P // BS
NST = 16
LEVELS = 2
AH, AD = 16, 16
NS = 16
FF = 1024


def rows_of(h):
    r = 64 * (h % 2)
    return slice(r, r + 64), h // 2


def setup(nc, ctx, A, K, dram, ps):
    sem = lambda n: ctx.enter_context(nc.semaphore(n))
    wl, cl, fl = sem("weights_loaded"), sem("consts_loaded"), sem("filters_loaded")
    pool_c, vst, pe_c, pad_st = sem("pool_consts"), sem("setup_vector_step"), sem("setup_pe_group"), sem("padded_stored")
    act_c = sem("setup_scalar_step")
    NB = A["x"].shape[0]
    NTT = NB * NT
    with ExitStack() as tmp, nc.Block() as block:
        sb = lambda n, shape, dt=F32: tmp.enter_context(nc.sbuf_tensor(n, shape, dt))
        wcat = sb("wcat", [P, KD, KE * P])
        ids_row = sb("ids_row", [NTT, P], I32)
        ids_rf = sb("ids_rf", [NTT, P])
        idf = sb("idf", [P, NTT])
        t1 = sb("t1", [P, NTT])
        t2 = sb("t2", [P, NTT])
        firw = sb("firw", [P, KD, FIR[1]])
        padded = sb("padded", [P, KD, FPAD])
        lt = sb("lt", [P, 8, 4])

        @block.sync
        def _(sp):
            col = 0
            for i, w in enumerate(EMB_W):
                sp.dma_start(wcat[:, :, col:col + w], A[f"L0_tok_w{i}"].rearrange("(k p) n -> p k n", p=P)).then_inc(wl, 16)
                col += w
            sp.dma_start(ids_row[:], A["x"].rearrange("b (t p) -> (b t) p", p=P)).then_inc(wl, 16)
            for w, n in ((K["firs"], "L0_attn_fir_short"), (firw, "L0_attn_fir_long")):
                sp.dma_start(w[:], A[n].rearrange("h d t -> (h d) t").rearrange("(k p) t -> p k t", p=P)).then_inc(fl, 16)
            for n in ("Wq", "Wk", "Wv", "Wo"):
                sp.dma_start(K[n][:], A["L0_attn_" + n].rearrange("(k p) n -> p k n", p=P)).then_inc(cl, 16)
            sp.dma_start(K["W1x"][:], A["L0_attn_W1"][0:D, :].rearrange("(k p) n -> p k n", p=P)).then_inc(cl, 16)
            sp.dma_start(K["W1s"][:], A["L0_attn_W1"][D:D + NST, :]).then_inc(cl, 16)
            sp.dma_start(K["W2"][:], A["L0_attn_W2"].rearrange("(k p) n -> p k n", p=P)).then_inc(cl, 16)
            sp.dma_start(K["Wb"][:], A["L0_attn_Wb"].rearrange("(k p) n -> p k n", p=P)).then_inc(cl, 16)
            sp.wait_ge(vst, 18)
            sp.dma_start(dram["fpad"].rearrange("(k p) t -> p k t", p=P), padded[:]).then_inc(pad_st, 16)
            sp.wait_ge(pad_st, 16)
            sp.wait_ge(cl, 16 * 14)

        @block.scalar
        def _(act):
            for j, n in enumerate(("conv_v", "conv_k", "conv_q")):
                act.dma_start(K["convw"][:, 2 * j:2 * j + 2, :], A["L0_attn_" + n].rearrange("(k p) t -> p k t", p=P)).then_inc(cl, 16)
            act.dma_start(K["b1"][:], A["L0_attn_b1"].rearrange("(k p o) -> p k o", p=P, o=1), allow_slow_non_contiguous=True).then_inc(cl, 16)
            for r in range(2):
                act.dma_start(K["rmsw"][64 * r:64 * r + 64, :], A["L0_attn_rms_w"].rearrange("(p o) -> p o", o=1)).then_inc(cl, 16)
            rowb = lambda ap, n: bass.AP(ap.tensor, 0, [[0, P], [1, n]])
            act.dma_start(K["lbias"][:], rowb(A["L0_attn_base_bias"], 16)).then_inc(fl, 16)
            act.dma_start(lt[:, 0, :], rowb(A["L0_attn_b2"], 4)).then_inc(fl, 16)
            act.dma_start(lt[:, 1, :], rowb(A["L0_attn_log_temp"], 4)).then_inc(fl, 16)
            act.dma_start(lt[:, 2, :], rowb(A["L0_attn_conv_residual_logit"], 4)).then_inc(fl, 16)
            act.wait_ge(fl, 16 * 6)
            nc.scalar.activation(lt[:, 3, :], lt[:, 1, :], ACT.Abs).then_inc(act_c, 1)
            act.wait_ge(act_c, 1)
            nc.scalar.activation(lt[:, 4, :], lt[:, 3, :], ACT.Exp, scale=-1.0).then_inc(act_c, 1)
            nc.scalar.activation(lt[:, 5, :], lt[:, 2, :], ACT.Exp, scale=-1.0).then_inc(act_c, 1)
            act.wait_ge(vst, 20)
            nc.scalar.activation(lt[:, 4, :], lt[:, 4, :], ACT.Ln).then_inc(act_c, 1)

        @block.gpsimd
        def _(pool):
            n = [0]

            def keep(where, cmp, fill, base, pattern, mult, before=None):
                pool.wait_ge(pool_c, n[0])
                nc.gpsimd.affine_select(out=where, in_=where, compare_op=cmp, fill=fill, base=base,
                                        pattern=pattern, channel_multiplier=mult).then_inc(pool_c, 1)
                n[0] += 1
                return n[0]

            def fill(where, value):
                if n[0]:
                    pool.wait_ge(pool_c, n[0])
                nc.gpsimd.memset(where, value).then_inc(pool_c, 1)
                n[0] += 1
                return n[0]

            keep(K["ident"][:], ALU.not_equal, 1.0, 0, [[-1, P]], 1, fill(K["ident"][:], 0.0))
            keep(K["up_strict"][:], ALU.is_gt, 0.0, 0, [[1, P]], -1, fill(K["up_strict"][:], 1.0))
            keep(K["up_incl"][:], ALU.is_ge, 0.0, 0, [[1, P]], -1, fill(K["up_incl"][:], 1.0))
            keep(K["anti"][:], ALU.not_equal, 1.0, 1 - P, [[1, P]], 1, fill(K["anti"][:], 0.0))
            at = fill(K["sel2"][:], 0.0)
            pool.wait_ge(pool_c, at)
            fill(K["sel2"][0:64, 0:1], 1.0)
            fill(K["sel2"][64:128, 1:2], 1.0)
            for l in range(LEVELS):
                m = BS << l
                w = K["wmask"][:, l, :]
                v = w.rearrange("i (g two m) -> i g two m", two=2, m=m)
                at = fill(w, 0.0)
                pool.wait_ge(pool_c, at)
                at = fill(v[:, :, 0, :], -1.0)
                at = keep(v[:, :, 0, :], ALU.is_ge, 0.0, -m, [[-2 * m, P // (2 * m)], [0, m]], 1, at)
                at = keep(v[:, :, 0, :], ALU.is_ge, 0.0, 2 * m - 1, [[2 * m, P // (2 * m)], [0, m]], -1, at)
                keep(w, ALU.not_equal, 1.0, 0, [[-1, P]], 1, at)
            at = fill(K["bmask"][:], 1.0)
            at = keep(K["bmask"][:], ALU.is_ge, 0.0, 0, [[-BS, NBLK]], 1, at)
            keep(K["bmask"][:], ALU.is_ge, 0.0, BS - 1, [[BS, NBLK]], -1, at)
            hm = K["hmask"]
            at = fill(hm[:], 1.0)
            for k in range(KD):
                at = keep(hm[:, k, :], ALU.is_ge, 0.0, k * P, [[-AD, AH]], 1, at)
                at = keep(hm[:, k, :], ALU.is_ge, 0.0, AD - 1 - k * P, [[AD, AH]], -1, at)
            fill(K["qsel"][:], 0.0)
            for g in range(P // NS):
                keep(K["qsel"][:], ALU.not_equal, 1.0, -NS * g, [[-1, NS]], 1)
            pool.wait_ge(pool_c, n[0])

        @block.tensor
        def _(pe):
            pe.wait_ge(pool_c, 2)
            pe.wait_ge(wl, 64)
            for k in range(KE):
                for dh in range(KD):
                    n = k * KD + dh
                    last = nc.tensor.transpose(ps[n // 4][:, (n % 4) * P:(n % 4 + 1) * P], wcat[:, dh, k * P:(k + 1) * P], K["ident"][:])
            last.then_inc(pe_c, 1)
            pe.wait_ge(vst, 1)
            nc.tensor.transpose(ps[2][:, 0:NTT], ids_rf[:], K["ident"][0:NTT, 0:NTT]).then_inc(pe_c, 1)

        @block.vector
        def _(v):
            n = [0]

            def step(ins, fence=True):
                ins.then_inc(vst, 1)
                n[0] += 1
                if fence:
                    v.wait_ge(vst, n[0])

            v.wait_ge(wl, 64)
            step(nc.vector.tensor_copy(ids_rf[:], ids_row[:]))
            v.wait_ge(pe_c, 1)
            step(nc.vector.tensor_copy(K["WcT"][:, 0:2, :], ps[0][:].rearrange("p (k n) -> p k n", k=2)), False)
            step(nc.vector.tensor_copy(K["WcT"][:, 2, :], ps[1][:, 0:D]), False)
            v.wait_ge(pe_c, 2)
            step(nc.vector.tensor_copy(idf[:], ps[2][:, 0:NTT]))
            for i in range(3):
                lo, hi = EDGES[i], EDGES[i + 1]
                step(nc.vector.tensor_scalar(t1[:], idf[:], float(-lo), 0.0, ALU.add, ALU.max), False)
                step(nc.vector.tensor_scalar(t2[:], idf[:], float(lo), None, ALU.is_ge))
                step(nc.vector.tensor_scalar(K["rows"][:, i, :], t1[:], float(hi - lo - 1), None, ALU.min), False)
                step(nc.vector.scalar_tensor_tensor(K["mask"][:, i, :], idf[:], float(hi), t2[:], ALU.is_lt, ALU.mult))
            assert n[0] == 16
            v.wait_ge(fl, 16 * 6)
            step(nc.vector.memset(padded[:], 0.0))
            a = firw[:]
            back = bass.AP(a.tensor, a.offset + FIR[1] - 1, [list(a.ap[0]), list(a.ap[1]), [-1, FIR[1]]])
            step(nc.vector.tensor_copy(padded[:, :, P - 1:P - 1 + FIR[1]], back))
            assert n[0] == 18
            v.wait_ge(act_c, 3)
            step(nc.vector.tensor_scalar(lt[:, 5, :], lt[:, 5, :], 1.0, None, ALU.add))
            step(nc.vector.tensor_scalar(lt[:, 4, :], lt[:, 4, :], 1.0, None, ALU.add))
            v.wait_ge(act_c, 4)
            step(nc.vector.tensor_scalar(lt[:, 6, :], lt[:, 1, :], 0.0, 1e-4, ALU.max, ALU.add))
            step(nc.vector.tensor_tensor(lt[:, 6, :], lt[:, 6, :], lt[:, 4, :], ALU.add))
            step(nc.vector.reciprocal(K["itemp"][:], lt[:, 6, :]))
            step(nc.vector.tensor_copy(K["itemp16"][:].rearrange("p (h j) -> p h j", h=H), K["itemp"][:].unsqueeze(2).to_broadcast([P, H, 4])))
            step(nc.vector.reciprocal(lt[:, 7, :], lt[:, 5, :]))
            step(nc.vector.tensor_scalar(K["halfsig"][:], lt[:, 7, :], 0.5, None, ALU.mult))
            step(nc.vector.tensor_tensor(K["lbias"][:].rearrange("p (h j) -> p h j", h=H), K["lbias"][:].rearrange("p (h j) -> p h j", h=H),
                                         lt[:, 0, :].unsqueeze(1).to_broadcast([P, H, 4]), ALU.add))
            v.wait_ge(cl, 16 * 14)
            for k in range(KD):
                step(nc.vector.tensor_scalar(K["Wo"][:, k, :], K["Wo"][:, k, :], K["rmsw"][:, 0:1], None, ALU.mult), False)
            v.wait_ge(vst, n[0])


def delta_phase(nc, ctx, A, K, dram, ps):
    NB = A["x"].shape[0]
    names = ["gathered", "rows_copied", "rows_masked", "gt_ps", "gt_sb", "h_ps", "h_sb", "h_stored", "ln_stats", "ln_aggr", "ln_eps",
             "ln_std", "ln_rstd", "xn_done", "xt_ps", "xt_sb", "pj_ps", "pj_sb", "conv_step", "silu_done", "sq_done", "ss_ps",
             "norm_eps", "norm_root", "norm_inv", "gamma_sq", "gamma_done", "tm_ps", "tm_sb", "vk_done", "v_stored", "xw1_stored",
             "gk_ps", "qk_ps", "at_sb", "qk_sb", "qkt_done", "a1_sb", "x1t_sb", "x1_ps", "p_ps", "q_sb", "x_ps", "x_sb", "xt2_ps", "xt2_sb",
             "blocks_stored", "blocks_loaded", "unit_set", "subst", "inverses_stored", "inverses_loaded",
             "ks_ps", "r_sb", "y_ps", "z_sb", "ds_ps", "s_sb", "o_ps", "o_sb", "delta_stored", "fir_step", "fs_ps", "fs_sb", "short_stored", "buffers_free", "pads", "gather_go", "ln_go"]
    S = {n: nc.alloc_semaphore(name=n) for n in names}

    with ExitStack() as tmp, nc.Block() as block:
        sb = lambda n, shape, dt=F32: tmp.enter_context(nc.sbuf_tensor(n, shape, dt))
        rowsb = sb("rowsb", [P, 3, NT], U32)
        G = sb("G", [P, NT, KE * P])
        GT = sb("GT", [P, KE, T])
        h_tm = sb("h_tm", [P, NT, D])
        stats = sb("stats", [P, NT, 6])
        mv = sb("mv", [P, NT, 2])
        rstd = sb("rstd", [P, 3, NT])
        xn = sb("xn", [P, NT, D])
        xnT = sb("xnT", [P, KD, T])
        raw = sb("raw", [P, 6, TAPS - 1 + T])
        cm = sb("cm", [P, 6, T])
        beta = sb("beta", [P, NT * H])
        nrm = sb("nrm", [P, 2, NT * H])
        inv = sb("inv", [P, 2, NT * H])
        gam = sb("gam", [P, 2, NT * H])
        xw1 = sb("xw1", [P, KD, T])
        v_tm = sb("v_tm", [P, NT, D])
        k_tm = sb("k_tm", [P, NT, D])
        vk = [raw[:, t // 4, TAPS - 1 + t % 4 * D:TAPS - 1 + (t % 4 + 1) * D] for t in range(NT)]
        dl = sb("dl", [P, NT, D])
        A1T = sb("A1T", [P, NT, H, P])
        gt_flat = GT[:].rearrange("p k t -> p (k t)")
        AB, XB, XC = [gt_flat[:, i * BS * BS:(i + 1) * BS * BS].rearrange("p (j i) -> p j i", i=BS) for i in range(3)]
        ys = xn[:].rearrange("p t n -> p (t n)").rearrange("p (k t) -> p k t", k=KD)
        prod, z, R = K["Md"][:, 0, :], K["Md"][:, 1, :], K["cWqT"][:, 0, :]
        St = K["cWqT"][:, 1, :].rearrange("p (q i n) -> p q i n", q=2, i=2)
        X = [sb(f"X{j}", [P, H, P]) for j in range(2)]
        Q = [sb(f"Q{j}", [P, H, P]) for j in range(2)]
        XT = [sb(f"XT{j}", [P, H, P]) for j in range(4)]
        QKT = sb("QKT", [P, NT, H, P])

        sq = raw[:, 2:6, TAPS - 1:]
        g4 = lambda bank: ps[bank][:].rearrange("p (h n) -> p h n", h=H)
        h4 = lambda bank: ps[bank][:, 0:D].rearrange("p (h n) -> p h n", h=H)
        per_head = lambda a, t, n: a[:, t * H:(t + 1) * H].unsqueeze(2).to_broadcast([P, H, n])
        by_head = lambda a: a.rearrange("p (h n) -> p h n", h=H)
        over_heads = lambda m: m.unsqueeze(1).to_broadcast([P, H, P])
        HB = (4, 5, 2, 3)
        TAIL = NT // 2

        def over_sequences(eng, body):
            with eng.Fori(0, NB - 1) as b:
                body(b, True)
            body(NB - 1, False)

        ORDER = (2, 3, 0, 1, 4, 5)
        C = 2 * LEVELS
        CT = C * NT // 2
        VS = 16 * (1 + H)

        @block.gpsimd
        def _(pool):
            def gather(b, later):
                if later:
                    pool.wait_ge(S["gathered"], b * (3 * NT * 16))
                    pool.wait_ge(S["gt_ps"], b * 6)
                nc.gpsimd.tensor_copy(rowsb[:], K["rows"][:, :, bass.ds(b * NT, NT)]).then_inc(S["rows_copied"], 1)
                pool.wait_ge(S["rows_copied"], b + 1).then_inc(S["gather_go"], 1)
                for t in range(NT):
                    col = 0
                    for i in range(3):
                        nc.gpsimd.indirect_dma_start(G[:, t, col:col + EMB_W[i]], None, A[f"L0_tok_emb{i}"],
                                                     bass.IndirectOffsetOnAxis(ap=rowsb[:, i, t:t + 1], axis=0)).then_inc(S["gathered"], 16)
                        col += EMB_W[i]

            def sequence(b, more):
                if more:
                    gather(b + 1, True)
                for t in range(NT):
                    pool.wait_ge(S["at_sb"], b * H * NT + H * t + H)
                    nc.gpsimd.tensor_tensor(A1T[:, t], A1T[:, t], over_heads(K["ident"][:]), ALU.add).then_inc(S["a1_sb"], 1)
                pool.wait_ge(S["norm_root"], b * 2 + 1)
                pool.wait_ge(S["tm_sb"], b * 8 + 4)
                for half in range(2):
                    ts = slice(4 * half, 4 * half + 4)
                    nc.gpsimd.tensor_tensor(raw[:, half, TAPS - 1:].rearrange("p (t n) -> p t n", n=DH), v_tm[:, ts, :].rearrange("p t (h n) -> p (t h) n", h=H),
                                            nrm[:, 0, half * 4 * H:(half + 1) * 4 * H].unsqueeze(2).to_broadcast([P, 4 * H, DH]), ALU.mult)\
                        .then_inc(S["vk_done"], 1)
                for p in range(NT // 2):
                    pool.wait_ge(S["qk_sb"], b * NT + 2 * p + 2)
                    for t in (2 * p, 2 * p + 1):
                        nc.gpsimd.tensor_tensor(QKT[:, t], QKT[:, t], over_heads(K["up_incl"][:]), ALU.mult).then_inc(S["qkt_done"], 1)
                pool.wait_ge(S["inverses_loaded"], b * 16 * NBLK + 16 * NBLK)
                for t in range(NT):
                    if t >= 4:
                        pool.wait_ge(S["y_ps"], b * NT + t - 3)
                    nc.gpsimd.tensor_tensor(XT[t % 4][:].rearrange("p h (g j) -> p h g j", j=BS),
                                            XC[:, t * H:(t + 1) * H, :].unsqueeze(2).to_broadcast([P, H, NBLK, BS]),
                                            K["bmask"][:].unsqueeze(1).unsqueeze(3).to_broadcast([P, H, NBLK, BS]), ALU.mult).then_inc(S["x1t_sb"], 1)

            gather(0, False)
            over_sequences(pool, sequence)

        @block.sync
        def _(sp):
            def sequence(b, more):
                sp.wait_ge(S["h_sb"], b * 4 + 4)
                sp.dma_start(dram["h"][:, bass.ds(b * NT, NT), :], h_tm[:]).then_inc(S["h_stored"], 16)
                sp.wait_ge(S["a1_sb"], b * NT + NT)
                for g in range(NBLK):
                    rows = slice(g * BS, (g + 1) * BS)
                    sp.dma_start(bass.AP(dram["blocks"].tensor, g * BS * BS, [[BS, BS], [NBLK * BS * BS, NT * H], [1, BS]]),
                                 A1T[rows, :, :, rows].rearrange("p t h n -> p (t h) n")).then_inc(S["blocks_stored"], 16)
                sp.wait_ge(S["blocks_stored"], b * 16 * NBLK + 16 * NBLK)
                sp.dma_start(AB.rearrange("p j i -> p (j i)"), dram["blocks"][:, :]).then_inc(S["blocks_loaded"], 16)
                sp.wait_ge(S["pj_sb"], b * 17 + 17)
                sp.dma_start(dram["xw1"][:, bass.ds(b * KD, KD), :], xw1[:]).then_inc(S["xw1_stored"], 16)
                sp.wait_ge(S["tm_sb"], b * 8 + 4)
                sp.dma_start(dram["v"][:, bass.ds(b * NT, NT), :], v_tm[:]).then_inc(S["v_stored"], 16)
                for h in range(H):
                    sp.dma_start(dram["vh"][h, :, bass.ds(b * NT, NT), :], v_tm[:, :, h * DH:(h + 1) * DH]).then_inc(S["v_stored"], 16)
                sp.wait_ge(S["subst"], b * 2 * (BS - 1) + 2 * (BS - 1))
                sp.dma_start(dram["inverses"][:, :], XB.rearrange("p j i -> p (j i)")).then_inc(S["inverses_stored"], 16)
                sp.wait_ge(S["inverses_stored"], b * 16 + 16)
                for g in range(NBLK):
                    sp.dma_start(XC[g * BS:(g + 1) * BS, :, :], bass.AP(dram["inverses"].tensor, g * BS * BS, [[BS, BS], [NBLK * BS * BS, NT * H], [1, BS]]))\
                        .then_inc(S["inverses_loaded"], 16)
                sp.wait_ge(S["fs_sb"], b * 4 + 4)
                sp.dma_start(dram["short"][:, bass.ds(b * NT, NT), :], v_tm[:]).then_inc(S["short_stored"], 16)
                sp.wait_ge(S["o_sb"], b * 2 * NT + 2 * NT)
                sp.dma_start(dram["delta"][:, bass.ds(b * NT, NT), :], dl[:]).then_inc(S["delta_stored"], 16)
                sp.wait_ge(S["v_stored"], b * VS + VS).then_inc(S["buffers_free"], 1)
                for n in ("xw1_stored", "short_stored", "delta_stored"):
                    sp.wait_ge(S[n], b * 16 + 16).then_inc(S["buffers_free"], 1)

            over_sequences(sp, sequence)
            sp.wait_ge(S["v_stored"], VS * NB)
            for n in ("h_stored", "xw1_stored", "short_stored", "delta_stored"):
                sp.wait_ge(S[n], 16 * NB)

        @block.tensor
        def _(pe):
            ident = K["ident"][:]

            def inverse(b, p, s):
                tiles = (2 * p, 2 * p + 1)
                if s == 0:
                    if p:
                        pe.wait_ge(S["xt2_sb"], b * CT + p * C)
                    for t in tiles:
                        j = t % 2
                        pe.wait_ge(S["x1t_sb"], b * NT + t + 1)
                        for h in range(H):
                            last = nc.tensor.transpose(g4(4 + j)[:, h, :], XT[t % 4][:, h, :], ident)
                        last.then_inc(S["x1_ps"], 1)
                    return
                l = s - 1
                for t in tiles:
                    j = t % 2
                    pe.wait_ge(S["x_sb"], b * CT + p * C + 2 * l + j + 1)
                    if l:
                        pe.wait_ge(S["xt2_sb"], b * CT + p * C + 2 * l + j - 1)
                    for h in range(H):
                        last = nc.tensor.matmul(g4(j)[:, h, :], A1T[:, t, h, :], X[j][:, h, :], start=True, stop=True)
                    last.then_inc(S["p_ps"], 1)

            def inverse_rest(b, p, s):
                l = s - 1
                for t in (2 * p, 2 * p + 1):
                    j = t % 2
                    pe.wait_ge(S["q_sb"], b * CT + p * C + 2 * l + j + 1)
                    if l < LEVELS - 1:
                        for h in range(H):
                            last = nc.tensor.matmul(g4(2 + j)[:, h, :], XT[t % 4][:, h, :], Q[j][:, h, :], start=True, stop=True)
                        last.then_inc(S["x_ps"], 1)
                    for h in range(H):
                        last = nc.tensor.matmul(g4(4 + j)[:, h, :], Q[j][:, h, :], XT[t % 4][:, h, :], start=True, stop=True)
                    last.then_inc(S["xt2_ps"], 1)

            def scan(b, p, s):
                t = 2 * p + s // 3
                tk = slice(t * P, (t + 1) * P)
                if s % 3 == 0:
                    pe.wait_ge(S["s_sb"], b * (NT + 1) + t + 1)
                    if t:
                        pe.wait_ge(S["o_sb"], b * 2 * NT + 2 * t)
                    for h in range(H):
                        rows, i = rows_of(h)
                        last = nc.tensor.matmul(h4(6 + h % 2)[:, i, :], cm[rows, 2 + i, tk], St[rows, t % 2, i, :], start=True, stop=True)
                    last.then_inc(S["ks_ps"], 1)
                elif s % 3 == 1:
                    pe.wait_ge(S["r_sb"], b * 2 * NT + 2 * t + 2)
                    pe.wait_ge(S["xt2_sb"], b * CT + C * p + C)
                    for h in range(H):
                        last = nc.tensor.matmul(h4(6)[:, h, :], XT[t % 4][:, h, :], R[:, h * DH:(h + 1) * DH], start=True, stop=True)
                    last.then_inc(S["y_ps"], 1)
                else:
                    pe.wait_ge(S["z_sb"], b * NT + t + 1)
                    for h in range(H):
                        rows, i = rows_of(h)
                        last = nc.tensor.matmul(ps[7][rows, i * DH:(i + 1) * DH], k_tm[:, t, h * DH:(h + 1) * DH], z[:, h * DH:(h + 1) * DH],
                                                start=True, stop=True)
                    last.then_inc(S["ds_ps"], 1)
                    for h in (0, 2, 1, 3):
                        rows, i = rows_of(h)
                        if h == 1:
                            pe.wait_ge(S["s_sb"], b * (NT + 1) + t + 2)
                        nc.tensor.matmul(h4(6 + h % 2)[:, i, :], cm[rows, 4 + i, tk], St[rows, t % 2, i, :], start=True, stop=False)
                        last = nc.tensor.matmul(h4(6 + h % 2)[:, i, :], QKT[:, t, h, :], z[:, h * DH:(h + 1) * DH], start=False, stop=True)
                    last.then_inc(S["o_ps"], 1)

            def turn_rows(b, later):
                pe.wait_ge(S["rows_masked"], b * 3 + 3)
                for n in range(6):
                    if n >= 4:
                        pe.wait_ge(S["gt_sb"], b * 6 + n - 3)
                    half, k = n // 3, n % 3
                    for q in range(4):
                        last = nc.tensor.transpose(ps[n % 4][:, q * P:(q + 1) * P], G[:, 4 * half + q, k * P:(k + 1) * P], ident)
                    last.then_inc(S["gt_ps"], 1)
                if later:
                    pe.wait_ge(S["xt2_sb"], b * CT)

            def embed(b, n):
                pe.wait_ge(S["gt_sb"], b * 6 + (3 if n < 1 else 6))
                for q in range(2):
                    t = 2 * n + q
                    for k in range(KE):
                        last = nc.tensor.matmul(ps[HB[n]][:, q * D:(q + 1) * D], GT[:, k, t * P:(t + 1) * P], K["WcT"][:, k, :],
                                                start=(k == 0), stop=(k == KE - 1))
                last.then_inc(S["h_ps"], 1)

            def sequence(b, more):
                for n in range(4):
                    half, k = n // 2, n % 2
                    pe.wait_ge(S["xn_done"], b * NT + 4 * half + 4)
                    for q in range(4):
                        last = nc.tensor.transpose(ps[n][:, q * P:(q + 1) * P], xn[:, 4 * half + q, k * P:(k + 1) * P], ident)
                    last.then_inc(S["xt_ps"], 1)
                pe.wait_ge(S["h_sb"], b * 4 + 4)
                pe.wait_ge(S["xt_sb"], b * 4 + 4)
                for t in range(NT):
                    for k in range(KD):
                        last = nc.tensor.matmul(ps[4][:, t * H:(t + 1) * H], xnT[:, k, t * P:(t + 1) * P], K["Wb"][:, k, :],
                                                start=(k == 0), stop=(k == KD - 1))
                last.then_inc(S["pj_ps"], 1)
                def project(ns):
                    for n in ns:
                        if n >= 4:
                            pe.wait_ge(S["pj_sb"], b * 17 + n - 3)
                        w, m, c = (n - 1) // 4, (n - 1) // 2 % 2, (n - 1) % 2
                        for k in range(KD):
                            last = nc.tensor.matmul(ps[4 + n % 4][:], K[("Wk", "Wv", "Wq", "W1x")[w]][:, k, m * P:(m + 1) * P],
                                                    xnT[:, k, c * 512:(c + 1) * 512], start=(k == 0), stop=(k == KD - 1))
                        last.then_inc(S["pj_ps"], 1)

                def squares(w, bank):
                    pe.wait_ge(S["sq_done"], b * 4 + 2 * w + 2)
                    for i in range(2):
                        for t in range(NT):
                            last = nc.tensor.matmul(ps[bank][:, t * H + 2 * i:t * H + 2 * i + 2], sq[:, 2 * w + i, t * P:(t + 1) * P], K["sel2"][:],
                                                    start=True, stop=True)
                    last.then_inc(S["ss_ps"], 1)

                def gram(p, w, done):
                    for t in (2 * p, 2 * p + 1):
                        tk = slice(t * P, (t + 1) * P)
                        for h in range(H):
                            rows, i = rows_of(h)
                            last = nc.tensor.matmul(g4(2 * (p % 2) + h % 2)[:, 2 * (t % 2) + i, :], cm[rows, 2 + i, tk], cm[rows, w + i, tk],
                                                    start=True, stop=True)
                    last.then_inc(S[done], 1)

                project(range(1, 13))
                squares(0, 2)
                for p in range(NT // 2):
                    if p == 1:
                        pe.wait_ge(S["norm_eps"], b * 2 + 1)
                    if p >= 2:
                        pe.wait_ge(S["at_sb"], b * NT * H + 2 * H * (p - 1))
                    gram(p, 2, "gk_ps")
                project(range(13, 17))
                for n in range(8):
                    i, half = n // 2, n % 2
                    pe.wait_ge(S["silu_done"], b * 6 + (3 + i if i < 2 else 4))
                    if n < 4:
                        pe.wait_ge(S["pj_sb"], b * 17 + 14 + n)
                    else:
                        pe.wait_ge(S["tm_sb"], b * 8 + n - 3)
                    bank = (5, 6, 7, 4)[n % 4]
                    for q in range(4):
                        t = 4 * half + q
                        last = nc.tensor.transpose(ps[bank][:, q * P:(q + 1) * P], cm[:, i, t * P:(t + 1) * P], ident)
                    last.then_inc(S["tm_ps"], 1)
                pe.wait_ge(S["silu_done"], b * 6 + 6)
                for p in range(NT // 2):
                    if p < 2:
                        pe.wait_ge(S["at_sb"], b * NT * H + 2 * H * (p + 3))
                    else:
                        pe.wait_ge(S["qk_sb"], b * NT + 2 * (p - 1))
                    gram(p, 4, "qk_ps")
                pe.wait_ge(S["tm_sb"], b * 8 + 8)
                squares(1, 6)

                def turn_filtered(ns):
                    pe.wait_ge(S["fir_step"], b * KD * FIR[0] + KD * FIR[0])
                    pe.wait_ge(S["norm_eps"], b * 2 + 2)
                    for n in ns:
                        if n >= 2:
                            pe.wait_ge(S["fs_sb"], b * 4 + n - 1)
                        for q in range(4):
                            t = 4 * (n % 2) + q
                            last = nc.tensor.transpose(ps[7 - n % 2][:, q * P:(q + 1) * P], ys[:, n // 2, t * P:(t + 1) * P], ident)
                        last.then_inc(S["fs_ps"], 1)

                pe.wait_ge(S["qk_sb"], b * NT + NT)
                for p in range(TAIL + 1):
                    if p == TAIL and more:
                        turn_rows(b + 1, True)
                    for s in range(6):
                        if p < NT // 2 and s % 2 == 0:
                            inverse(b, p, s // 2)
                        if p:
                            if p == 1 and s == 0:
                                pe.wait_ge(S["fs_sb"], b * 4 + 4)
                            if s == 0:
                                pe.wait_ge(S["qkt_done"], b * NT + 2 * p)
                            scan(b, p - 1, s)
                        if p < NT // 2 and s in (2, 4):
                            inverse_rest(b, p, s // 2)
                        if p == 0 and s in (3, 5):
                            turn_filtered((0, 1) if s == 3 else (2, 3))
                        if p == TAIL and more and s < 4:
                            embed(b + 1, s)

            turn_rows(0, False)
            for n in range(4):
                embed(0, n)
            over_sequences(pe, sequence)

        @block.scalar
        def _(act):
            ident_copy = lambda o, i: nc.scalar.activation(o, i, ACT.Copy)
            def embedded(b, later):
                for n in range(6):
                    act.wait_ge(S["gt_ps"], b * 6 + n + 1)
                    ident_copy(GT[:, n % 3, n // 3 * 512:(n // 3 + 1) * 512], ps[n % 4][:]).then_inc(S["gt_sb"], 1)
                if later:
                    act.wait_ge(S["h_stored"], b * 16)
                for n in range(4):
                    act.wait_ge(S["h_ps"], b * 4 + n + 1)
                    ident_copy(h_tm[:, 2 * n:2 * n + 2, :], ps[HB[n]][:].rearrange("p (t n) -> p t n", t=2)).then_inc(S["h_sb"], 1)

            def sequence(b, more):
                act.wait_ge(S["ln_eps"], b + 1)
                nc.scalar.activation(rstd[:, 1, :], rstd[:, 0, :], ACT.Sqrt).then_inc(S["ln_std"], 1)
                for n in range(4):
                    act.wait_ge(S["xt_ps"], b * 4 + n + 1)
                    ident_copy(xnT[:, n % 2, n // 2 * 512:(n // 2 + 1) * 512], ps[n][:]).then_inc(S["xt_sb"], 1)
                act.wait_ge(S["pj_ps"], b * 17 + 1)
                nc.scalar.activation(beta[:], ps[4][:, 0:NT * H], ACT.Sigmoid).then_inc(S["pj_sb"], 1)
                act.wait_ge(S["pads"], 1)
                def projected(ns):
                    for n in ns:
                        act.wait_ge(S["pj_ps"], b * 17 + n + 1)
                        i, c = (n - 1) // 2, (n - 1) % 2
                        if i < 6:
                            ident_copy(raw[:, ORDER[i], TAPS - 1 + c * 512:TAPS - 1 + (c + 1) * 512], ps[4 + n % 4][:]).then_inc(S["pj_sb"], 1)
                        else:
                            if n == 13:
                                act.wait_ge(S["h_stored"], b * 16 + 16)
                            ident_copy(xw1[:, i - 6, c * 512:(c + 1) * 512], ps[4 + n % 4][:]).then_inc(S["pj_sb"], 1)

                def silu(w):
                    for i in range(2):
                        act.wait_ge(S["conv_step"], b * 24 + 8 * w + 7 + i)
                        nc.scalar.activation(cm[:, ORDER[2 * w + i], :], cm[:, ORDER[2 * w + i], :], ACT.Silu).then_inc(S["silu_done"], 1)

                def squares(w):
                    act.wait_ge(S["silu_done"], b * 6 + (2, 6)[w])
                    for i in range(2):
                        nc.scalar.activation(sq[:, 2 * w + i, :], cm[:, 2 + 2 * w + i, :], ACT.Square).then_inc(S["sq_done"], 1)

                def root(w):
                    act.wait_ge(S["norm_eps"], b * 2 + w + 1)
                    nc.scalar.activation(nrm[:, w, :], nrm[:, w, :], ACT.Sqrt).then_inc(S["norm_root"], 1)

                projected(range(1, 9))
                silu(0)
                squares(0)
                projected(range(9, 13))
                root(0)
                projected(range(13, 17))
                silu(1)
                for n in range(8):
                    i, half = n // 2, n % 2
                    act.wait_ge(S["tm_ps"], b * 8 + n + 1)
                    dst = (v_tm, k_tm)[i // 2][:, 4 * half:4 * half + 4, (i % 2) * P:(i % 2 + 1) * P]
                    ident_copy(dst, ps[(5, 6, 7, 4)[n % 4]][:].rearrange("p (t n) -> p t n", t=4)).then_inc(S["tm_sb"], 1)
                silu(2)
                for p in range(NT // 2):
                    act.wait_ge(S["qk_ps"], b * (NT // 2) + p + 1)
                    for r in range(2):
                        ident_copy(QKT[:, 2 * p:2 * p + 2, r::2, :].rearrange("p t i n -> p (t i) n"), g4(2 * (p % 2) + r)).then_inc(S["qk_sb"], 1)
                squares(1)
                root(1)
                for p in range(NT // 2):
                    for t in (2 * p, 2 * p + 1):
                        act.wait_ge(S["x1_ps"], b * NT + t + 1)
                        ident_copy(X[t % 2][:], g4(4 + t % 2)).then_inc(S["x_sb"], 1)
                    for l in range(LEVELS):
                        for t in (2 * p, 2 * p + 1):
                            if l < LEVELS - 1:
                                act.wait_ge(S["x_ps"], b * (CT - NT) + p * (C - 2) + 2 * l + t % 2 + 1)
                                ident_copy(X[t % 2][:], g4(2 + t % 2)).then_inc(S["x_sb"], 1)
                            act.wait_ge(S["xt2_ps"], b * CT + p * C + 2 * l + t % 2 + 1)
                            ident_copy(XT[t % 4][:], g4(4 + t % 2)).then_inc(S["xt2_sb"], 1)
                        if p == 0:
                            act.wait_ge(S["v_stored"], b * VS + VS)
                            for n in (2 * l, 2 * l + 1):
                                act.wait_ge(S["fs_ps"], b * 4 + n + 1)
                                ident_copy(v_tm[:, 4 * (n % 2):4 * (n % 2) + 4, n // 2 * P:(n // 2 + 1) * P],
                                           ps[7 - n % 2][:].rearrange("p (t n) -> p t n", t=4)).then_inc(S["fs_sb"], 1)
                if more:
                    embedded(b + 1, True)

            embedded(0, False)
            over_sequences(act, sequence)

        @block.vector
        def _(v):
            nc.vector.memset(raw[:, :, 0:TAPS - 1], 0.0).then_inc(S["pads"], 1)
            def mask_rows(b):
                v.wait_ge(S["gathered"], b * (3 * NT * 16) + 3 * NT * 16)
                col = 0
                for i in range(3):
                    g = G[:, :, col:col + EMB_W[i]]
                    nc.vector.tensor_tensor(g, g, K["mask"][:, i, bass.ds(b * NT, NT)].unsqueeze(2).to_broadcast([P, NT, EMB_W[i]]),
                                            ALU.mult).then_inc(S["rows_masked"], 1)
                    col += EMB_W[i]

            def moments(b, n):
                v.wait_ge(S["h_sb"], b * 4 + n + 1)
                for t in (2 * n, 2 * n + 1):
                    nc.vector.bn_stats(stats[:, t, :], h_tm[:, t, :]).then_inc(S["ln_stats"], 1)

            def sequence(b, more):
                v.wait_ge(S["ln_stats"], b * NT + NT).then_inc(S["ln_go"], 1)
                for t in range(NT):
                    nc.vector.bn_aggr(mv[:, t, :], stats[:, t, :]).then_inc(S["ln_aggr"], 1)
                v.wait_ge(S["ln_aggr"], b * NT + NT)
                nc.vector.tensor_scalar(rstd[:, 0, :], mv[:, :, 1], 1e-5, None, ALU.add).then_inc(S["ln_eps"], 1)
                v.wait_ge(S["ln_std"], b + 1)
                nc.vector.reciprocal(rstd[:, 2, :], rstd[:, 1, :]).then_inc(S["ln_rstd"], 1)
                v.wait_ge(S["ln_rstd"], b + 1)
                for t in range(NT):
                    nc.vector.tensor_scalar(xn[:, t, :], h_tm[:, t, :], mv[:, t, 0:1], rstd[:, 2, t:t + 1], ALU.subtract, ALU.mult)\
                        .then_inc(S["xn_done"], 1)
                def conv(w):
                    for n in range(2 * TAPS):
                        j, i = n // 2, ORDER[2 * w + n % 2]
                        if j == 0:
                            v.wait_ge(S["pj_sb"], b * 17 + 3 + 2 * (2 * w + n % 2))
                            nc.vector.tensor_scalar(cm[:, i, :], raw[:, i, 0:T], K["convw"][:, i, 0:1], None, ALU.mult).then_inc(S["conv_step"], 1)
                        else:
                            v.wait_ge(S["conv_step"], b * 24 + 8 * w + n - 1)
                            nc.vector.scalar_tensor_tensor(cm[:, i, :], raw[:, i, j:j + T], K["convw"][:, i, j:j + 1], cm[:, i, :],
                                                           ALU.mult, ALU.add).then_inc(S["conv_step"], 1)

                def norms(w, bank):
                    v.wait_ge(S["ss_ps"], b * 2 + w + 1)
                    nc.vector.tensor_scalar(nrm[:, w, :], ps[bank][:, 0:NT * H], 1e-6, None, ALU.add).then_inc(S["norm_eps"], 1)
                    v.wait_ge(S["norm_root"], b * 2 + w + 1)
                    nc.vector.reciprocal(inv[:, w, :], nrm[:, w, :]).then_inc(S["norm_inv"], 1)
                    v.wait_ge(S["norm_inv"], b * 2 + w + 1)

                conv(0)
                conv(1)
                norms(0, 2)
                nc.vector.tensor_tensor(gam[:, 1, :], inv[:, 0, :], inv[:, 0, :], ALU.mult).then_inc(S["gamma_sq"], 1)
                v.wait_ge(S["gamma_sq"], b + 1)
                nc.vector.tensor_tensor(gam[:, 0, :], gam[:, 1, :], beta[:], ALU.mult).then_inc(S["gamma_done"], 1)
                v.wait_ge(S["gamma_done"], b + 1)
                nc.vector.memset(St[:, 0, :, :], 0.0).then_inc(S["s_sb"], 1)
                for p in range(NT // 2):
                    v.wait_ge(S["gk_ps"], b * (NT // 2) + p + 1)
                    for t in (2 * p, 2 * p + 1):
                        for h in range(H):
                            nc.vector.scalar_tensor_tensor(A1T[:, t, h, :], g4(2 * (p % 2) + h % 2)[:, 2 * (t % 2) + h // 2, :],
                                                           gam[:, 0, t * H + h:t * H + h + 1], K["up_strict"][:], ALU.mult, ALU.mult)\
                                .then_inc(S["at_sb"], 1)
                conv(2)
                nc.vector.memset(XB, 0.0).then_inc(S["unit_set"], 1)
                v.wait_ge(S["unit_set"], b * 2 + 1)
                nc.vector.memset(gt_flat[:, BS * BS:2 * BS * BS:BS + 1], 1.0).then_inc(S["unit_set"], 1)
                v.wait_ge(S["blocks_loaded"], b * 16 + 16)
                v.wait_ge(S["unit_set"], b * 2 + 2)
                for n, r in enumerate(range(BS - 1, 0, -1)):
                    w = BS - r
                    pr = prod[:, 0:r * w].rearrange("p (j c) -> p j c", c=w)
                    if n:
                        v.wait_ge(S["subst"], b * 2 * (BS - 1) + 2 * n)
                    nc.vector.tensor_tensor(pr, AB[:, 0:r, r:r + 1].to_broadcast([P, r, w]), XB[:, r:r + 1, r:].to_broadcast([P, r, w]), ALU.mult)\
                        .then_inc(S["subst"], 1)
                    v.wait_ge(S["subst"], b * 2 * (BS - 1) + 2 * n + 1)
                    nc.vector.tensor_tensor(XB[:, 0:r, r:], XB[:, 0:r, r:], pr, ALU.subtract).then_inc(S["subst"], 1)
                norms(1, 6)
                for n in range(KD * FIR[0]):
                    lag, i = n // KD, n % KD
                    w = K["firs"][:, i, FIR[0] - 1 - lag:FIR[0] - lag]
                    if n < KD:
                        nc.vector.tensor_scalar(ys[:, i, :], cm[:, i, :], w, None, ALU.mult).then_inc(S["fir_step"], 1)
                    else:
                        v.wait_ge(S["fir_step"], b * KD * FIR[0] + n - 1)
                        nc.vector.scalar_tensor_tensor(ys[:, i, lag:], cm[:, i, 0:T - lag], w, ys[:, i, lag:], ALU.mult, ALU.add)\
                            .then_inc(S["fir_step"], 1)

                def inverse(p, s):
                    for j in range(2):
                        v.wait_ge(S["p_ps"], b * CT + p * C + 2 * (s - 1) + j + 1)
                        nc.vector.tensor_tensor(Q[j][:], g4(j), over_heads(K["wmask"][:, s - 1, :]), ALU.mult).then_inc(S["q_sb"], 1)

                def scan(p, s):
                    t = 2 * p + s // 3
                    if s % 3 == 0:
                        v.wait_ge(S["ks_ps"], b * NT + t + 1)
                        v.wait_ge(S["vk_done"], b * 2 + 2)
                        for r in range(2):
                            nc.vector.tensor_tensor(by_head(R[:])[:, r::2, :], by_head(vk[t])[:, r::2, :], h4(6 + r)[:, 0:2, :],
                                                    ALU.subtract).then_inc(S["r_sb"], 1)
                    elif s % 3 == 1:
                        v.wait_ge(S["y_ps"], b * NT + t + 1)
                        nc.vector.tensor_tensor(z[:].rearrange("p (h n) -> p h n", h=H), h4(6), per_head(gam[:, 0, :], t, DH), ALU.mult)\
                            .then_inc(S["z_sb"], 1)
                    else:
                        v.wait_ge(S["ds_ps"], b * NT + t + 1)
                        nc.vector.tensor_tensor(St[:, (t + 1) % 2, :, :], St[:, t % 2, :, :], ps[7][:, 0:P].rearrange("p (i n) -> p i n", i=2),
                                                ALU.add).then_inc(S["s_sb"], 1)
                        v.wait_ge(S["o_ps"], b * NT + t + 1)
                        if t == 0:
                            v.wait_ge(S["h_stored"], b * 16 + 16)
                        for r in range(2):
                            nc.vector.tensor_tensor(by_head(dl[:, t, :])[:, r::2, :], h4(6 + r)[:, 0:2, :],
                                                    per_head(inv[:, 1, :], t, DH)[:, r::2, :], ALU.mult).then_inc(S["o_sb"], 1)

                for p in range(TAIL + 1):
                    if p == TAIL and more:
                        mask_rows(b + 1)
                    for s in range(6):
                        if p < NT // 2 and s in (2, 4):
                            inverse(p, s // 2)
                        if p:
                            scan(p - 1, s)
                        if p == TAIL and more and s >= 2:
                            moments(b + 1, s - 2)

            mask_rows(0)
            for n in range(4):
                moments(0, n)
            over_sequences(v, sequence)


def constants(nc, ctx, NB):
    shapes = {"ident": [P, P], "up_strict": [P, P], "up_incl": [P, P], "anti": [P, P], "bmask": [P, NBLK], "wmask": [P, LEVELS, P], "sel2": [P, 2],
              "hmask": [P, KD, AH], "vecs": [P, 12], "cbo": [P, D], "dWv": [P, KD, D], "cWqT": [P, KD, D], "Md": [P, KD, D],
              "drow": [P, KD], "OT": [P, KD, NB * NS], "kT": [P, KD, NB * NS], "vT": [P, KD, NB * NS], "WcT": [P, KE, D], "Wq": [P, KD, D], "Wk": [P, KD, D], "Wv": [P, KD, D],
              "Wo": [P, KD, D], "W1x": [P, KD, D], "W1s": [NST, D], "W2": [P, KD, 4], "Wb": [P, KD, H], "convw": [P, 6, TAPS], "firs": [P, KD, FIR[0]],
              "b1": [P, KD, 1], "rmsw": [P, 1], "lbias": [P, 4 * H], "itemp": [P, H], "itemp16": [P, 4 * H], "qsel": [P, NS], "halfsig": [P, H], "mask": [P, 3, NB * NT]}
    K = {n: ctx.enter_context(nc.sbuf_tensor("k_" + n, s, F32)) for n, s in shapes.items()}
    K["rows"] = ctx.enter_context(nc.sbuf_tensor("k_rows", [P, 3, NB * NT], U32))
    return K


def scratch(nc, NB, kind="Internal"):
    t = lambda n, shape: nc.dram_tensor("scr_" + n, shape, F32, kind=kind).ap()
    return {"fpad": t("fpad", (D, FPAD)),
            "h": t("h", (P, NB * NT, D)), "v": t("v", (P, NB * NT, D)), "delta": t("delta", (P, NB * NT, D)),
            "xw1": t("xw1", (P, NB * KD, T)), "short": t("short", (P, NB * NT, D)), "vh": t("vh", (H, P, NB * NT, DH)),
            "long": t("long", (H, P, NB * NT, DH)),
            "blocks": t("blocks", (P, BS * BS)), "inverses": t("inverses", (P, BS * BS)), "h2": t("h2", (P, NB * NT, D)), "xn2T": t("xn2T", (P, NB * KD, T))}


def filter_phase(nc, ctx, A, K, dram, ps):
    NB = A["x"].shape[0]
    CG = 8
    NG = DH // CG
    NL = 8
    NTT = NB * NT
    VT = NTT * DH // 512
    sem = lambda n: ctx.enter_context(nc.semaphore(n))
    v_loaded, zeroed, vr_ps, vr_sb = sem("vh_loaded"), sem("vh_zeroed"), sem("vrev_ps"), sem("vrev_sb")
    t_loaded = [sem(f"toeplitz{q}_loaded") for q in range(NL)]
    f_ps = sem("fir_ps")
    f_sb = [sem(f"fir{r}_sb") for r in range(2)]
    f_stored = sem("fir_stored")
    with ExitStack() as tmp, nc.Block() as block:
        sb = lambda n, shape, dt=F32: tmp.enter_context(nc.sbuf_tensor(n, shape, dt))
        V = sb("Vh", [P, NTT, DH])
        VR = [sb(f"Vrev{q}", [P, DH, NB, 1 + NT]) for q in range(2)]
        TB = sb("TB", [P, NL, CG, FW])
        F = [sb(f"F{q}", [P, NTT, DH]) for q in range(2)]

        @block.sync
        def _(sp):
            for hd in range(H):
                for g in range(NG):
                    n = hd * NG + g
                    if n >= NL:
                        sp.wait_ge(f_ps, n - NL + 1)
                    src = bass.AP(dram["fpad"].tensor, (hd * DH + g * CG) * FPAD, [[1, P], [FPAD, CG], [1, FW]])
                    sp.dma_start(TB[:, n % NL, :, :], src).then_inc(t_loaded[n % NL], 16)

        @block.gpsimd
        def _(pool):
            def load_v(hd):
                if hd:
                    pool.wait_ge(vr_ps, hd * VT)
                pool.dma_start(V[:], dram["vh"][hd, :, :, :]).then_inc(v_loaded, 16)

            load_v(0)
            for q in range(2):
                nc.gpsimd.memset(VR[q][:, :, :, 0], 0.0).then_inc(zeroed, 1)
            load_v(1)
            for hd in range(H):
                for r in range(2):
                    pool.wait_ge(f_sb[r], (hd + 1) * NG // 2)
                pool.dma_start(dram["long"][hd, :, :, :], F[hd % 2][:]).then_inc(f_stored, 16)
                if hd + 2 < H:
                    load_v(hd + 2)
            pool.wait_ge(f_stored, 16 * H)

        @block.tensor
        def _(pe):
            def turn(hd):
                pe.wait_ge(v_loaded, 16 * (hd + 1))
                v2 = V[:].rearrange("p n c -> p (n c)")
                for i in range(VT):
                    n = hd * VT + i
                    if n >= 2:
                        pe.wait_ge(vr_sb, n - 1)
                    nc.tensor.matmul(ps[6 + n % 2][:], K["anti"][:], v2[:, i * 512:(i + 1) * 512], start=True, stop=True).then_inc(vr_ps, 1)

            pe.wait_ge(zeroed, 2)
            turn(0)
            for hd in range(H):
                pe.wait_ge(vr_sb, (hd + 1) * VT)
                for g in range(NG):
                    n = hd * NG + g
                    bank = n % 6
                    pe.wait_ge(t_loaded[n % NL], 16 * (n // NL + 1))
                    if n >= 6:
                        pe.wait_ge(f_sb[n % 2], (n - 6) // 2 + 1)
                    for c in range(CG):
                        cols = slice(c * NTT, (c + 1) * NTT)
                        v3 = VR[hd % 2][:, g * CG + c, :, :]
                        nc.tensor.matmul(ps[bank][:, cols], TB[:, n % NL, c, 0:P], v3[:, :, 1:], start=True, stop=False, skip_group_check=True)
                        last = nc.tensor.matmul(ps[bank][0:FW - P, cols], TB[:, n % NL, c, P:FW], v3[:, :, 0:NT],
                                                start=False, stop=True, skip_group_check=True)
                    last.then_inc(f_ps, 1)
                    if g == NG // 2 and hd + 1 < H:
                        turn(hd + 1)

        def turned(hd, i):
            n = hd * VT + i
            return VR[hd % 2][:, :, i, 1:], ps[6 + n % 2][:].rearrange("p (t c) -> p c t", c=DH)

        def evacuate(eng, r, copy):
            def turns(hd):
                for i in range(VT):
                    if i % 2 == r:
                        eng.wait_ge(vr_ps, hd * VT + i + 1)
                        o, s = turned(hd, i)
                        if hd * VT + i:
                            eng.wait_ge(vr_sb, hd * VT + i)
                        copy(o, s).then_inc(vr_sb, 1)

            turns(0)
            for hd in range(H):
                if hd >= 2:
                    eng.wait_ge(f_stored, 16 * (hd - 1))
                for g in range(NG):
                    n = hd * NG + g
                    if n % 2 == r:
                        eng.wait_ge(f_ps, n + 1)
                        copy(F[hd % 2][:, :, g * CG:(g + 1) * CG].rearrange("p n c -> p c n"),
                             ps[n % 6][:, 0:CG * NTT].rearrange("p (c n) -> p c n", c=CG)).then_inc(f_sb[r], 1)
                    if g == NG // 2 and hd + 1 < H:
                        turns(hd + 1)

        @block.scalar
        def _(act):
            evacuate(act, 0, lambda o, i: nc.scalar.activation(o, i, ACT.Copy))

        @block.vector
        def _(v):
            evacuate(v, 1, lambda o, i: nc.vector.tensor_copy(o, i))


def slot_setup(nc, ctx, A, K, dram, ps):
    sem = lambda n: ctx.enter_context(nc.semaphore(n))
    ld, pe_c, vst, act_c = sem("slot_loaded"), sem("slot_pe_group"), sem("slot_vector_step"), sem("slot_scalar_step")
    VECS = ("d_bq", "d_bk", "d_bv", "c_bq", "c_bk", "c_bv")
    with ExitStack() as tmp, nc.Block() as block:
        sb = lambda n, shape, dt=F32: tmp.enter_context(nc.sbuf_tensor(n, shape, dt))
        vrow = sb("vrow", [2 * len(VECS), P])
        slot = sb("slot", [NS, D])
        slotT = sb("slotT", [P, KD, NS])
        wqs = sb("wqs", [P, KD, D])
        wks = sb("wks", [P, KD, D])
        wkT = sb("wkT", [P, KD, D])
        qT = sb("qT", [P, KD, NS])
        qblk = sb("qblk", [P, KD, AH, NS])
        cwq = sb("cwq", [P, KD, D])

        @block.sync
        def _(sp):
            for i, n in enumerate(VECS):
                sp.dma_start(vrow[2 * i:2 * i + 2, :], A["L0_ffn_" + n].rearrange("(k p) -> k p", p=P)).then_inc(ld, 16)
            sp.dma_start(slot[:], A["L0_ffn_slot_query"][0]).then_inc(ld, 16)
            for t, n in ((wqs, "d_Wq"), (wks, "d_Wk"), (cwq, "c_Wq"), (K["dWv"], "d_Wv")):
                sp.dma_start(t[:], A["L0_ffn_" + n].rearrange("(k p) n -> p k n", p=P)).then_inc(ld, 16)
            sp.dma_start(K["cbo"][:], bass.AP(A["L0_ffn_c_bo"].tensor, 0, [[0, P], [1, D]])).then_inc(ld, 16)
            sp.wait_ge(ld, 16 * (len(VECS) + 6))

        @block.tensor
        def _(pe):
            ident = K["ident"]
            pe.wait_ge(ld, 16 * (len(VECS) + 6))
            nc.tensor.transpose(ps[0][:, 0:12], vrow[:], ident[0:12, 0:12]).then_inc(pe_c, 1)
            for k in range(KD):
                last = nc.tensor.transpose(ps[1][:, k * NS:(k + 1) * NS], slot[:, k * P:(k + 1) * P], ident[0:NS, 0:NS])
            last.then_inc(pe_c, 1)
            for w, src in ((2, wks), (3, cwq)):
                for c in range(KD):
                    for k in range(KD):
                        last = nc.tensor.transpose(ps[w][:, c * D + k * P:c * D + (k + 1) * P], src[:, k, c * P:(c + 1) * P], ident[:])
            last.then_inc(pe_c, 1)
            pe.wait_ge(vst, 4)
            for c in range(KD):
                for k in range(KD):
                    last = nc.tensor.matmul(ps[4][:, c * NS:(c + 1) * NS], wqs[:, k, c * P:(c + 1) * P], slotT[:, k, :], start=(k == 0), stop=(k == KD - 1))
            last.then_inc(pe_c, 1)
            pe.wait_ge(vst, 8)
            for c in range(KD):
                for k in range(KD):
                    last = nc.tensor.matmul(ps[5][:, c * D:(c + 1) * D], wkT[:, k, c * P:(c + 1) * P], qblk[:, k, :, :].rearrange("p h q -> p (h q)"),
                                            start=(k == 0), stop=(k == KD - 1))
            for m in range(KD):
                for k in range(KD):
                    last = nc.tensor.matmul(ps[6][:, m:m + 1], qblk[:, k, :, :].rearrange("p h q -> p (h q)")[:, m * P:(m + 1) * P],
                                            K["vecs"][:, 2 + k:3 + k], start=(k == 0), stop=(k == KD - 1))
            last.then_inc(pe_c, 1)

        @block.vector
        def _(v):
            n = [0]

            def step(ins, fence=True):
                ins.then_inc(vst, 1)
                n[0] += 1
                if fence:
                    v.wait_ge(vst, n[0])

            v.wait_ge(pe_c, 3)
            step(nc.vector.tensor_copy(K["vecs"][:], ps[0][:, 0:12]))
            step(nc.vector.tensor_copy(slotT[:], ps[1][:, 0:KD * NS].rearrange("p (k n) -> p k n", k=KD)))
            step(nc.vector.tensor_copy(wkT[:], ps[2][:].rearrange("p (k n) -> p k n", k=KD)))
            step(nc.vector.tensor_copy(K["cWqT"][:], ps[3][:].rearrange("p (k n) -> p k n", k=KD)))
            v.wait_ge(pe_c, 4)
            for c in range(KD):
                step(nc.vector.tensor_scalar(qT[:, c, :], ps[4][:, c * NS:(c + 1) * NS], K["vecs"][:, c:c + 1], None, ALU.add))
            for c in range(KD):
                step(nc.vector.tensor_tensor(qblk[:, c, :, :], qT[:, c, :].unsqueeze(1).to_broadcast([P, AH, NS]),
                                             K["hmask"][:, c, :].unsqueeze(2).to_broadcast([P, AH, NS]), ALU.mult))
            v.wait_ge(pe_c, 5)
            step(nc.vector.tensor_copy(K["Md"][:], ps[5][:].rearrange("p (k n) -> p k n", k=KD)))
            step(nc.vector.tensor_scalar(K["drow"][:], ps[6][:, 0:KD], 0.25, None, ALU.mult))


def gate_phase(nc, ctx, A, K, dram, ps):
    NB = A["x"].shape[0]
    names = ["ln_go", "src0_loaded", "src1_loaded", "xw1_loaded", "h_loaded", "square", "red", "st_step", "st_root", "pad", "w_split", "w8_loaded", "st_ps", "st_sb", "pre_ps", "pre_sb",
             "gelu", "lg_ps", "sm", "sm_exp", "pool_mix", "mix", "osq", "rms", "rms_root", "on", "ot_ps", "ot_sb", "h2_ps", "h2_sb",
             "ln_stats", "ln_aggr", "ln_eps", "ln_std", "ln_rstd", "xn_done", "h2b", "h2_stored", "xt_ps", "xt_sb", "xt_stored",
             "sc_ps", "sc_max", "sc_exp", "sum_inv", "sq_sum", "floor", "et_ps", "et_sb", "ctx_ps", "ctx_sb", "ctxT_ps", "ctxT_sb", "z_ps", "z_sb", "o_ps", "o_sb"]
    S = {n: nc.alloc_semaphore(name="g_" + n) for n in names}
    N2 = NT * H
    with ExitStack() as tmp, nc.Block() as block:
        sb = lambda n, shape, dt=F32: tmp.enter_context(nc.sbuf_tensor("g_" + n, shape, dt))
        srcs = [sb(f"src{q}", [P, 4, NT, D]) for q in range(2)]
        sqr = sb("sqr", [P, NT, D])
        xw1 = sb("xw1", [P, KD, T])
        h_tm = sb("h", [P, NT, D])
        red = sb("red", [P, 4, 3, N2])
        tiny = sb("tiny", [P, 4, 3, N2])
        st = sb("st", [P, N2, NST])
        st8 = sb("st8", [P, N2, 8, NST], BF16)
        stT = sb("stT", [P, H, T], BF16)
        w8 = sb("w8", [P, D], BF16)
        w3 = sb("w3", [NST, 3, D], BF16)
        wr = sb("wr", [NST, D])
        identb = sb("identb", [P, P], BF16)
        h1 = sb("h1", [P, KD, H, T])
        lg = sb("lg", [P, N2, 4])
        pr = sb("pr", [P, N2, 4])
        sm = sb("sm", [P, 6, N2])
        oT = sb("oT", [P, KD, T])
        stats = sb("stats", [P, NT, 6])
        mv = sb("mv", [P, NT, 2])
        rstd = sb("rstd", [P, 3, NT])
        xn = sb("xn", [P, NT, D])
        xnT = sb("xnT", [P, KD, T])
        ex = oT
        eT = sqr
        at = sb("at", [P, 8, KD])
        cx = sb("cx", [P, KD, D])
        cxT = sb("cxT", [P, KD, D])
        zm = sb("zm", [P, KD, D])

        flat = lambda a: a.rearrange("p t (h n) -> p (t h) n", h=H)
        bank2 = lambda b0: K["psum"][:, b0:b0 + 2, :].rearrange("p k n -> p (k n)")
        mixw = lambda i: pr[:, :, i:i + 1].to_broadcast([P, N2, DH])
        MIX, LONG, DELTA, VAL = 0, 1, 2, 3

        SL = 8 * (3 + H)

        def over_sequences(eng, body):
            if NB > 2:
                with eng.Fori(0, NB // 2 - 1) as c:
                    body(c * 2, 0, True, True)
                    body(c * 2 + 1, 1, True, True)
            body(NB - 2, 0, True, False)
            body(NB - 1, 1, False, False)

        @block.sync
        def _(sp):
            def load_src(b, q):
                for i, n in ((MIX, "short"), (DELTA, "delta"), (VAL, "v")):
                    sp.dma_start(srcs[q][:, i, :, :], dram[n][:, bass.ds(b * NT, NT), :]).then_inc(S[f"src{q}_loaded"], 16)
                for h in range(H):
                    sp.dma_start(srcs[q][:, LONG, :, h * DH:(h + 1) * DH], dram["long"][h, :, bass.ds(b * NT, NT), :]).then_inc(S[f"src{q}_loaded"], 16)

            def load_xw1(b):
                sp.dma_start(xw1[:], dram["xw1"][:, bass.ds(b * KD, KD), :]).then_inc(S["xw1_loaded"], 16)

            def load_h(b):
                sp.dma_start(h_tm[:], dram["h"][:, bass.ds(b * NT, NT), :]).then_inc(S["h_loaded"], 16)

            def body(b, q, more, far):
                if more:
                    sp.wait_ge(S["pre_sb"], b * 4 + 4)
                    load_xw1(b + 1)
                if far:
                    sp.wait_ge(S["ot_ps"], b * 4 + 4)
                    load_src(b + 2, q)
                sp.wait_ge(S["xt_sb"], b * 4 + 4)
                sp.dma_start(dram["xn2T"][:, bass.ds(b * KD, KD), :], xnT[:]).then_inc(S["xt_stored"], 16)
                sp.wait_ge(S["h2b"], b + 1)
                sp.dma_start(dram["h2"][:, bass.ds(b * NT, NT), :], h_tm[:]).then_inc(S["h2_stored"], 16)
                if more:
                    sp.wait_ge(S["h2_stored"], b * 16 + 16)
                    load_h(b + 1)

            load_src(0, 0)
            sp.wait_ge(S["w_split"], 5)
            for r, part in enumerate((0, 1, 2, 0, 1, 2, 0, 1)):
                sp.dma_start(w8[r * NST:(r + 1) * NST, :], w3[:, part, :]).then_inc(S["w8_loaded"], 16)
            load_xw1(0)
            load_h(0)
            load_src(1, 1)
            over_sequences(sp, body)
            sp.wait_ge(S["xt_stored"], 16 * NB)
            sp.wait_ge(S["h2_stored"], 16 * NB)

        @block.gpsimd
        def _(pool):
            def body(b, q, more, far):
                src = srcs[q]
                pool.wait_ge(S["sm"], b * 11 + 11)
                f = flat(src[:, VAL, :, :])
                nc.gpsimd.tensor_tensor(f, f, mixw(3), ALU.mult).then_inc(S["pool_mix"], 1)
                pool.wait_ge(S["xn_done"], b * NT + NT)
                nc.gpsimd.tensor_tensor(h_tm[:], h_tm[:], K["cbo"][:].unsqueeze(1).to_broadcast([P, NT, D]), ALU.add).then_inc(S["h2b"], 1)

            over_sequences(pool, body)

        @block.tensor
        def _(pe):
            ident = K["ident"][:]
            def hidden(b, later):
                pe.wait_ge(S["st_step"], b * 9 + 9)
                for c in range(2):
                    if later and c:
                        pe.wait_ge(S["h2_sb"], b * 4)
                    for h in range(H):
                        for q in range(4):
                            last = nc.tensor.matmul(ps[4 * c + h][:, q * P:(q + 1) * P],
                                                    st8[:, (4 * c + q) * H + h].rearrange("p r j -> p (r j)"), identb[:], start=True, stop=True)
                    last.then_inc(S["st_ps"], 1)
                for n in range(4):
                    m, c = n // 2, n % 2
                    if n < 2:
                        pe.wait_ge(S["st_sb"], b * 2 + n + 1)
                    else:
                        pe.wait_ge(S["pre_sb"], b * 4 + n - 1)
                    for h in range(H):
                        last = nc.tensor.matmul(ps[4 * c + h][:], w8[:, m * P:(m + 1) * P], stT[:, h, c * 512:(c + 1) * 512], start=True, stop=True)
                    last.then_inc(S["pre_ps"], 1)

            def logits(b):
                pe.wait_ge(S["pre_sb"], b * 4 + 4)
                pe.wait_ge(S["gelu"], b * 4 + 4)
                for t in range(NT):
                    for h in range(H):
                        for m in range(KD):
                            last = nc.tensor.matmul(ps[3][:, (t * H + h) * 4:(t * H + h + 1) * 4], h1[:, m, h, t * P:(t + 1) * P], K["W2"][:, m, :],
                                                    start=(m == 0), stop=(m == KD - 1))
                last.then_inc(S["lg_ps"], 1)

            def body(b, q, more, far):
                src = srcs[q]
                pe.wait_ge(S["on"], b + 1)
                for n in range(4):
                    half, k = n // 2, n % 2
                    for g in range(4):
                        last = nc.tensor.transpose(ps[n][:, g * P:(g + 1) * P], src[:, MIX, 4 * half + g, k * P:(k + 1) * P], ident)
                    last.then_inc(S["ot_ps"], 1)
                for n in range(4):
                    pe.wait_ge(S["ot_sb"], b * 4 + (2 if n < 2 else 4))
                    for q in range(2):
                        t = 2 * n + q
                        for k in range(KD):
                            last = nc.tensor.matmul(ps[4 + n][:, q * D:(q + 1) * D], oT[:, k, t * P:(t + 1) * P], K["Wo"][:, k, :],
                                                    start=(k == 0), stop=(k == KD - 1))
                    last.then_inc(S["h2_ps"], 1)
                if more:
                    hidden(b + 1, True)
                    pe.wait_ge(S["pre_sb"], b * 4 + 8)
                for n in range(4):
                    half, k = n // 2, n % 2
                    pe.wait_ge(S["xn_done"], b * NT + 4 * half + 4)
                    for q in range(4):
                        last = nc.tensor.transpose(ps[n][:, q * P:(q + 1) * P], xn[:, 4 * half + q, k * P:(k + 1) * P], ident)
                    last.then_inc(S["xt_ps"], 1)
                pe.wait_ge(S["xt_sb"], b * 4 + 4)
                for m in range(KD):
                    for c in range(2):
                        for k in range(KD):
                            last = nc.tensor.matmul(ps[4 + 2 * m + c][:], K["Md"][:, k, m * P:(m + 1) * P], xnT[:, k, c * 512:(c + 1) * 512],
                                                    start=(k == 0), stop=(k == KD - 1))
                    last.then_inc(S["sc_ps"], 1)
                if more:
                    logits(b + 1)
                pe.wait_ge(S["sc_exp"], b * KD + KD)
                for n in range(4):
                    if n == 3:
                        pe.wait_ge(S["et_sb"], b * 4 + 1)
                    for q in range(4):
                        t, m = 2 * n + q // 2, q % 2
                        last = nc.tensor.transpose(ps[n % 3][:, q * P:(q + 1) * P], ex[:, m, t * P:(t + 1) * P], ident)
                    last.then_inc(S["et_ps"], 1)
                pe.wait_ge(S["et_sb"], b * 4 + 4)
                for m in range(KD):
                    for t in range(NT):
                        last = nc.tensor.matmul(ps[4 + m][:, 0:D], eT[:, t, m * P:(m + 1) * P], xn[:, t, :], start=(t == 0), stop=(t == NT - 1))
                    last.then_inc(S["ctx_ps"], 1)
                pe.wait_ge(S["ctx_sb"], b * KD + KD)
                for k in range(KD):
                    for m in range(KD):
                        last = nc.tensor.transpose(ps[6][:, k * D + m * P:k * D + (m + 1) * P], cx[:, m, k * P:(k + 1) * P], ident)
                last.then_inc(S["ctxT_ps"], 1)
                pe.wait_ge(S["ctxT_sb"], b + 1)
                for m in range(KD):
                    for k in range(KD):
                        last = nc.tensor.matmul(ps[7][:, m * D:(m + 1) * D], cxT[:, k, m * P:(m + 1) * P], K["dWv"][:, k, :],
                                                start=(k == 0), stop=(k == KD - 1))
                last.then_inc(S["z_ps"], 1)
                pe.wait_ge(S["z_sb"], b * KD + KD)
                for c in range(KD):
                    for m in range(KD):
                        last = nc.tensor.matmul(ps[4][:, c * NS:(c + 1) * NS], zm[:, m, c * P:(c + 1) * P], K["qsel"][:], start=(m == 0), stop=(m == KD - 1))
                last.then_inc(S["o_ps"], 1)
                pe.wait_ge(S["o_sb"], b * KD + KD)

            pe.wait_ge(S["w8_loaded"], 16 * 8)
            pe.wait_ge(S["pad"], 1)
            hidden(0, False)
            logits(0)
            over_sequences(pe, body)

        @block.scalar
        def _(act):
            copy = lambda o, i: nc.scalar.activation(o, i, ACT.Copy)
            def squares(b, q, later):
                act.wait_ge(S[f"src{q}_loaded"], b * SL + (2 - q) * SL)
                for i in range(4):
                    if i:
                        act.wait_ge(S["red"], b * 12 + 3 * i)
                    elif later:
                        act.wait_ge(S["sq_sum"], b - 1)
                    nc.scalar.activation(sqr[:], srcs[q][:, i, :, :], ACT.Square).then_inc(S["square"], 1)
                act.wait_ge(S["red"], b * 12 + 12)
                nc.scalar.activation(st[:, :, 3:NST:4].rearrange("p n s -> p s n"), red[:, :, 2, :], ACT.Sqrt).then_inc(S["st_root"], 1)

            def turned(b):
                for n in range(2):
                    act.wait_ge(S["st_ps"], b * 2 + n + 1)
                    copy(stT[:, :, n * 512:(n + 1) * 512], K["psum"][:, 4 * n:4 * n + 4, :]).then_inc(S["st_sb"], 1)

            def gelus(b):
                for n in range(4):
                    m, c = n // 2, n % 2
                    act.wait_ge(S["pre_sb"], b * 4 + n + 1)
                    g = h1[:, m, :, c * 512:(c + 1) * 512]
                    nc.scalar.activation(g, g, ACT.Gelu, bias=K["b1"][:, m, :]).then_inc(S["gelu"], 1)

            def exps(b):
                act.wait_ge(S["sm"], b * 11 + 4)
                nc.scalar.activation(pr[:], lg[:], ACT.Exp).then_inc(S["sm_exp"], 1)

            def body(b, q, more, far):
                act.wait_ge(S["mix"], b * 6 + 6)
                nc.scalar.activation(sqr[:], srcs[q][:, MIX, :, :], ACT.Square).then_inc(S["osq"], 1)
                act.wait_ge(S["rms"], b * 2 + 1)
                nc.scalar.activation(sm[:, 4, :], sm[:, 3, :], ACT.Sqrt).then_inc(S["rms_root"], 1)
                for n in range(4):
                    act.wait_ge(S["ot_ps"], b * 4 + n + 1)
                    copy(oT[:, n % 2, n // 2 * 512:(n // 2 + 1) * 512], ps[n][:]).then_inc(S["ot_sb"], 1)
                if more:
                    turned(b + 1)
                act.wait_ge(S["ln_eps"], b + 1)
                nc.scalar.activation(rstd[:, 1, :], rstd[:, 0, :], ACT.Sqrt).then_inc(S["ln_std"], 1)
                if more:
                    gelus(b + 1)
                for n in range(4):
                    act.wait_ge(S["xt_ps"], b * 4 + n + 1)
                    copy(xnT[:, n % 2, n // 2 * 512:(n // 2 + 1) * 512], ps[n][:]).then_inc(S["xt_sb"], 1)
                for m in range(KD):
                    act.wait_ge(S["sc_max"], b * 6 + 3 * m + 3)
                    nc.scalar.activation(ex[:, m, :], bank2(4 + 2 * m), ACT.Exp, bias=at[:, 2, m:m + 1], scale=0.25, accum_out=at[:, 3, m:m + 1])\
                        .then_inc(S["sc_exp"], 1)
                if far:
                    squares(b + 2, q, True)
                for n in range(4):
                    act.wait_ge(S["et_ps"], b * 4 + n + 1)
                    copy(eT[:, 2 * n:2 * n + 2, :], ps[n % 3][:].rearrange("p (t n) -> p t n", t=2)).then_inc(S["et_sb"], 1)
                if more:
                    exps(b + 1)
                act.wait_ge(S["ctxT_ps"], b + 1)
                copy(cxT[:], ps[6][:].rearrange("p (k n) -> p k n", k=KD)).then_inc(S["ctxT_sb"], 1)
                act.wait_ge(S["o_ps"], b + 1)
                for c in range(KD):
                    nc.scalar.activation(K["OT"][:, c, bass.ds(b * NS, NS)], ps[4][:, c * NS:(c + 1) * NS], ACT.Identity,
                                         bias=K["vecs"][:, 4 + c:5 + c]).then_inc(S["o_sb"], 1)
                act.wait_ge(S["xt_stored"], b * 16 + 16)

            squares(0, 0, False)
            turned(0)
            gelus(0)
            squares(1, 1, False)
            exps(0)
            over_sequences(act, body)

        @block.vector
        def _(v):
            nc.vector.tensor_copy(identb[:], K["ident"][:]).then_inc(S["pad"], 1)
            for i in range(3):
                nc.vector.tensor_copy(w3[:, i, :], wr[:] if i else K["W1s"][:]).then_inc(S["w_split"], 1)
                if i < 2:
                    v.wait_ge(S["w_split"], 2 * i + 1)
                    nc.vector.tensor_tensor(wr[:], wr[:] if i else K["W1s"][:], w3[:, i, :], ALU.subtract).then_inc(S["w_split"], 1)
                    v.wait_ge(S["w_split"], 2 * i + 2)
            def statistics(b, q):
                src = srcs[q]
                v.wait_ge(S[f"src{q}_loaded"], b * SL + (2 - q) * SL)
                for i in range(4):
                    f = flat(src[:, i, :, :])
                    nc.vector.tensor_reduce(red[:, i, 0, :], f, AX.X, ALU.add).then_inc(S["red"], 1)
                    nc.vector.tensor_reduce(red[:, i, 1, :], f, AX.X, ALU.add, apply_absolute_value=True).then_inc(S["red"], 1)
                    v.wait_ge(S["square"], b * 4 + i + 1)
                    nc.vector.tensor_reduce(red[:, i, 2, :], flat(sqr[:]), AX.X, ALU.add).then_inc(S["red"], 1)
                v.wait_ge(S["red"], b * 12 + 12)
                col = lambda j: st[:, :, j:NST:4].rearrange("p n s -> p s n")
                nc.vector.tensor_scalar(col(0), red[:, :, 0, :], 1.0 / DH, None, ALU.mult).then_inc(S["st_step"], 1)
                nc.vector.tensor_scalar(col(2), red[:, :, 1, :], 1.0 / DH, None, ALU.mult).then_inc(S["st_step"], 1)
                v.wait_ge(S["st_step"], b * 9 + 1)
                nc.vector.tensor_tensor(tiny[:, :, 0, :], col(0), col(0), ALU.mult).then_inc(S["st_step"], 1)
                v.wait_ge(S["st_step"], b * 9 + 3)
                nc.vector.scalar_tensor_tensor(col(1), red[:, :, 2, :], 1.0 / DH, tiny[:, :, 0, :], ALU.mult, ALU.subtract)\
                    .then_inc(S["st_step"], 1)
                v.wait_ge(S["st_step"], b * 9 + 4)
                v.wait_ge(S["st_root"], b + 1)
                for i, (at_, rows) in enumerate(((0, 3), (3, 3), (6, 2))):
                    nc.vector.tensor_copy(st8[:, :, at_:at_ + rows, :], st[:].unsqueeze(2).to_broadcast([P, N2, rows, NST])).then_inc(S["st_step"], 1)
                    if i < 2:
                        v.wait_ge(S["st_step"], b * 9 + 5 + 2 * i)
                        nc.vector.tensor_tensor(st[:], st[:], st8[:, :, at_, :], ALU.subtract).then_inc(S["st_step"], 1)
                        v.wait_ge(S["st_step"], b * 9 + 6 + 2 * i)

            def hidden(b):
                v.wait_ge(S["xw1_loaded"], b * 16 + 16)
                for n in range(4):
                    m, c = n // 2, n % 2
                    v.wait_ge(S["pre_ps"], b * 4 + n + 1)
                    bk = 4 * c
                    nc.vector.tensor_tensor(h1[:, m, :, c * 512:(c + 1) * 512], K["psum"][:, bk:bk + 4, :],
                                            xw1[:, m, c * 512:(c + 1) * 512].unsqueeze(1).to_broadcast([P, H, 512]), ALU.add).then_inc(S["pre_sb"], 1)

            def softmax(b):
                k = [0]

                def step(ins):
                    ins.then_inc(S["sm"], 1)
                    k[0] += 1
                    v.wait_ge(S["sm"], b * 11 + k[0])

                last4 = lambda a: a.unsqueeze(2).to_broadcast([P, N2, 4])
                by_t = lambda a: a.rearrange("p (t h) j -> p t (h j)", h=H)
                v.wait_ge(S["lg_ps"], b + 1)
                step(nc.vector.tensor_tensor(by_t(lg[:]), ps[3][:, 0:4 * N2].rearrange("p (t n) -> p t n", t=NT),
                                             K["lbias"][:].unsqueeze(1).to_broadcast([P, NT, 16]), ALU.add))
                step(nc.vector.tensor_tensor(by_t(lg[:]), by_t(lg[:]), K["itemp16"][:].unsqueeze(1).to_broadcast([P, NT, 16]), ALU.mult))
                step(nc.vector.tensor_reduce(sm[:, 0, :], lg[:], AX.X, ALU.max))
                step(nc.vector.tensor_tensor(lg[:], lg[:], last4(sm[:, 0, :]), ALU.subtract))
                v.wait_ge(S["sm_exp"], b + 1)
                step(nc.vector.tensor_reduce(sm[:, 1, :], pr[:], AX.X, ALU.add))
                step(nc.vector.reciprocal(sm[:, 2, :], sm[:, 1, :]))
                step(nc.vector.tensor_tensor(lg[:], pr[:], last4(sm[:, 2, :]), ALU.mult))
                nc.vector.tensor_scalar(pr[:, :, 0:2], lg[:, :, 0:2], 0.05, None, ALU.max).then_inc(S["floor"], 1)
                nc.vector.tensor_scalar(pr[:, :, 2:4], lg[:, :, 2:4], 0.0, None, ALU.max).then_inc(S["floor"], 1)
                v.wait_ge(S["floor"], b * 2 + 2)
                step(nc.vector.tensor_reduce(sm[:, 1, :], pr[:], AX.X, ALU.add))
                step(nc.vector.reciprocal(sm[:, 2, :], sm[:, 1, :]))
                step(nc.vector.tensor_tensor(pr[:], pr[:], last4(sm[:, 2, :]), ALU.mult))
                p0 = pr[:, :, 0].rearrange("p (t h) -> p t h", h=H)
                step(nc.vector.tensor_tensor(p0, p0, K["halfsig"][:].unsqueeze(1).to_broadcast([P, NT, H]), ALU.add))
                assert k[0] == 11

            def body(b, q, more, far):
                src = srcs[q]
                f = flat(src[:, MIX, :, :])
                for n, i in enumerate((MIX, LONG, DELTA)):
                    w = flat(src[:, i, :, :])
                    nc.vector.tensor_tensor(w, w, mixw(i), ALU.mult).then_inc(S["mix"], 1)
                for n, i in enumerate((LONG, DELTA, VAL)):
                    v.wait_ge(S["mix"], b * 6 + 3 + n)
                    if i == VAL:
                        v.wait_ge(S["pool_mix"], b + 1)
                    nc.vector.tensor_tensor(f, f, flat(src[:, i, :, :]), ALU.add).then_inc(S["mix"], 1)
                v.wait_ge(S["osq"], b + 1)
                nc.vector.tensor_reduce(sm[:, 5, :], flat(sqr[:]), AX.X, ALU.add).then_inc(S["sq_sum"], 1)
                v.wait_ge(S["sq_sum"], b + 1)
                nc.vector.tensor_scalar(sm[:, 3, :], sm[:, 5, :], 1.0 / DH, 1e-5, ALU.mult, ALU.add).then_inc(S["rms"], 1)
                v.wait_ge(S["rms_root"], b + 1)
                nc.vector.reciprocal(sm[:, 5, :], sm[:, 4, :]).then_inc(S["rms"], 1)
                v.wait_ge(S["rms"], b * 2 + 2)
                nc.vector.tensor_tensor(f, f, sm[:, 5, :].unsqueeze(2).to_broadcast([P, N2, DH]), ALU.mult).then_inc(S["on"], 1)
                v.wait_ge(S["h_loaded"], b * 16 + 16)
                for n in range(4):
                    v.wait_ge(S["h2_ps"], b * 4 + n + 1)
                    t2 = h_tm[:, 2 * n:2 * n + 2, :]
                    nc.vector.tensor_tensor(t2, ps[4 + n][:].rearrange("p (t n) -> p t n", t=2), t2, ALU.add).then_inc(S["h2_sb"], 1)
                for t in range(NT):
                    v.wait_ge(S["h2_sb"], b * 4 + t // 2 + 1)
                    nc.vector.bn_stats(stats[:, t, :], h_tm[:, t, :]).then_inc(S["ln_stats"], 1)
                v.wait_ge(S["ln_stats"], b * NT + NT).then_inc(S["ln_go"], 1)
                for t in range(NT):
                    nc.vector.bn_aggr(mv[:, t, :], stats[:, t, :]).then_inc(S["ln_aggr"], 1)
                v.wait_ge(S["ln_aggr"], b * NT + NT)
                nc.vector.tensor_scalar(rstd[:, 0, :], mv[:, :, 1], 1e-5, None, ALU.add).then_inc(S["ln_eps"], 1)
                v.wait_ge(S["ln_std"], b + 1)
                nc.vector.reciprocal(rstd[:, 2, :], rstd[:, 1, :]).then_inc(S["ln_rstd"], 1)
                v.wait_ge(S["ln_rstd"], b + 1)
                for t in range(NT):
                    nc.vector.tensor_scalar(xn[:, t, :], h_tm[:, t, :], mv[:, t, 0:1], rstd[:, 2, t:t + 1], ALU.subtract, ALU.mult)\
                        .then_inc(S["xn_done"], 1)
                if more:
                    hidden(b + 1)
                for m in range(KD):
                    v.wait_ge(S["sc_ps"], b * KD + m + 1)
                    nc.vector.tensor_reduce(at[:, 0, m:m + 1], bank2(4 + 2 * m), AX.X, ALU.max).then_inc(S["sc_max"], 1)
                    v.wait_ge(S["sc_max"], b * 6 + 3 * m + 1)
                    nc.vector.scalar_tensor_tensor(at[:, 1, m:m + 1], at[:, 0, m:m + 1], 0.25, K["drow"][:, m:m + 1], ALU.mult, ALU.add)\
                        .then_inc(S["sc_max"], 1)
                    v.wait_ge(S["sc_max"], b * 6 + 3 * m + 2)
                    nc.vector.tensor_tensor(at[:, 2, m:m + 1], K["drow"][:, m:m + 1], at[:, 1, m:m + 1], ALU.subtract).then_inc(S["sc_max"], 1)
                if far:
                    statistics(b + 2, q)
                if more:
                    softmax(b + 1)
                v.wait_ge(S["sc_exp"], b * KD + KD)
                nc.vector.reciprocal(at[:, 4, :], at[:, 3, :]).then_inc(S["sum_inv"], 1)
                v.wait_ge(S["sum_inv"], b + 1)
                for m in range(KD):
                    v.wait_ge(S["ctx_ps"], b * KD + m + 1)
                    nc.vector.tensor_scalar(cx[:, m, :], ps[4 + m][:, 0:D], at[:, 4, m:m + 1], None, ALU.mult).then_inc(S["ctx_sb"], 1)
                v.wait_ge(S["z_ps"], b + 1)
                for m in range(KD):
                    nc.vector.tensor_tensor(zm[:, m, :].rearrange("p (g n) -> p g n", g=AH), ps[7][:, m * D:(m + 1) * D].rearrange("p (g n) -> p g n", g=AH),
                                            K["hmask"][:, m, :].unsqueeze(2).to_broadcast([P, AH, AD]), ALU.mult).then_inc(S["z_sb"], 1)

            statistics(0, 0)
            hidden(0)
            statistics(1, 1)
            softmax(0)
            over_sequences(v, body)

    nc.clear_and_free_semaphores(list(S.values()))
    nc.all_engine_barrier()


def expert_phase(nc, ctx, A, K, dram, ps):
    sem = lambda n: ctx.enter_context(nc.semaphore("e_" + n))
    NB = A["x"].shape[0]
    NR = NB * NS
    NF = FF // P
    NW = 2
    NP = 3
    NE = NS
    ld, vst, pe_c, root, bias_sb = sem("loaded"), sem("vector_step"), sem("pe_group"), sem("root"), sem("bias_step")
    w_loaded = [sem(f"w{q}_loaded") for q in range(NW)]
    u_ps, u_pre, u_act, ug_sb, y_ps, o2_sb, kv_ps, kv_sb = (sem(n) for n in ("u_ps", "u_pre", "u_act", "ug_sb", "y_ps", "o2_sb", "kv_ps", "kv_sb"))
    rows_ld, w_p1, w_r, w_p2, w_p3, u_sum, ug_step, y_sum, x_split = (sem(n) for n in ("rows_loaded", "w_part1", "w_rest", "w_part2", "w_part3", "u_sum", "ug_step", "y_sum", "x_split"))
    with ExitStack() as tmp, nc.Block() as block:
        sb = lambda n, shape, dt=F32: tmp.enter_context(nc.sbuf_tensor("e_" + n, shape, dt))
        dWo, cWk, cWv = K["Wq"], K["Wk"], K["Wv"]
        slotb = sb("slotb", [P, D])
        bo = sb("bo", [P, D])
        lng = sb("lng", [P, D])
        lnb = sb("lnb", [P, D])
        brow = [sb(f"brow{q}", [NE * NF, P]) for q in range(2)]
        b2row = sb("b2row", [NE * KD, P])
        b1c = sb("b1c", [P, 2, NE, NF])
        b2c = sb("b2c", [P, NE, KD])
        W = [sb(f"W_{q}", [P, 3, KD * FF]) for q in range(NW)]
        WP = [sb(f"WP_{q}", [P, 3, 3, KD * FF], BF16) for q in range(NP)]
        o1 = sb("o1", [P, D])
        stats = sb("stats", [P, 6])
        mv = sb("mv", [P, 2])
        rs = sb("rs", [P, 4])
        hl = sb("hl", [P, D])
        hT = sb("hT", [P, KD, NR])
        o1T = sb("o1T", [P, KD, NR])
        o2T = sb("o2T", [P, KD, NR])
        ub = [sb(f"ub{q}", [P, 2, NF, NB]) for q in range(2)]
        ug = [sb(f"ug{q}", [P, NF, NB]) for q in range(2)]
        us = [sb(f"us{q}", [P, 2 * NF, NB]) for q in range(2)]
        ys = [sb(f"ys{q}", [P, KD, NB]) for q in range(2)]
        ug3 = [sb(f"ug3_{q}", [P, NF, 3, NB], BF16) for q in range(2)]
        hT3 = sb("hT3", [P, KD, 3, NR], BF16)
        SPLITS = ((0, 0), (1, 0), (0, 1), (2, 0), (1, 1), (2, 1))
        NLOAD = 3 + NB + 1 + 2 + 1

        @block.sync
        def _(sp):
            def load(e):
                q = e % NW
                if e >= NW:
                    sp.wait_ge(w_p3, 3 * (e - NW + 1))
                for m, n in enumerate(("W1", "Wg")):
                    sp.dma_start(W[q][:, m, :].rearrange("p (k f) -> p k f", k=KD), A["L0_ffn_e_" + n][e].rearrange("(k p) f -> p k f", p=P))\
                        .then_inc(w_loaded[q], 16)
                sp.dma_start(W[q][:, 2, :].rearrange("p (k n) -> p k n", k=NF), A["L0_ffn_e_W2"][e].rearrange("(k p) n -> p k n", p=P))\
                    .then_inc(w_loaded[q], 16)

            for e in range(NE):
                load(e)

        @block.scalar
        def _(act):
            for t, n in ((dWo, "d_Wo"), (cWk, "c_Wk"), (cWv, "c_Wv")):
                act.dma_start(t[:], A["L0_ffn_" + n].rearrange("(k p) n -> p k n", p=P)).then_inc(ld, 16)
            for b in range(NB):
                act.dma_start(slotb[b * NS:(b + 1) * NS, :], A["L0_ffn_slot_query"][0]).then_inc(ld, 16)
            act.dma_start(bo[:], bass.AP(A["L0_ffn_d_bo"].tensor, 0, [[0, P], [1, D]])).then_inc(ld, 16)
            for q, n in enumerate(("e_b1", "e_bg")):
                act.dma_start(brow[q][:], A["L0_ffn_" + n].rearrange("e (f p) -> (e f) p", p=P)).then_inc(ld, 16)
            act.dma_start(b2row[:], A["L0_ffn_e_b2"].rearrange("e (k p) -> (e k) p", p=P)).then_inc(ld, 16)
            def part(e, m, r):
                if r == 0:
                    if m == 0:
                        act.wait_ge(w_loaded[e % NW], 48 * (e // NW + 1))
                        if e >= NP:
                            act.wait_ge(y_ps, e - NP + 1)
                else:
                    act.wait_ge(w_r, 3 * e + m + 1)
                nc.scalar.activation(WP[e % NP][:, m, r, :], W[e % NW][:, m, :], ACT.Copy).then_inc((w_p1, w_p2)[r], 1)

            for m, r in SPLITS:
                part(0, m, r)
            act.wait_ge(vst, 4)
            nc.scalar.activation(rs[0:NR, 1:2], rs[0:NR, 0:1], ACT.Sqrt).then_inc(root, 1)

            for e in range(NE + 1):
                if 0 < e < NE:
                    for m, r in SPLITS:
                        part(e, m, r)
                if e:
                    act.wait_ge(u_pre, e)
                    nc.scalar.activation(ub[(e - 1) % 2][:], ub[(e - 1) % 2][:], ACT.Silu).then_inc(u_act, 1)

        @block.gpsimd
        def _(pool):
            for b in range(NB):
                pool.dma_start(lng[b * NS:(b + 1) * NS, :], A["L0_ffn_e_ln_g"]).then_inc(rows_ld, 16)
                pool.dma_start(lnb[b * NS:(b + 1) * NS, :], A["L0_ffn_e_ln_b"]).then_inc(rows_ld, 16)

        @block.tensor
        def _(pe):
            ident = K["ident"]
            pe.wait_ge(ld, 16 * NLOAD)
            for q in range(2):
                nc.tensor.transpose(ps[q][:, 0:P], brow[q][:], ident[:])
            nc.tensor.transpose(ps[2][:, 0:NE * KD], b2row[:], ident[0:NE * KD, 0:NE * KD]).then_inc(pe_c, 1)
            for k in range(KD):
                last = nc.tensor.matmul(ps[3][0:NR, 0:D], K["OT"][:, k, :], dWo[:, k, :], start=(k == 0), stop=(k == KD - 1))
            last.then_inc(pe_c, 1)
            pe.wait_ge(vst, 8)
            for k in range(KD):
                nc.tensor.transpose(ps[4][:, k * P:k * P + NR], hl[0:NR, k * P:(k + 1) * P], ident[0:NR, 0:NR])
                last = nc.tensor.transpose(ps[5][:, k * P:k * P + NR], o1[0:NR, k * P:(k + 1) * P], ident[0:NR, 0:NR])
            last.then_inc(pe_c, 1)

            def up(e):
                q, bank = e % NP, 6 + e % 2
                pe.wait_ge(w_p3, 3 * e + 3)
                if e >= 2:
                    pe.wait_ge(u_sum, e - 1)
                for m in range(2):
                    for f in range(NF):
                        at = (m * NF + f) * 3 * NB
                        for n in range(3 * KD):
                            k, r = n // 3, n % 3
                            last = nc.tensor.matmul(ps[bank][:, at:at + 3 * NB], WP[q][:, m, r, k * FF + f * P:k * FF + (f + 1) * P],
                                                    hT3[:, k, :, e:NR:NE], start=(n == 0), stop=(n == 3 * KD - 1))
                last.then_inc(u_ps, 1)

            def down(e):
                q, bank = e % NP, e % 2
                pe.wait_ge(ug_sb, e + 1)
                if e >= 2:
                    pe.wait_ge(y_sum, e - 1)
                for c in range(KD):
                    for n in range(3 * NF):
                        f, r = n // 3, n % 3
                        last = nc.tensor.matmul(ps[bank][:, c * 3 * NB:(c + 1) * 3 * NB], WP[q][:, 2, r, f * D + c * P:f * D + (c + 1) * P],
                                                ug3[e % 2][:, f].rearrange("p j b -> p (j b)"), start=(n == 0), stop=(n == 3 * NF - 1))
                last.then_inc(y_ps, 1)

            pe.wait_ge(vst, 9)
            pe.wait_ge(bias_sb, 3)
            pe.wait_ge(x_split, 5)
            for e in range(NE + 1):
                if e < NE:
                    up(e)
                if e:
                    down(e - 1)
            pe.wait_ge(o2_sb, NE)
            for w, wt in enumerate((cWk, cWv)):
                for c in range(KD):
                    for k in range(KD):
                        last = nc.tensor.matmul(ps[2 + w][:, c * P:c * P + NR], wt[:, k, c * P:(c + 1) * P], o2T[:, k, :], start=(k == 0), stop=(k == KD - 1))
            last.then_inc(kv_ps, 1)

        @block.vector
        def _(v):
            n = [0]

            def step(ins):
                ins.then_inc(vst, 1)
                n[0] += 1
                v.wait_ge(vst, n[0])

            def rest(e, m, r):
                w = W[e % NW][:, m, :]
                v.wait_ge((w_p1, w_p2)[r], 3 * e + m + 1)
                nc.vector.tensor_tensor(WP[e % NP][:, m, 2, :] if r else w, w, WP[e % NP][:, m, r, :], ALU.subtract).then_inc((w_r, w_p3)[r], 1)

            for m, r in SPLITS:
                rest(0, m, r)
            R = slice(0, NR)
            v.wait_ge(ld, 16 * NLOAD)
            v.wait_ge(rows_ld, 16 * 2 * NB)
            v.wait_ge(pe_c, 2)
            step(nc.vector.tensor_tensor(o1[R, :], ps[3][R, 0:D], slotb[R, :], ALU.add))
            step(nc.vector.tensor_tensor(o1[R, :], o1[R, :], bo[R, :], ALU.add))
            step(nc.vector.bn_stats(stats[R, :], o1[R, :]))
            nc.vector.bn_aggr(mv[R, :], stats[R, :]).then_inc(kv_sb, 1)
            v.wait_ge(kv_sb, 1)
            step(nc.vector.tensor_scalar(rs[R, 0:1], mv[R, 1:2], 1e-5, None, ALU.add))
            v.wait_ge(root, 1)
            step(nc.vector.reciprocal(rs[R, 2:3], rs[R, 1:2]))
            step(nc.vector.tensor_scalar(hl[R, :], o1[R, :], mv[R, 0:1], rs[R, 2:3], ALU.subtract, ALU.mult))
            step(nc.vector.tensor_tensor(hl[R, :], hl[R, :], lng[R, :], ALU.mult))
            step(nc.vector.tensor_tensor(hl[R, :], hl[R, :], lnb[R, :], ALU.add))
            for q in range(2):
                nc.vector.tensor_copy(b1c[:, q, :, :].rearrange("p e f -> p (e f)"), ps[q][:, 0:P]).then_inc(bias_sb, 1)
            nc.vector.tensor_copy(b2c[:].rearrange("p e k -> p (e k)"), ps[2][:, 0:NE * KD]).then_inc(bias_sb, 1)
            v.wait_ge(bias_sb, 3)
            v.wait_ge(pe_c, 3)
            nr = lambda bank: ps[bank][:, 0:KD * P].rearrange("p (k n) -> p k n", k=KD)[:, :, 0:NR]
            step(nc.vector.tensor_copy(hT[:], nr(4)))
            step(nc.vector.tensor_copy(o1T[:], nr(5)))
            for k in range(KD):
                o = o1T[:, k, :].rearrange("p (b e) -> p b e", e=NE)
                step(nc.vector.tensor_tensor(o, o, b2c[:, :, k].unsqueeze(1).to_broadcast([P, NB, NE]), ALU.add))

            for r in range(3):
                nc.vector.tensor_copy(hT3[:, :, r, :], hT[:]).then_inc(x_split, 1)
                if r < 2:
                    v.wait_ge(x_split, 2 * r + 1)
                    nc.vector.tensor_tensor(hT[:], hT[:], hT3[:, :, r, :], ALU.subtract).then_inc(x_split, 1)
                    v.wait_ge(x_split, 2 * r + 2)

            def pre(e):
                q = e % 2
                v.wait_ge(u_ps, e + 1)
                nc.vector.tensor_reduce(us[q][:], ps[6 + q][:, 0:6 * NF * NB].rearrange("p (x j b) -> p x b j", j=3, b=NB), AX.X, ALU.add).then_inc(u_sum, 1)
                v.wait_ge(u_sum, e + 1)
                nc.vector.tensor_tensor(ub[q][:], us[q][:].rearrange("p (g f) b -> p g f b", g=2),
                                        b1c[:, :, e, :].unsqueeze(3).to_broadcast([P, 2, NF, NB]), ALU.add).then_inc(u_pre, 1)
                v.wait_ge(u_act, e + 1)
                nc.vector.tensor_tensor(ug[q][:], ub[q][:, 0, :, :], ub[q][:, 1, :, :], ALU.mult).then_inc(ug_step, 1)
                for r in range(3):
                    v.wait_ge(ug_step, 5 * e + 2 * r + 1)
                    part = nc.vector.tensor_copy(ug3[q][:, :, r, :], ug[q][:])
                    if r < 2:
                        part.then_inc(ug_step, 1)
                        v.wait_ge(ug_step, 5 * e + 2 * r + 2)
                        nc.vector.tensor_tensor(ug[q][:], ug[q][:], ug3[q][:, :, r, :], ALU.subtract).then_inc(ug_step, 1)
                    else:
                        part.then_inc(ug_sb, 1)

            def post(e):
                q = e % 2
                v.wait_ge(y_ps, e + 1)
                nc.vector.tensor_reduce(ys[q][:], ps[q][:, 0:KD * 3 * NB].rearrange("p (k j b) -> p k b j", k=KD, j=3), AX.X, ALU.add).then_inc(y_sum, 1)
                v.wait_ge(y_sum, e + 1)
                nc.vector.tensor_tensor(o2T[:, :, e:NR:NE], ys[q][:], o1T[:, :, e:NR:NE], ALU.add).then_inc(o2_sb, 1)

            for e in range(NE + 2):
                if 0 < e < NE:
                    for m, r in SPLITS:
                        rest(e, m, r)
                if e >= 2:
                    post(e - 2)
                if 1 <= e <= NE:
                    pre(e - 1)
            v.wait_ge(kv_ps, 1)
            for w, dst in enumerate((K["kT"], K["vT"])):
                for c in range(KD):
                    nc.vector.tensor_scalar(dst[:, c, :], ps[2 + w][:, c * P:c * P + NR], K["vecs"][:, 8 + 2 * w + c:9 + 2 * w + c], None, ALU.add)\
                        .then_inc(kv_sb, 1)
            v.wait_ge(kv_sb, 5)


def final_phase(nc, ctx, A, K, dram, ps, out):
    sem = lambda n: ctx.enter_context(nc.semaphore("t_" + n))
    NB = A["x"].shape[0]
    names = ["cwo", "vq_set", "biased", "xt0_loaded", "xt1_loaded", "h0_loaded", "h1_loaded", "kblk", "vblk", "m_ps", "m_sb", "row_sb", "vo_ps", "vo_sb", "sc_ps",
             "mx", "dif", "exp", "sum", "rec", "attn", "at_ps", "at_sb", "o_ps", "o_sb", "out0_stored", "out1_stored"]
    S = {n: sem(n) for n in names}
    with ExitStack() as tmp, nc.Block() as block:
        sb = lambda n, shape, dt=F32: tmp.enter_context(nc.sbuf_tensor("t_" + n, shape, dt))
        cWo = sb("cWo", [P, KD, D])
        xT = [sb(f"xT{q}", [P, KD, T]) for q in range(2)]
        h = [sb(f"h{q}", [P, NT, D]) for q in range(2)]
        kb = sb("kb", [P, KD, AH, NS])
        vb = sb("vb", [P, KD, AH, NS])
        Mc = sb("Mc", [P, KD, D])
        crow = sb("crow", [P, D])
        vq = sb("vq", [P, KD, P])
        VW = sb("VW", [P, KD, D])
        sc = [sb(f"sc{q}", [P, 32, NS]) for q in range(2)]
        ex = [sb(f"ex{q}", [P, 32, NS]) for q in range(2)]
        at = [sb(f"at{q}", [P, 2, D]) for q in range(2)]
        aT = [sb(f"aT{q}", [P, 2, KD, P]) for q in range(2)]
        mx = sb("mx", [P, 4, 3, 32])
        blk = lambda a: a.rearrange("p h q -> p (h q)")
        outv = out.rearrange("b (t p) d -> b p t d", p=P)
        GR = NT // 2

        @block.sync
        def _(sp):
            sp.dma_start(cWo[:], A["L0_ffn_c_Wo"].rearrange("(k p) n -> p k n", p=P)).then_inc(S["cwo"], 16)

            def load_x(b, q):
                sp.dma_start(xT[q][:], dram["xn2T"][:, bass.ds(b * KD, KD), :]).then_inc(S[f"xt{q}_loaded"], 16)

            def load_h(b, q):
                sp.dma_start(h[q][:], dram["h2"][:, bass.ds(b * NT, NT), :]).then_inc(S[f"h{q}_loaded"], 16)

            for q in range(2):
                load_x(q, q)
                load_h(q, q)
            if NB > 2:
                with sp.Fori(0, NB // 2 - 1) as c:
                    for q in range(2):
                        sp.wait_ge(S["sc_ps"], c * 2 * GR + (q + 1) * GR)
                        load_x(c * 2 + (2 + q), q)
                        sp.wait_ge(S[f"out{q}_stored"], c * 16 + 16)
                        load_h(c * 2 + (2 + q), q)

        @block.gpsimd
        def _(pool):
            hm = lambda k: K["hmask"][:, k, :].unsqueeze(2).to_broadcast([P, AH, NS])
            with pool.Fori(0, NB // 2) as c:
                for q in range(2):
                    b = c * 2 + q
                    for k in range(KD):
                        nc.gpsimd.tensor_tensor(kb[:, k, :, :], K["kT"][:, k, bass.ds(b * NS, NS)].unsqueeze(1).to_broadcast([P, AH, NS]), hm(k), ALU.mult)\
                            .then_inc(S["kblk"], 1)
                    for k in range(KD):
                        nc.gpsimd.tensor_tensor(vb[:, k, :, :], K["vT"][:, k, bass.ds(b * NS, NS)].unsqueeze(1).to_broadcast([P, AH, NS]), hm(k), ALU.mult)\
                            .then_inc(S["vblk"], 1)
                    for g in range(GR):
                        n = b * GR + g
                        if g == 0:
                            pool.wait_ge(S["m_ps"], b + 1)
                            pool.wait_ge(S["vo_ps"], b + 1)
                        pool.wait_ge(S["rec"], n + 1)
                        if g >= 2:
                            pool.wait_ge(S["at_ps"], n - 1)
                        nc.gpsimd.tensor_tensor(at[g % 2][:].rearrange("p t (h s) -> p (t h) s", s=NS), ex[g % 2][:],
                                                mx[:, g, 2, :].unsqueeze(2).to_broadcast([P, 32, NS]), ALU.mult).then_inc(S["attn"], 1)

        @block.tensor
        def _(pe):
            def scores(b, q, g):
                n = b * GR + g
                if g >= 2:
                    pe.wait_ge(S["biased"], n - 1)
                bank = g % 2
                for j in range(2):
                    t = 2 * g + j
                    o = ps[bank][:, j * D:(j + 1) * D]
                    for k in range(KD):
                        last = nc.tensor.matmul(o, xT[q][:, k, t * P:(t + 1) * P], Mc[:, k, :], start=(k == 0), stop=(k == KD - 1))
                last.then_inc(S["sc_ps"], 1)

            def values(b, q, g):
                n = b * GR + g
                pe.wait_ge(S["attn"], n + 1)
                if g >= 2:
                    pe.wait_ge(S["at_sb"], n - 1)
                    pe.wait_ge(S["o_sb"], n - 1)
                for j in range(2):
                    for m in range(KD):
                        last = nc.tensor.transpose(ps[2 + g % 2][:, (j * KD + m) * P:(j * KD + m + 1) * P], at[g % 2][:, j, m * P:(m + 1) * P], K["ident"][:])
                last.then_inc(S["at_ps"], 1)
                pe.wait_ge(S["at_sb"], n + 1)
                for j in range(2):
                    for m in range(KD):
                        last = nc.tensor.matmul(ps[4 + g % 2][:, j * D:(j + 1) * D], aT[g % 2][:, j, m, :], VW[:, m, :], start=(m == 0), stop=(m == KD - 1))
                last.then_inc(S["o_ps"], 1)

            pe.wait_ge(S["cwo"], 16)
            pe.wait_ge(S["vq_set"], KD)
            with pe.Fori(0, NB // 2) as c:
                for q in range(2):
                    b = c * 2 + q
                    pe.wait_ge(S["kblk"], b * 2 + 2)
                    for d in range(KD):
                        for k in range(KD):
                            last = nc.tensor.matmul(ps[6][:, d * D:(d + 1) * D], K["cWqT"][:, k, d * P:(d + 1) * P], blk(kb[:, k, :, :]), start=(k == 0), stop=(k == KD - 1))
                    for k in range(KD):
                        last = nc.tensor.matmul(ps[0][:, 0:D], vq[:, k, :], blk(kb[:, k, :, :]), start=(k == 0), stop=(k == KD - 1))
                    last.then_inc(S["m_ps"], 1)
                    pe.wait_ge(S["vblk"], b * 2 + 2)
                    for m in range(KD):
                        for k in range(KD):
                            last = nc.tensor.matmul(ps[7][:, m * D:(m + 1) * D], blk(vb[:, k, :, :])[:, m * P:(m + 1) * P], cWo[:, k, :], start=(k == 0), stop=(k == KD - 1))
                    last.then_inc(S["vo_ps"], 1)
                    pe.wait_ge(S["m_sb"], b + 1)
                    pe.wait_ge(S["row_sb"], b + 1)
                    pe.wait_ge(S["vo_sb"], b + 1)
                    pe.wait_ge(S[f"xt{q}_loaded"], c * 16 + 16)
                    for g in range(GR + 2):
                        if g < GR:
                            scores(b, q, g)
                        if g >= 2:
                            values(b, q, g - 2)

        @block.scalar
        def _(act):
            copy = lambda o, i: nc.scalar.activation(o, i, ACT.Copy)
            with act.Fori(0, NB // 2) as c:
                for q in range(2):
                    b = c * 2 + q
                    act.wait_ge(S["m_ps"], b + 1)
                    copy(Mc[:], ps[6][:].rearrange("p (k n) -> p k n", k=KD)).then_inc(S["m_sb"], 1)
                    copy(crow[:], ps[0][:, 0:D]).then_inc(S["row_sb"], 1)
                    act.wait_ge(S["vo_ps"], b + 1)
                    copy(VW[:], ps[7][:].rearrange("p (k n) -> p k n", k=KD)).then_inc(S["vo_sb"], 1)
                    for g in range(GR + 1):
                        n = b * GR + g
                        if g < GR:
                            act.wait_ge(S["dif"], n + 1)
                            if g >= 2:
                                act.wait_ge(S["attn"], n - 1)
                            nc.scalar.activation(ex[g % 2][:], sc[g % 2][:], ACT.Exp, scale=0.25).then_inc(S["exp"], 1)
                        if g:
                            act.wait_ge(S["at_ps"], n)
                            copy(aT[(g - 1) % 2][:].rearrange("p j m n -> p (j m n)"), ps[2 + (g - 1) % 2][:]).then_inc(S["at_sb"], 1)
                            if g == GR:
                                act.wait_ge(S["o_sb"], n)
                                act.dma_start(outv[bass.ds(b, 1), :, :, :].rearrange("b p t d -> (b p) t d"), h[q][:]).then_inc(S[f"out{q}_stored"], 16)
            for q in range(2):
                act.wait_ge(S[f"out{q}_stored"], 16 * (NB // 2))

        @block.vector
        def _(v):
            for k in range(KD):
                nc.vector.tensor_copy(vq[:, k, :], K["vecs"][:, 6 + k:7 + k].to_broadcast([P, P])).then_inc(S["vq_set"], 1)
            with v.Fori(0, NB // 2) as c:
                for q in range(2):
                    b = c * 2 + q
                    for g in range(GR + 2):
                        n = b * GR + g
                        if g < GR:
                            b3 = lambda a: a.unsqueeze(2).to_broadcast([P, 32, NS])
                            v.wait_ge(S["sc_ps"], n + 1)
                            if g == 0:
                                v.wait_ge(S["row_sb"], b + 1)
                            if g >= 2:
                                v.wait_ge(S["exp"], n - 1)
                            s3 = sc[g % 2][:]
                            nc.vector.tensor_tensor(s3.rearrange("p (j n) s -> p j (n s)", j=2), ps[g % 2][:].rearrange("p (j n) -> p j n", j=2),
                                                    crow[:].unsqueeze(1).to_broadcast([P, 2, D]), ALU.add).then_inc(S["biased"], 1)
                            v.wait_ge(S["biased"], n + 1)
                            nc.vector.tensor_reduce(mx[:, g, 0, :], s3, AX.X, ALU.max).then_inc(S["mx"], 1)
                            v.wait_ge(S["mx"], n + 1)
                            nc.vector.tensor_tensor(s3, s3, b3(mx[:, g, 0, :]), ALU.subtract).then_inc(S["dif"], 1)
                        if 1 <= g <= GR:
                            v.wait_ge(S["exp"], n)
                            nc.vector.tensor_reduce(mx[:, g - 1, 1, :], ex[(g - 1) % 2][:], AX.X, ALU.add).then_inc(S["sum"], 1)
                            v.wait_ge(S["sum"], n)
                            nc.vector.reciprocal(mx[:, g - 1, 2, :], mx[:, g - 1, 1, :]).then_inc(S["rec"], 1)
                        if g >= 2:
                            if g == 2:
                                v.wait_ge(S[f"h{q}_loaded"], c * 16 + 16)
                            v.wait_ge(S["o_ps"], n - 1)
                            h2 = h[q][:, 2 * g - 4:2 * g - 2, :]
                            nc.vector.tensor_tensor(h2, ps[4 + g % 2][:].rearrange("p (t n) -> p t n", t=2), h2, ALU.add).then_inc(S["o_sb"], 1)


def tower(nc, A, out):
    NB = A["x"].shape[0]
    with ExitStack() as ctx:
        dram = scratch(nc, NB)
        K = constants(nc, ctx, NB)
        K["psum"] = ctx.enter_context(nc.psum_tensor("psum", [P, 8, 512], F32))
        ps = [K["psum"][:, i, :] for i in range(8)]
        setup(nc, ctx, A, K, dram, ps)
        delta_phase(nc, ctx, A, K, dram, ps)
        filter_phase(nc, ctx, A, K, dram, ps)
        slot_setup(nc, ctx, A, K, dram, ps)
        gate_phase(nc, ctx, A, K, dram, ps)
        expert_phase(nc, ctx, A, K, dram, ps)
        final_phase(nc, ctx, A, K, dram, ps, out)


_ATTN = ("Wq", "Wk", "Wv", "Wb", "conv_q", "conv_k", "conv_v", "fir_long", "fir_short", "W1", "b1", "W2", "b2", "log_temp",
         "base_bias", "conv_residual_logit", "rms_w", "Wo")
_FFN = ("slot_query", "d_Wq", "d_Wk", "d_Wv", "d_Wo", "d_bq", "d_bk", "d_bv", "d_bo", "c_Wq", "c_Wk", "c_Wv", "c_Wo", "c_bq", "c_bk",
        "c_bv", "c_bo", "e_ln_g", "e_ln_b", "e_W1", "e_b1", "e_Wg", "e_bg", "e_W2", "e_b2")
_INS = ["x"] + [f"L0_tok_{n}{i}" for i in range(3) for n in ("emb", "w")] + ["L0_attn_" + n for n in _ATTN] + ["L0_ffn_" + n for n in _FFN]


def kernel(**inputs):
    import numpy as _np
    import concourse.bacc as _bacc
    from concourse import mybir as _mybir
    from concourse.bass_utils import run_bass_kernel_spmd as _run

    nc = _bacc.Bacc("TRN2", target_bir_lowering=False, num_devices=1)
    arrays, args = {}, {}
    for name in _INS:
        a = _np.ascontiguousarray(inputs[name])
        arrays[f"in_{name}_dram"] = a
        args[name] = nc.dram_tensor(f"in_{name}_dram", a.shape, _mybir.dt.from_np(a.dtype), kind="ExternalInput").ap()
    shape = tuple(inputs["x"].shape) + (D,)
    out = nc.dram_tensor("out_0_dram", shape, F32, kind="ExternalOutput").ap()
    tower(nc, args, out)
    r = _run(nc, [arrays], core_ids=[0])
    return r.results[0]["out_0_dram"]
```
